# Optimizing a Trainium2 kernel written in Bass

```python
import numpy as np
import jax
import jax.numpy as jnp

def _softmax(x, axis=-1):
    return jax.nn.softmax(x, axis=axis)

def _gelu(x):
    return jax.nn.gelu(x, approximate=True)

def _silu(x):
    return jax.nn.silu(x)

def _sigmoid(x):
    return jax.nn.sigmoid(x)

def _layernorm(x, axis=-1, eps=1e-05):
    m = jnp.mean(x, axis=axis, keepdims=True)
    v = jnp.var(x, axis=axis, keepdims=True)
    return (x - m) / jnp.sqrt(v + eps)

def _scatter_add(tgt, idx, src, axis=0):
    return tgt.at[idx].add(src)

def _segment_sum(src, seg, n):
    return jax.ops.segment_sum(src, seg, n)
kernel_name = 'mk_lm_tower_d2_tok_ids768_r4_53eee7'

def setup_inputs(seed: int=0):
    np.random.seed(seed)
    _w = jnp.asarray

    def _rec_inputs():
        import jax
        import jax.numpy as jnp
        _rk = jax.random.key(seed)
        x = jax.random.randint(jax.random.fold_in(_rk, 1), (16, 128), 0, 30522, jnp.int32)
        mask_BS_i1_0 = jnp.where(jnp.ones((16, 128), dtype=bool), 1, 0).astype(jnp.int32)
        return (x, mask_BS_i1_0)
    x, mask_BS_i1_0 = _rec_inputs()

    def _L0_tok_setup():
        import jax, jax.numpy as jnp
        import numpy as np
        VOCAB = 30522
        SEG_VOCAB = 2
        D_MODEL = 192
        MAX_LEN = 128
        B, S = (64, 128)
        EPS = 1e-05
        key = jax.random.key(seed)
        k1, k2, k3, k4, k5 = jax.random.split(key, 5)
        token_ids = jax.random.randint(k1, (B, S), 0, VOCAB)
        segment_ids = jax.random.randint(k2, (B, S), 0, SEG_VOCAB)
        tok_table = jax.random.normal(k3, (VOCAB, D_MODEL), dtype=jnp.float32) * 0.02
        seg_table = jax.random.normal(k4, (SEG_VOCAB, D_MODEL), dtype=jnp.float32) * 0.02
        pos_table = jax.random.normal(k5, (MAX_LEN, D_MODEL), dtype=jnp.float32) * 0.02
        gamma = jnp.ones((D_MODEL,), dtype=jnp.float32)
        beta = jnp.zeros((D_MODEL,), dtype=jnp.float32)
        return {'token_ids': token_ids, 'segment_ids': segment_ids, 'tok_table': tok_table, 'seg_table': seg_table, 'pos_table': pos_table, 'gamma': gamma, 'beta': beta}
    _L0_tok_all = _L0_tok_setup()
    _L0_tok_in = {k: v for k, v in _L0_tok_all.items() if k in ('tok_table', 'seg_table', 'pos_table', 'gamma', 'beta')}
    del _L0_tok_all

    def _L0_attn_setup():
        import jax, jax.numpy as jnp
        import numpy as np
        D_MODEL = 192
        D_INNER = 384
        D_STATE = 16
        DT_RANK = 96
        H_FFN = 512
        B, L = (1, 512)
        EPS = 1e-06

        def rmsnorm(x, w):
            return x * jax.lax.rsqrt(jnp.mean(x * x, axis=-1, keepdims=True) + EPS) * w

        def selective_scan(z, W_xproj, W_dt, b_dt, A_log, D_skip):
            xdbl = jnp.einsum('bld,kd->blk', z, W_xproj)
            dt_in, Bm, Cm = jnp.split(xdbl, [DT_RANK, DT_RANK + D_STATE], axis=-1)
            dt = jax.nn.softplus(jnp.einsum('blr,dr->bld', dt_in, W_dt) + b_dt)
            A = -jnp.exp(A_log)
            A_bar = jnp.exp(dt[..., None] * A)
            Bx = (dt * z)[..., None] * Bm[:, :, None, :]

            def comb(e1, e2):
                a1, b1 = e1
                a2, b2 = e2
                return (a1 * a2, a2 * b1 + b2)
            _, h = jax.lax.associative_scan(comb, (A_bar, Bx), axis=1)
            y = jnp.einsum('blds,bls->bld', h, Cm) + D_skip * z
            return y
        key = jax.random.key(seed)
        ks = jax.random.split(key, 10)
        s = lambda k, shape, scale=0.02: jax.random.normal(k, shape, dtype=jnp.float32) * scale
        return {'x': jax.random.normal(ks[0], (B, L, D_MODEL), dtype=jnp.float32), 'w_norm1': jnp.ones((D_MODEL,), jnp.float32), 'W_in': s(ks[1], (D_INNER, D_MODEL)), 'W_gate': s(ks[2], (D_INNER, D_MODEL)), 'W_xproj': s(ks[3], (DT_RANK + 2 * D_STATE, D_INNER)), 'W_dt': s(ks[4], (D_INNER, DT_RANK)), 'b_dt': jnp.full((D_INNER,), -4.6, jnp.float32), 'A_log': jnp.log(jnp.tile(jnp.arange(1, D_STATE + 1, dtype=jnp.float32), (D_INNER, 1))), 'D_skip': jnp.ones((D_INNER,), jnp.float32), 'W_out': s(ks[5], (D_MODEL, D_INNER)), 'w_ffn_norm': jnp.ones((D_MODEL,), jnp.float32), 'W_up': s(ks[6], (H_FFN, D_MODEL)), 'W_gate_ffn': s(ks[7], (H_FFN, D_MODEL)), 'W_down': s(ks[8], (D_MODEL, H_FFN))}
    _L0_attn_all = _L0_attn_setup()
    _L0_attn_in = {k: v for k, v in _L0_attn_all.items() if k in ('w_norm1', 'W_in', 'W_gate', 'W_xproj', 'W_dt', 'b_dt', 'A_log', 'D_skip', 'W_out', 'w_ffn_norm', 'W_up', 'W_gate_ffn', 'W_down')}
    del _L0_attn_all

    def _L0_ffn_setup():
        import jax, jax.numpy as jnp
        import numpy as np
        E = 8
        K = 2
        D = 192
        F = 4 * D
        key = jax.random.key(seed)
        ks = jax.random.split(key, 10)
        s_exp = 0.02
        return {'x': jax.random.normal(ks[0], (4, 256, D), jnp.float32), 'W1': jax.random.normal(ks[1], (E, F, D), jnp.float32) * s_exp, 'b1': jax.random.normal(ks[2], (E, F), jnp.float32) * s_exp, 'W2': jax.random.normal(ks[3], (E, D, F), jnp.float32) * s_exp, 'b2': jax.random.normal(ks[4], (E, D), jnp.float32) * s_exp, 'Wr1': jax.random.normal(ks[5], (D, D), jnp.float32) * s_exp, 'br1': jax.random.normal(ks[6], (D,), jnp.float32) * s_exp, 'Wr2': jax.random.normal(ks[7], (E, D), jnp.float32) * s_exp, 'br2': jax.random.normal(ks[8], (E,), jnp.float32) * s_exp}
    _L0_ffn_all = _L0_ffn_setup()
    _L0_ffn_in = {k: v for k, v in _L0_ffn_all.items() if k in ('W1', 'b1', 'W2', 'b2', 'Wr1', 'br1', 'Wr2', 'br2')}
    del _L0_ffn_all

    def _L1_attn_setup():
        import jax, jax.numpy as jnp
        import numpy as np
        NUM_HEADS = 12
        key = jax.random.key(seed)
        ks = jax.random.split(key, 5)
        B, S, D = (4, 512, 192)
        scale = 0.02
        return {'hidden_states': jax.random.normal(ks[0], (B, S, D), dtype=jnp.float32), 'c_attn_w': jax.random.normal(ks[1], (D, 3 * D), dtype=jnp.float32) * scale, 'c_attn_b': jax.random.normal(ks[2], (3 * D,), dtype=jnp.float32) * scale, 'c_proj_w': jax.random.normal(ks[3], (D, D), dtype=jnp.float32) * scale, 'c_proj_b': jax.random.normal(ks[4], (D,), dtype=jnp.float32) * scale}
    _L1_attn_all = _L1_attn_setup()
    _L1_attn_in = {k: v for k, v in _L1_attn_all.items() if k in ('c_attn_w', 'c_attn_b', 'c_proj_w', 'c_proj_b')}
    del _L1_attn_all

    def _L1_ffn_setup():
        import jax, jax.numpy as jnp
        import numpy as np
        DIM = 192
        MOE_INTER = 512
        N_EXPERTS = 16
        TOP_K = 2
        SHARED_INTER = 2 * 512
        ROUTE_SCALE = 1.0
        B, S = (8, 196)
        key = jax.random.key(seed)
        ks = jax.random.split(key, 8)
        sc = 0.02
        return {'x': jax.random.normal(ks[0], (B, S, DIM), jnp.float32), 'gate_w': jax.random.normal(ks[1], (N_EXPERTS, DIM), jnp.float32) * sc, 'w1': jax.random.normal(ks[2], (N_EXPERTS, MOE_INTER, DIM), jnp.float32) * sc, 'w2': jax.random.normal(ks[3], (N_EXPERTS, DIM, MOE_INTER), jnp.float32) * sc, 'w3': jax.random.normal(ks[4], (N_EXPERTS, MOE_INTER, DIM), jnp.float32) * sc, 'sw1': jax.random.normal(ks[5], (SHARED_INTER, DIM), jnp.float32) * sc, 'sw2': jax.random.normal(ks[6], (DIM, SHARED_INTER), jnp.float32) * sc, 'sw3': jax.random.normal(ks[7], (SHARED_INTER, DIM), jnp.float32) * sc}
    _L1_ffn_all = _L1_ffn_setup()
    _L1_ffn_in = {k: v for k, v in _L1_ffn_all.items() if k in ('gate_w', 'w1', 'w2', 'w3', 'sw1', 'sw2', 'sw3')}
    del _L1_ffn_all
    return {'x': x, 'mask_BS_i1_0': mask_BS_i1_0, 'L0_tok_tok_table': _L0_tok_in['tok_table'], 'L0_tok_seg_table': _L0_tok_in['seg_table'], 'L0_tok_pos_table': _L0_tok_in['pos_table'], 'L0_tok_gamma': _L0_tok_in['gamma'], 'L0_tok_beta': _L0_tok_in['beta'], 'L0_attn_w_norm1': _L0_attn_in['w_norm1'], 'L0_attn_W_in': _L0_attn_in['W_in'], 'L0_attn_W_gate': _L0_attn_in['W_gate'], 'L0_attn_W_xproj': _L0_attn_in['W_xproj'], 'L0_attn_W_dt': _L0_attn_in['W_dt'], 'L0_attn_b_dt': _L0_attn_in['b_dt'], 'L0_attn_A_log': _L0_attn_in['A_log'], 'L0_attn_D_skip': _L0_attn_in['D_skip'], 'L0_attn_W_out': _L0_attn_in['W_out'], 'L0_attn_w_ffn_norm': _L0_attn_in['w_ffn_norm'], 'L0_attn_W_up': _L0_attn_in['W_up'], 'L0_attn_W_gate_ffn': _L0_attn_in['W_gate_ffn'], 'L0_attn_W_down': _L0_attn_in['W_down'], 'L0_ffn_W1': _L0_ffn_in['W1'], 'L0_ffn_b1': _L0_ffn_in['b1'], 'L0_ffn_W2': _L0_ffn_in['W2'], 'L0_ffn_b2': _L0_ffn_in['b2'], 'L0_ffn_Wr1': _L0_ffn_in['Wr1'], 'L0_ffn_br1': _L0_ffn_in['br1'], 'L0_ffn_Wr2': _L0_ffn_in['Wr2'], 'L0_ffn_br2': _L0_ffn_in['br2'], 'L1_attn_c_attn_w': _L1_attn_in['c_attn_w'], 'L1_attn_c_attn_b': _L1_attn_in['c_attn_b'], 'L1_attn_c_proj_w': _L1_attn_in['c_proj_w'], 'L1_attn_c_proj_b': _L1_attn_in['c_proj_b'], 'L1_ffn_gate_w': _L1_ffn_in['gate_w'], 'L1_ffn_w1': _L1_ffn_in['w1'], 'L1_ffn_w2': _L1_ffn_in['w2'], 'L1_ffn_w3': _L1_ffn_in['w3'], 'L1_ffn_sw1': _L1_ffn_in['sw1'], 'L1_ffn_sw2': _L1_ffn_in['sw2'], 'L1_ffn_sw3': _L1_ffn_in['sw3']}

def reference(x, mask_BS_i1_0, L0_tok_tok_table, L0_tok_seg_table, L0_tok_pos_table, L0_tok_gamma, L0_tok_beta, L0_attn_w_norm1, L0_attn_W_in, L0_attn_W_gate, L0_attn_W_xproj, L0_attn_W_dt, L0_attn_b_dt, L0_attn_A_log, L0_attn_D_skip, L0_attn_W_out, L0_attn_w_ffn_norm, L0_attn_W_up, L0_attn_W_gate_ffn, L0_attn_W_down, L0_ffn_W1, L0_ffn_b1, L0_ffn_W2, L0_ffn_b2, L0_ffn_Wr1, L0_ffn_br1, L0_ffn_Wr2, L0_ffn_br2, L1_attn_c_attn_w, L1_attn_c_attn_b, L1_attn_c_proj_w, L1_attn_c_proj_b, L1_ffn_gate_w, L1_ffn_w1, L1_ffn_w2, L1_ffn_w3, L1_ffn_sw1, L1_ffn_sw2, L1_ffn_sw3):
    import jax
    import jax.numpy as jnp

    def _L0_tok_ref(token_ids, segment_ids, tok_table, seg_table, pos_table, gamma, beta):
        import jax, jax.numpy as jnp
        import numpy as np
        VOCAB = 30522
        SEG_VOCAB = 2
        D_MODEL = 192
        MAX_LEN = 128
        B, S = (64, 128)
        EPS = 1e-05
        seq_len = token_ids.shape[1]
        emb = tok_table[token_ids] + seg_table[segment_ids] + pos_table[:seq_len][None, :, :]
        mu = jnp.mean(emb, axis=-1, keepdims=True)
        var = jnp.mean(jnp.square(emb - mu), axis=-1, keepdims=True)
        out = (emb - mu) * jax.lax.rsqrt(var + EPS) * gamma + beta
        return out

    def _L0_attn_ref(x, w_norm1, W_in, W_gate, W_xproj, W_dt, b_dt, A_log, D_skip, W_out, w_ffn_norm, W_up, W_gate_ffn, W_down):
        import jax, jax.numpy as jnp
        import numpy as np
        D_MODEL = 192
        D_INNER = 384
        D_STATE = 16
        DT_RANK = 96
        H_FFN = 512
        B, L = (1, 512)
        EPS = 1e-06

        def rmsnorm(x, w):
            return x * jax.lax.rsqrt(jnp.mean(x * x, axis=-1, keepdims=True) + EPS) * w

        def selective_scan(z, W_xproj, W_dt, b_dt, A_log, D_skip):
            xdbl = jnp.einsum('bld,kd->blk', z, W_xproj)
            dt_in, Bm, Cm = jnp.split(xdbl, [DT_RANK, DT_RANK + D_STATE], axis=-1)
            dt = jax.nn.softplus(jnp.einsum('blr,dr->bld', dt_in, W_dt) + b_dt)
            A = -jnp.exp(A_log)
            A_bar = jnp.exp(dt[..., None] * A)
            Bx = (dt * z)[..., None] * Bm[:, :, None, :]

            def comb(e1, e2):
                a1, b1 = e1
                a2, b2 = e2
                return (a1 * a2, a2 * b1 + b2)
            _, h = jax.lax.associative_scan(comb, (A_bar, Bx), axis=1)
            y = jnp.einsum('blds,bls->bld', h, Cm) + D_skip * z
            return y
        residual = x
        h = rmsnorm(x, w_norm1)
        z = h @ W_in.T
        z = z * jax.nn.sigmoid(h @ W_gate.T)
        y = selective_scan(z, W_xproj, W_dt, b_dt, A_log, D_skip)
        x = residual + y @ W_out.T
        hf = rmsnorm(x, w_ffn_norm)
        ffn = jax.nn.silu(hf @ W_gate_ffn.T) * (hf @ W_up.T) @ W_down.T
        return x + ffn

    def _L0_ffn_ref(x, W1, b1, W2, b2, Wr1, br1, Wr2, br2):
        import jax, jax.numpy as jnp
        import numpy as np
        E = 8
        K = 2
        D = 192
        F = 4 * D
        h = jax.nn.relu(jnp.einsum('bsd,hd->bsh', x, Wr1) + br1)
        score = jnp.einsum('bsd,ed->bse', h, Wr2) + br2
        _, idx = jax.lax.top_k(score, K)
        mask = (jax.nn.one_hot(idx, E) > 0).any(axis=-2)
        w = jax.nn.softmax(jnp.where(mask, score, -jnp.inf), axis=-1)
        out = jnp.zeros_like(x)
        for e in range(E):
            mid = jax.nn.relu(jnp.einsum('bsd,fd->bsf', x, W1[e]) + b1[e])
            ye = jnp.einsum('bsf,df->bsd', mid, W2[e]) + b2[e]
            out = out + w[..., e:e + 1] * ye
        return out

    def _L1_attn_ref(hidden_states, c_attn_w, c_attn_b, c_proj_w, c_proj_b):
        import jax, jax.numpy as jnp
        import numpy as np
        NUM_HEADS = 12
        B, S, D = hidden_states.shape
        H = NUM_HEADS
        hd = D // H
        qkv = hidden_states @ c_attn_w + c_attn_b
        q, k, v = jnp.split(qkv, 3, axis=-1)

        def split_heads(t):
            return t.reshape(B, S, H, hd).transpose(0, 2, 1, 3)
        q, k, v = (split_heads(q), split_heads(k), split_heads(v))
        scores = jnp.einsum('bhqd,bhkd->bhqk', q, k) / jnp.asarray(np.sqrt(hd), dtype=q.dtype)
        causal = jnp.tril(jnp.ones((S, S), dtype=bool))
        mask_value = jnp.finfo(scores.dtype).min
        scores = jnp.where(causal[None, None, :, :], scores, mask_value)
        attn = jax.nn.softmax(scores, axis=-1)
        out = jnp.einsum('bhqk,bhkd->bhqd', attn, v)
        out = out.transpose(0, 2, 1, 3).reshape(B, S, D)
        return out @ c_proj_w + c_proj_b

    def _L1_ffn_ref(x, gate_w, w1, w2, w3, sw1, sw2, sw3):
        import jax, jax.numpy as jnp
        import numpy as np
        DIM = 192
        MOE_INTER = 512
        N_EXPERTS = 16
        TOP_K = 2
        SHARED_INTER = 2 * 512
        ROUTE_SCALE = 1.0
        B, S = (8, 196)
        Bb, Ss, D = x.shape
        xf = x.reshape(-1, D)
        T = xf.shape[0]
        scores = jax.nn.softmax(xf @ gate_w.T, axis=-1)
        topw, topi = jax.lax.top_k(scores, TOP_K)
        topw = topw * ROUTE_SCALE
        comb = jnp.zeros((T, N_EXPERTS), xf.dtype).at[jnp.arange(T)[:, None], topi].set(topw)
        h = jax.nn.silu(jnp.einsum('td,eid->tei', xf, w1)) * jnp.einsum('td,eid->tei', xf, w3)
        h = h * comb[:, :, None]
        y = jnp.einsum('tei,edi->td', h, w2)
        z = jax.nn.silu(xf @ sw1.T) * (xf @ sw3.T) @ sw2.T
        return (y + z).reshape(Bb, Ss, D)
    h = _L0_tok_ref(x, mask_BS_i1_0, L0_tok_tok_table, L0_tok_seg_table, L0_tok_pos_table, L0_tok_gamma, L0_tok_beta)
    h = h + _L0_attn_ref(_layernorm(h, axis=-1), L0_attn_w_norm1, L0_attn_W_in, L0_attn_W_gate, L0_attn_W_xproj, L0_attn_W_dt, L0_attn_b_dt, L0_attn_A_log, L0_attn_D_skip, L0_attn_W_out, L0_attn_w_ffn_norm, L0_attn_W_up, L0_attn_W_gate_ffn, L0_attn_W_down)
    h = h + _L0_ffn_ref(_layernorm(h, axis=-1), L0_ffn_W1, L0_ffn_b1, L0_ffn_W2, L0_ffn_b2, L0_ffn_Wr1, L0_ffn_br1, L0_ffn_Wr2, L0_ffn_br2)
    h = h + _L1_attn_ref(_layernorm(h, axis=-1), L1_attn_c_attn_w, L1_attn_c_attn_b, L1_attn_c_proj_w, L1_attn_c_proj_b)
    h = h + _L1_ffn_ref(_layernorm(h, axis=-1), L1_ffn_gate_w, L1_ffn_w1, L1_ffn_w2, L1_ffn_w3, L1_ffn_sw1, L1_ffn_sw2, L1_ffn_sw3)
    return h

_drawn_inputs = setup_inputs


def setup_inputs(seed=0):
    import zlib

    import numpy as np

    out = dict(_drawn_inputs(seed))
    spreads = {'L0_tok_gamma': (1.0, 0.2),
     'L0_tok_beta': (0.0, 0.1),
     'L0_attn_w_norm1': (1.0, 0.6),
     'L0_attn_b_dt': (-4.599999904632568, 0.6),
     'L0_attn_D_skip': (1.0, 0.6),
     'L0_attn_w_ffn_norm': (1.0, 0.6)}
    factors = {'L0_attn_W_gate': 8.0,
     'L0_attn_W_xproj': 8.0,
     'L0_attn_W_dt': 8.0,
     'L0_attn_A_log': 8.0,
     'L0_attn_W_up': 5.535,
     'L0_attn_W_gate_ffn': 5.697,
     'L0_attn_W_down': 5.593,
     'L0_ffn_b1': 24.251,
     'L0_ffn_b2': 8.0,
     'L0_ffn_br1': 15.141,
     'L1_attn_c_attn_b': 8.0,
     'L1_attn_c_proj_w': 2.686,
     'L1_attn_c_proj_b': 6.042,
     'L1_ffn_gate_w': 8.0,
     'L1_ffn_w1': 8.0,
     'L1_ffn_w2': 8.0,
     'L1_ffn_w3': 8.0,
     'L1_ffn_sw1': 4.638,
     'L1_ffn_sw2': 4.599,
     'L1_ffn_sw3': 4.559,
     'L0_ffn_br2': 2.681,
     'L0_ffn_Wr1': 2.928}
    for name, (base, spread) in spreads.items():
        noise = np.random.default_rng([zlib.crc32(name.encode()), seed]).standard_normal(out[name].shape)
        drawn = base * np.exp(spread * noise) if base else spread * noise
        out[name] = jnp.asarray(drawn.astype(out[name].dtype))
    for name, factor in factors.items():
        out[name] = (out[name] * factor).astype(out[name].dtype)
    return out
```

```python
from contextlib import ExitStack

import concourse.bass as bass
from concourse import mybir

F32 = mybir.dt.float32
I32 = mybir.dt.int32
BF16 = mybir.dt.bfloat16
ACT = mybir.ActivationFunctionType
ALU = mybir.AluOpType
AXX = mybir.AxisListType.X
ds = bass.ds

P = 128
B = 16
D = 192
KH = 96
CT = 4
NCH = B // CT
CN = CT * P
NST = 16
DG = 3
FF0 = 4
E0, E1 = 8, 16
EF0, EF1 = 6, 4
SF = 8
H = 12
HD = D // H
NEG = -3.0e38
LN_EPS, RMS_EPS = 1e-5, 1e-6


def blocks_needed(experts):
    n = 2 * B * P // P + experts - 1
    return n + n % 2


NB0, NB1 = blocks_needed(E0), blocks_needed(E1)

C_ID, C_TRI, C_ONE, C_CAUSAL = 0, 128, 256, 384
C_SEL = 512
C_REV = C_SEL + 32
C_THR = C_REV + 16
C_BLK = C_THR + 16
C_RES = C_BLK + NB1
C_END = C_RES + 256
R_GAM, R_BET, R_BV, R_BP, R_BR2, R_END = 0, D, 2 * D, 3 * D, 4 * D, 4 * D + E0
V_N1, V_NF, V_BR1, V_BDT, V_DSK, V_BQK, V_ALOG, V_END = 0, 2, 4, 6, 9, 12, 18, 18 + DG * NST


def tower(nc, tok, seg, tok_tab, seg_tab, pos_tab, consts, rows, cols, w_in, w_gate, w_xdt, w_xbc, w_dt, w_out,
          w_up, w_gf, w_down, w_r1, w_r2, w_qk, w_v, w_proj, w_g, w_s1, w_s3, w_s2, e0_in, e0_out, e1_in, e1_out,
          out):
    with ExitStack() as ctx:
        def sb(name, shape, dt=F32):
            return ctx.enter_context(nc.sbuf_tensor(name, shape, dt))

        def sem(name):
            return ctx.enter_context(nc.semaphore(name))

        ps = ctx.enter_context(nc.psum_tensor("ps", [P, 8, 512], F32))
        sorted_rows = [nc.dram_tensor(f"sorted{n}", (nb * P, D), F32, kind="Internal").ap() for n, nb in ((0, NB0), (1, NB1))]
        expert_rows = [nc.dram_tensor(f"expert{n}", (nb * P, D), F32, kind="Internal").ap() for n, nb in ((0, NB0), (1, NB1))]

        h_rows = sb("h_rows", [P, B, D])
        x_rows = sb("x_rows", [P, B, D])
        tok_i = sb("tok_i", [P, B], I32)
        seg_i = sb("seg_i", [P, B], I32)
        cst = sb("cst", [P, C_END])
        row = sb("row", [P, R_END])
        col = sb("col", [P, V_END])
        pos = sb("pos", [P, D])
        sel = sb("sel", [KH, 32], BF16)
        neg_a = sb("neg_a", [P, DG, NST])
        diag_d = sb("diag_d", [P, DG, P])
        win = sb("win", [KH, 2, DG * P])
        wgate = sb("wgate", [KH, 2, DG * P])
        wxdt = sb("wxdt", [P, DG, KH])
        wxbc = sb("wxbc", [P, DG, KH])
        wdt = sb("wdt", [KH, DG * P])
        wout = sb("wout", [P, DG, D])
        wup = sb("wup", [KH, 2, FF0 * P])
        wgf = sb("wgf", [KH, 2, FF0 * P])
        wdown = sb("wdown", [P, FF0, D])
        wr1 = sb("wr1", [KH, 2, D])
        wr2 = sb("wr2", [KH, 2, E0])
        wqk = sb("wqk", [KH, 2, 6 * P])
        wv = sb("wv", [KH, 2, D])
        wproj = sb("wproj", [KH, 2, D])
        wg = sb("wg", [KH, 2, E1])
        ws1 = sb("ws1", [KH, 2, SF * P])
        ws3 = sb("ws3", [KH, 2, SF * P])
        ws2 = sb("ws2", [P, SF, D])
        ew_in = [sb(f"ew_in{k}", [KH, 2048]) for k in range(2)]
        ew_out = [sb(f"ew_out{k}", [P, EF0 * D + EF0 + D]) for k in range(2)]

        er = sb("er", [P, CT, D])
        mr = sb("mr", [P, CT, D])
        nr = sb("nr", [P, CT, D])
        xT = sb("xT", [KH, 2, CN])
        st = sb("st", [P, CT, 6])
        mv = sb("mv", [P, CT, 2])
        vv = sb("vv", [P, CT])
        vh = sb("vh", [P, CT])
        yy = sb("yy", [P, CT])
        tt = sb("tt", [P, CT])
        ti = sb("ti", [P, CT], I32)
        arena = sb("arena", [P, 12 * 1536])

        def part(n, words, parts=P):
            return arena[0:parts, n:n + words]

        def wide(n):
            return part(n * 1536, 1536).rearrange("p (g t) -> p g t", g=DG)

        zT, dtT, uT, tA = wide(0), wide(1), wide(2), wide(3)
        dec, bxs, hid, hc = [wide(4), wide(5)], [wide(6), wide(7)], [wide(8), wide(9)], [wide(10), wide(11)]
        tB = wide(8)
        actT0 = part(8 * 1536, FF0 * CN).rearrange("p (f t) -> p f t", f=FF0)
        hrT = part(10 * 1536, 2 * CN, KH).rearrange("p (f t) -> p f t", f=2)
        cs = sb("cs", [P, 2, CN])
        dti = cs[0:KH, 0, :]
        bc_r = cs[0:KH, 1, :]
        bc_p = sb("bc_p", [KH, CN], BF16)
        bc_b = nr[0:KH, 0:2, :].rearrange("p j d -> p (j d)").bitcast(BF16)[:, 0:CN]
        g1 = part(0, B * D).rearrange("p (t d) -> p t d", t=B)
        g2 = part(B * D, B * D).rearrange("p (t d) -> p t d", t=B)
        qkT = part(6144, 6 * CN).rearrange("p (f t) -> p f t", f=6)
        vr = part(9216, CT * H * (HD + 1)).rearrange("p (t h d) -> p t h d", t=CT, h=H)
        sm = [part(n, H * P).rearrange("p (b a k) -> p b a k", b=4, a=3) for n in (10240, 13824)]
        pT = [part(n, H * P).rearrange("p (h q) -> p h q", h=H) for n in (11776, 15360)]
        rden = part(13312, H)
        smax = part(13328, H)
        actT1 = part(13824, SF * CN).rearrange("p (f t) -> p f t", f=SF)
        xb = [part(6144 + 256 * k, D) for k in range(2)]
        xbT = [part(6656 + 256 * k, 2 * P, KH).rearrange("p (k t) -> p k t", k=2) for k in range(2)]
        hbT = [part(7168 + 768 * k, EF0 * P).rearrange("p (f t) -> p f t", f=EF0) for k in range(2)]
        yb = [part(8704 + 256 * k, D) for k in range(2)]
        NR = 256

        def rt(n, words=NR):
            return part(9216 + NR * n, words)

        sc1 = sb("sc1", [P, B, E1])
        sc0 = sc1[:, :, 0:E0]
        gate_w = sb("gate_w", [P, 2, B])
        pos_i = sb("pos_i", [P, 2, B], I32)
        eid = sb("eid", [1, NB1], I32)
        zero = arena[:, 0:768]

        ident = cst[:, C_ID:C_ID + P]
        gamma_b = row[:, R_GAM:R_GAM + D].rearrange("p (a d) -> p a d", a=1).broadcast_to((P, CT, D))
        beta_b = row[:, R_BET:R_BET + D].rearrange("p (a d) -> p a d", a=1).broadcast_to((P, CT, D))
        pos_b = pos[:, :].rearrange("p (a d) -> p a d", a=1).broadcast_to((P, CT, D))
        bproj_b = row[:, R_BP:R_BP + D].rearrange("p (a d) -> p a d", a=1).broadcast_to((P, CT, D))

        s_idx, s_wa, s_wb, s_zero, s_zz = sem("s_idx"), sem("s_wa"), sem("s_wb"), sem("s_zero"), sem("s_zz")
        s_emb = sem("s_emb")
        s_cst, s_neg = sem("s_cst"), sem("s_neg")
        s_hn, s_hnT, s_xT = sem("s_hn"), sem("s_hnT"), sem("s_xT")
        s_z, s_gate, s_sig, s_zs = sem("s_z"), sem("s_gate"), sem("s_sig"), sem("s_zs")
        s_xd, s_xbc, s_dti, s_bcp, s_dt, s_sp, s_u = [sem(n) for n in ("s_xd", "s_xbc", "s_dti", "s_bcp", "s_dt", "s_sp", "s_u")]
        s_bb, s_cb, s_bfree, s_cfree = sem("s_bb"), sem("s_cb"), sem("s_bfree"), sem("s_cfree")
        s_decfree, s_cbfree = sem("s_decfree"), sem("s_cbfree")
        s_dec, s_scan, s_cs, s_hc, s_sumd = sem("s_dec"), sem("s_scan"), sem("s_cs"), sem("s_hc"), sem("s_sumd")
        s_y, s_yT, s_op = sem("s_y"), sem("s_yT"), sem("s_op")
        s_hf, s_hfT, s_fT = sem("s_hf"), sem("s_hfT"), sem("s_fT")
        s_gu, s_sl, s_act, s_dn = sem("s_gu"), sem("s_sl"), sem("s_act"), sem("s_dn")
        s_xn, s_xnT, s_rT, s_r1, s_hr, s_sc, s_ch = [sem(n) for n in ("s_xn", "s_xnT", "s_rT", "s_r1", "s_hr", "s_sc", "s_ch")]
        s_mask, s_rank, s_dl, s_ex, s_pos = [[sem(f"{n}{m}") for m in range(2)] for n in ("s_mask", "s_rank", "s_dl", "s_ex", "s_pos")]
        s_scat = [sem(f"s_scat{m}") for m in range(2)]
        s_w1 = [[sem(f"s_w1_{m}{k}") for k in range(2)] for m in range(2)]
        s_w2 = [[sem(f"s_w2_{m}{k}") for k in range(2)] for m in range(2)]
        s_xb = [[sem(f"s_xb_{m}{k}") for k in range(2)] for m in range(2)]
        s_w1f = [[sem(f"s_w1f_{m}{k}") for k in range(2)] for m in range(2)]
        s_w2f = [[sem(f"s_w2f_{m}{k}") for k in range(2)] for m in range(2)]
        s_xbf = [[sem(f"s_xbf_{m}{k}") for k in range(2)] for m in range(2)]
        s_bt, s_bx, s_bh, s_ba, s_by, s_yb, s_bg = [[sem(f"{n}{m}") for m in range(2)] for n in ("s_bt", "s_bx", "s_bh", "s_ba", "s_by", "s_yb", "s_bg")]
        s_ybf = [[sem(f"s_ybf_{m}{k}") for k in range(2)] for m in range(2)]
        s_yo = [[sem(f"s_yo_{m}{k}") for k in range(2)] for m in range(2)]
        s_g = [sem(f"s_g{m}") for m in range(2)]
        t_xn, t_xnT, t_xT, t_qk, t_qkT, t_v, t_vr = [sem(n) for n in ("t_xn", "t_xnT", "t_xT", "t_qk", "t_qkT", "t_v", "t_vr")]
        t_s, t_ms, t_sm, t_p, t_pt, t_pT, t_o, t_or = [sem(n) for n in ("t_s", "t_ms", "t_sm", "t_p", "t_pt", "t_pT", "t_o", "t_or")]
        t_oT, t_oTs, t_pr, t_fn, t_fnT, t_fT = [sem(n) for n in ("t_oT", "t_oTs", "t_pr", "t_fn", "t_fnT", "t_fT")]
        t_rs, t_gu, t_sl, t_act, t_dn, t_ch = [sem(n) for n in ("t_rs", "t_gu", "t_sl", "t_act", "t_dn", "t_ch")]
        s_fin, s_out = sem("s_fin"), sem("s_out")

        ctx.enter_context(nc.allow_non_contiguous_dma("small vectors"))
        block = ctx.enter_context(nc.Block())

        @block.sync
        def _(sp):
            sp.dma_start(tok_i[:, :], tok).then_inc(s_idx, 16)
            sp.dma_start(seg_i[:, :], seg).then_inc(s_idx, 16)
            first = [(cst[:, :], consts), (row[:, :], rows.broadcast_to((P, R_END))), (col[:, :], cols), (pos[:, :], pos_tab),
                     (win[:, :, :], w_in), (wgate[:, :, :], w_gate), (wxdt[:, :, :], w_xdt), (wxbc[:, :, :], w_xbc),
                     (wdt[:, :], w_dt), (wout[:, :, :], w_out), (wup[:, :, :], w_up), (wgf[:, :, :], w_gf),
                     (wdown[:, :, :], w_down), (wr1[:, :, :], w_r1), (wr2[:, :, :], w_r2)]
            later = [(wqk[:, :, :], w_qk), (wv[:, :, :], w_v), (wproj[:, :, :], w_proj), (wg[:, :, :], w_g),
                     (ws1[:, :, :], w_s1), (ws3[:, :, :], w_s3), (ws2[:, :, :], w_s2)]
            for dst, src in first:
                sp.dma_start(dst, src).then_inc(s_wa, 16)
            for dst, src in later:
                sp.dma_start(dst, src).then_inc(s_wb, 16)
            sp.wait_ge(s_zz, 1)
            for m, nb in ((0, NB0), (1, NB1)):
                dst = sorted_rows[m].rearrange("(p n c) d -> p n (c d)", p=P, c=4)
                sp.dma_start(dst, zero.rearrange("p (a c) -> p a c", a=1).broadcast_to((P, nb // 4, 768)))\
                  .then_inc(s_zero, 16)

            def expert_loads(m, nb, t_in, t_out, n_in, n_out):
                sp.wait_ge(s_pos[m], 1)
                sp.wait_ge(s_scat[m], 32 * 16)
                with sp.Fori(0, nb // 2) as i:
                    for k in range(2):
                        sp.wait_ge(s_xbf[m][k], i + 1)
                        sp.nop(nofuse=True)
                        sp.dma_start(xb[k], sorted_rows[m][ds((i * 2 + k) * P, P), :]).then_inc(s_xb[m][k], 16)
                    e = [sp.value_load(eid[0:1, ds(i * 2 + k, 1)], min_val=0, max_val=t_in.shape[0] - 1) for k in range(2)]
                    for k in range(2):
                        sp.wait_ge(s_w1f[m][k], i + 1)
                        sp.nop(nofuse=True)
                        sp.dma_start(ew_in[k][:, 0:n_in], t_in[ds(e[k], 1), :, :].rearrange("a p n -> (a p) n"))\
                          .then_inc(s_w1[m][k], 16)
                    for k in range(2):
                        sp.wait_ge(s_w2f[m][k], i + 1)
                        sp.nop(nofuse=True)
                        sp.dma_start(ew_out[k][:, 0:n_out], t_out[ds(e[k], 1), :, :].rearrange("a p n -> (a p) n"))\
                          .then_inc(s_w2[m][k], 16)

            expert_loads(0, NB0, e0_in, e0_out, 2 * EF0 * P, EF0 * D + EF0 + D)
            expert_loads(1, NB1, e1_in, e1_out, 4 * EF1 * P, EF1 * D)
            for c in range(NCH):
                sp.wait_ge(s_fin, c + 1)
                sp.dma_start(out[c * CT:(c + 1) * CT].rearrange("t p d -> p t d"), h_rows[:, c * CT:(c + 1) * CT, :])\
                  .then_inc(s_out, 16)
            sp.wait_ge(s_out, NCH * 16)

        @block.gpsimd
        def _(pool):
            pool.wait_ge(s_idx, 32)
            for c in range(NCH):
                for t in range(c * CT, (c + 1) * CT):
                    pool.indirect_dma_start(h_rows[:, t, :], None, tok_tab, bass.IndirectOffsetOnAxis(tok_i[:, t:t + 1], 0))\
                        .then_inc(s_emb, 16)
                    pool.indirect_dma_start(x_rows[:, t, :], None, seg_tab, bass.IndirectOffsetOnAxis(seg_i[:, t:t + 1], 0))\
                        .then_inc(s_emb, 16)
                pool.wait_ge(s_emb, (c + 1) * 2 * CT * 16)

            pool.sem_inc(s_cfree, 2)
            with pool.Fori(0, NCH) as i:
                with pool.Fori(0, NST // 2) as q:
                    for k in range(2):
                        n = i * NST + q * 2 + k
                        pool.wait_ge(s_scan, n + 1)
                        pool.wait_ge(s_cs, n + 1)
                        pool.wait_ge(s_sumd, n + 1)
                        pool.tensor_tensor(hc[k], hid[k], cs[:, k:k + 1, :].broadcast_to((P, DG, CN)), ALU.mult)\
                            .then_inc(s_hc, 1)
                        pool.drain().then_inc(s_cfree, 1)

            def scatter(m):
                pool.wait_ge(s_zero, 32)
                pool.wait_ge(s_pos[m], 1)
                for t in range(B):
                    for r in range(2):
                        pool.indirect_dma_start(sorted_rows[m], bass.IndirectOffsetOnAxis(pos_i[:, r, t:t + 1], 0),
                                                x_rows[:, t, :], None).then_inc(s_scat[m], 16)

            def store_blocks(m, nb):
                with pool.Fori(0, nb // 2) as i:
                    for k in range(2):
                        pool.wait_ge(s_yb[m], i * 2 + k + 1)
                        pool.nop(nofuse=True)
                        pool.dma_start(expert_rows[m][ds((i * 2 + k) * P, P), :], yb[k]).then_inc(s_yo[m][k], 16)
                        pool.wait_ge(s_yo[m][k], i * 16 + 16)
                        pool.nop(nofuse=True)
                        pool.drain().then_inc(s_ybf[m][k], 1)

            def gather(m, nb):
                for k in range(2):
                    pool.wait_ge(s_yo[m][k], 16 * (nb // 2))
                for c in range(NCH):
                    for t in range(c * CT, (c + 1) * CT):
                        for r, g in ((0, g1), (1, g2)):
                            pool.indirect_dma_start(g[:, t, :], None, expert_rows[m],
                                                    bass.IndirectOffsetOnAxis(pos_i[:, r, t:t + 1], 0)).then_inc(s_g[m], 16)
                    pool.wait_ge(s_g[m], (c + 1) * 2 * CT * 16)

            for m, nb in ((0, NB0), (1, NB1)):
                scatter(m)
                store_blocks(m, nb)
                gather(m, nb)

        @block.scalar
        def _(act):
            act.wait_ge(s_wa, 15 * 16)
            act.activation(neg_a[:, :, :], col[:, V_ALOG:V_END].rearrange("p (g s) -> p g s", g=DG), ACT.Exp).then_inc(s_neg, 1)
            act.sem_inc(s_cbfree, 2)
            with act.Fori(0, NCH) as i:
                for g in range(DG):
                    act.wait_ge(s_gate, i * DG + g + 1)
                    act.activation(tA[:, g, :], ps[:, 5 + g, :], ACT.Sigmoid).then_inc(s_sig, 1)
                act.wait_ge(s_xd, i + 1)
                act.activation(dti, ps[0:KH, 0, :], ACT.Copy).then_inc(s_dti, 1)
                for g in range(DG):
                    act.wait_ge(s_dt, i * DG + g + 1)
                    bdt = col[:, V_BDT + g:V_BDT + g + 1]
                    act.activation(tA[:, g, :], ps[:, 5 + g, :], ACT.Abs, bias=bdt)
                    act.activation(dtT[:, g, :], ps[:, 5 + g, :], ACT.Relu, bias=bdt)
                act.drain()
                act.activation(tB, tA, ACT.Exp, scale=-1.0)
                act.drain()
                act.activation(tA, tB, ACT.Ln, bias=1.0)
                act.drain().then_inc(s_sp, 1)
                act.wait_ge(s_u, i + 1)
                with act.Fori(0, NST // 2) as q:
                    for k in range(2):
                        n = i * NST + q * 2 + k
                        act.wait_ge(s_decfree, n + 1)
                        for g in range(DG):
                            o = dec[k][:, g, :].rearrange("p (b t) -> p b t", b=CT)
                            s = dtT[:, g, :].rearrange("p (b t) -> p b t", b=CT)
                            act.activation(o[:, :, 1:P], s[:, :, 1:P], ACT.Exp,
                                           scale=neg_a[:, g, ds(q * 2 + k, 1)])
                        act.drain().then_inc(s_dec, 1)
                        act.wait_ge(s_cb, n + 1)
                        act.wait_ge(s_cfree, n + 1)
                        act.activation(cs[:, k, :], ps[:, 5 + k, :], ACT.Copy).then_inc(s_cs, 1)
                        act.drain().then_inc(s_cbfree, 1)
                act.wait_ge(s_y, i + 1)
                act.activation(uT, ps[:, 2:5, :], ACT.Copy).then_inc(s_yT, 1)
                for f in range(FF0):
                    act.wait_ge(s_gu, i * FF0 + f + 1)
                    act.activation(actT0[:, f, :], ps[:, 4 + f, :], ACT.Silu).then_inc(s_sl, 1)
                act.wait_ge(s_r1, i + 1)
                for k in range(2):
                    act.activation(hrT[:, k, :], ps[0:KH, k, :], ACT.Relu, bias=col[0:KH, V_BR1 + k:V_BR1 + k + 1])
                act.drain().then_inc(s_hr, 1)

            def route_exp(m, ne):
                act.wait_ge(s_dl[m], 1)
                act.activation(rt(5, B), rt(4, B), ACT.Exp)
                if m:
                    act.activation(rt(7, B * ne), rt(6, B * ne), ACT.Exp)
                act.drain().then_inc(s_ex[m], 1)

            route_exp(0, E0)
            with act.Fori(0, NB0 // 2) as i:
                for k in range(2):
                    act.wait_ge(s_w2[0][k], i * 16 + 16)
                    act.wait_ge(s_bh[0], i * 2 + k + 1)
                    for f in range(EF0):
                        act.activation(hbT[k][:, f, :], ps[:, 1 + 2 * k + f // 4, (f % 4) * P:(f % 4 + 1) * P], ACT.Relu,
                                       bias=ew_out[k][:, EF0 * D + f:EF0 * D + f + 1])
                    act.drain().then_inc(s_ba[0], 1)

            with act.Fori(0, NCH) as i:
                act.wait_ge(t_qk, i + 1)
                for f in range(6):
                    act.activation(qkT[:, f, :], ps[:, 2 + f, :], ACT.Identity, bias=col[:, V_BQK + f:V_BQK + f + 1])
                act.drain().then_inc(t_qkT, 1)
                for t in range(CT):
                    act.wait_ge(t_sm, i * CT + t + 1)
                    act.activation(sm[t % 2], sm[t % 2], ACT.Exp, scale=HD ** -0.5)
                    act.drain().then_inc(t_p, 1)
                    act.wait_ge(t_pt, i * CT + t + 1)
                    if t >= 2:
                        act.wait_ge(t_o, i * CT + t - 1)
                    for a, bank in ((0, 6), (1, 7), (2, 0)):
                        act.activation(pT[t % 2][:, 4 * a:4 * a + 4, :], ps[:, bank, :].rearrange("p (h q) -> p h q", h=4), ACT.Copy)
                    act.drain().then_inc(t_pT, 1)
                for f in range(SF):
                    act.wait_ge(t_gu, i * SF + f + 1)
                    act.activation(actT1[:, f, :], ps[:, 2 * (f % 3), :], ACT.Silu).then_inc(t_sl, 1)

            route_exp(1, E1)
            with act.Fori(0, NB1 // 2) as i:
                for k in range(2):
                    act.wait_ge(s_bh[1], i * 2 + k + 1)
                    act.activation(hbT[k][:, 0:EF1, :], ps[:, 1 + 2 * k, :].rearrange("p (f t) -> p f t", f=EF1), ACT.Silu)
                    act.drain().then_inc(s_bg[1], 1)

        @block.tensor
        def _(pe):
            def transposes(src, bank):
                for k in range(2):
                    for j in range(CT):
                        last = pe.transpose(ps[0:KH, bank + k, j * P:(j + 1) * P], src[:, j, k * KH:(k + 1) * KH], ident)
                return last

            def accumulate(o, pairs):
                for n, (lhs, rhs) in enumerate(pairs):
                    last = pe.matmul(o, lhs, rhs, start=(n == 0), stop=(n == len(pairs) - 1))
                return last

            def row_slot(bank, j):
                return ps[:, bank + j // 2, (j % 2) * D:(j % 2 + 1) * D]

            pe.wait_ge(s_wa, 15 * 16)
            pe.wait_ge(s_cst, 1)
            pe.sem_inc(s_sumd, 2)
            with pe.Fori(0, NCH) as i:
                pe.wait_ge(s_hn, i + 1)
                transposes(nr, 0).then_inc(s_hnT, 1)
                pe.wait_ge(s_xT, i + 1)
                for g in range(DG):
                    m = slice(g * P, (g + 1) * P)
                    accumulate(ps[:, 5 + g, :], [(wgate[:, k, m], xT[:, k, :]) for k in range(2)]).then_inc(s_gate, 1)
                for g in range(DG):
                    m = slice(g * P, (g + 1) * P)
                    last = accumulate(ps[:, 2 + g, :], [(win[:, k, m], xT[:, k, :]) for k in range(2)])
                last.then_inc(s_z, 1)
                pe.wait_ge(s_zs, i + 1)
                accumulate(ps[0:KH, 0, :], [(wxdt[:, g, :], zT[:, g, :]) for g in range(DG)]).then_inc(s_xd, 1)
                accumulate(ps[0:KH, 1, :], [(wxbc[:, g, :], zT[:, g, :]) for g in range(DG)]).then_inc(s_xbc, 1)
                pe.wait_ge(s_dti, i + 1)
                for g in range(DG):
                    pe.matmul(ps[:, 5 + g, :], wdt[:, g * P:(g + 1) * P], dti, start=True, stop=True).then_inc(s_dt, 1)

                def spread(q, k):
                    n = i * NST + q * 2 + k
                    pe.wait_ge(s_bfree, n + 1)
                    pe.nop(nofuse=True)
                    pe.matmul(ps[:, k, :], sel[:, ds(q * 2 + k, 1)].broadcast_to((KH, P)), bc_p[:, :],
                              start=True, stop=True).then_inc(s_bb, 1)
                    pe.wait_ge(s_cbfree, n + 1)
                    pe.nop(nofuse=True)
                    pe.matmul(ps[:, 5 + k, :], sel[:, ds(q * 2 + k + NST, 1)].broadcast_to((KH, P)), bc_p[:, :],
                              start=True, stop=True).then_inc(s_cb, 1)

                def add_state(q, k, stop=False):
                    pe.wait_ge(s_hc, i * NST + q * 2 + k + 1)
                    for g in range(DG):
                        last = pe.matmul(ps[:, 2 + g, :], ident, hc[k][:, g, :], start=False, stop=stop)
                    last.then_inc(s_sumd, 1)

                pe.wait_ge(s_u, i + 1)
                for g in range(DG):
                    pe.matmul(ps[:, 2 + g, :], diag_d[:, g, :], zT[:, g, :], start=True, stop=False)
                spread(0, 0)
                spread(0, 1)
                with pe.Fori(0, NST // 2 - 1) as q:
                    for k in range(2):
                        spread(q + 1, k)
                        add_state(q, k)
                add_state(NST // 2 - 1, 0)
                add_state(NST // 2 - 1, 1, stop=True)
                pe.drain().then_inc(s_y, 1)

                pe.wait_ge(s_yT, i + 1)
                for j in range(CT):
                    last = accumulate(row_slot(0, j), [(uT[:, g, j * P:(j + 1) * P], wout[:, g, :]) for g in range(DG)])
                last.then_inc(s_op, 1)
                pe.wait_ge(s_hf, i + 1)
                transposes(nr, 2).then_inc(s_hfT, 1)
                pe.wait_ge(s_fT, i + 1)
                for f in range(FF0):
                    m = slice(f * P, (f + 1) * P)
                    accumulate(ps[:, 4 + f, :], [(wgf[:, k, m], xT[:, k, :]) for k in range(2)])
                    accumulate(ps[:, f, :], [(wup[:, k, m], xT[:, k, :]) for k in range(2)]).then_inc(s_gu, 1)
                pe.wait_ge(s_act, i * FF0 + FF0)
                for j in range(CT):
                    last = accumulate(row_slot(4, j), [(actT0[:, f, j * P:(j + 1) * P], wdown[:, f, :]) for f in range(FF0)])
                last.then_inc(s_dn, 1)
                pe.wait_ge(s_xn, i + 1)
                transposes(nr, 6).then_inc(s_xnT, 1)
                pe.wait_ge(s_rT, i + 1)
                for f in range(2):
                    last = accumulate(ps[0:KH, f, :], [(wr1[:, k, f * KH:(f + 1) * KH], xT[:, k, :]) for k in range(2)])
                last.then_inc(s_r1, 1)
                pe.wait_ge(s_hr, i + 1)
                for j in range(CT):
                    last = accumulate(ps[:, 2, j * E0:(j + 1) * E0], [(hrT[:, k, j * P:(j + 1) * P], wr2[:, k, :]) for k in range(2)])
                last.then_inc(s_sc, 1)

            def route_counts(m, ne):
                pe.wait_ge(s_mask[m], 1)
                pe.matmul(ps[:, 0, 0:B * ne], cst[:, C_TRI:C_TRI + P], rt(2, B * ne), start=True, stop=True)
                pe.matmul(ps[:, 1, 0:B * ne], cst[:, C_ONE:C_ONE + P], rt(2, B * ne), start=True, stop=True).then_inc(s_rank[m], 1)

            def expert_blocks(m, nb, fg, gated):
                for k in range(2):
                    pe.sem_inc(s_xbf[m][k], 1)
                    pe.sem_inc(s_w1f[m][k], 1)
                    pe.sem_inc(s_w2f[m][k], 1)
                n_in = fg * P

                def turn(i):
                    for k in range(2):
                        pe.wait_ge(s_xb[m][k], i * 16 + 16)
                        for c in range(2):
                            last = pe.transpose(ps[0:KH, 7 * k, c * P:(c + 1) * P], xb[k][:, c * KH:(c + 1) * KH], ident)
                        last.then_inc(s_bt[m], 1)

                def pair(i, more):
                    for k in range(2):
                        pe.wait_ge(s_bx[m], i * 2 + k + 1)
                        pe.wait_ge(s_w1[m][k], i * 16 + 16)
                        for half in range(2 if gated else 1):
                            for f in range(fg):
                                bank = 1 + 2 * k + (half if gated else f // 4)
                                base = 2 * n_in * half
                                last = accumulate(ps[:, bank, (f % 4) * P:(f % 4 + 1) * P],
                                                  [(ew_in[k][:, base + c * n_in + f * P:base + c * n_in + (f + 1) * P], xbT[k][:, c, :])
                                                   for c in range(2)])
                        last.then_inc(s_bh[m], 1)
                        pe.drain().then_inc(s_w1f[m][k], 1)
                    if more:
                        turn(i + 1)
                    for k in range(2):
                        pe.wait_ge(s_ba[m], i * 2 + k + 1)
                        pe.wait_ge(s_w2[m][k], i * 16 + 16)
                        accumulate(ps[:, 5 + k, 0:D], [(hbT[k][:, f, :], ew_out[k][:, f * D:(f + 1) * D]) for f in range(fg)])\
                            .then_inc(s_by[m], 1)

                turn(0)
                with pe.Fori(0, nb // 2 - 1) as i:
                    pair(i, True)
                pair(nb // 2 - 1, False)

            route_counts(0, E0)
            expert_blocks(0, NB0, EF0, False)

            def attention_chunk(i):
                pe.wait_ge(t_xn, i + 1)
                transposes(nr, 0).then_inc(t_xnT, 1)
                pe.wait_ge(t_xT, i + 1)
                for f in range(6):
                    last = accumulate(ps[:, 2 + f, :], [(wqk[:, k, f * P:(f + 1) * P], xT[:, k, :]) for k in range(2)])
                last.then_inc(t_qk, 1)
                for j in range(CT):
                    last = accumulate(row_slot(0, j), [(xT[:, k, j * P:(j + 1) * P], wv[:, k, :]) for k in range(2)])
                last.then_inc(t_v, 1)
                pe.wait_ge(t_qkT, i + 1)
                pe.wait_ge(t_vr, i + 1)

                def scores(t):
                    if t:
                        pe.wait_ge(t_ms, i * CT + t)
                    m = slice(t * P, (t + 1) * P)
                    for a in range(3):
                        for b in range(4):
                            s = slice(32 * b, 32 * b + 32)
                            last = pe.matmul(ps[:, 2 + b, a * P:(a + 1) * P], qkT[s, a, m], qkT[s, 3 + a, m], start=True, stop=True)
                    last.then_inc(t_s, 1)

                def turn_probs(t):
                    pe.wait_ge(t_p, i * CT + t + 1)
                    if t:
                        pe.wait_ge(t_pT, i * CT + t)
                    for a, bank in ((0, 6), (1, 7), (2, 0)):
                        for b in range(4):
                            last = pe.transpose(ps[:, bank, b * P:(b + 1) * P], sm[t % 2][:, b, a, :], ident)
                    last.then_inc(t_pt, 1)

                def values(t):
                    pe.wait_ge(t_pT, i * CT + t + 1)
                    if t:
                        pe.wait_ge(t_or, i * CT + t)
                    for h in range(H):
                        last = pe.matmul(ps[:, 1, h * (HD + 1):(h + 1) * (HD + 1)], pT[t % 2][:, h, :], vr[:, t, h, :],
                                         start=True, stop=True)
                    last.then_inc(t_o, 1)

                scores(0)
                for t in range(CT + 1):
                    if t + 1 < CT:
                        scores(t + 1)
                    if t < CT:
                        turn_probs(t)
                    if t:
                        values(t - 1)
                pe.wait_ge(t_or, i * CT + CT)
                transposes(nr, 2).then_inc(t_oT, 1)
                pe.wait_ge(t_oTs, i + 1)
                for j in range(CT):
                    last = accumulate(row_slot(4, j), [(xT[:, k, j * P:(j + 1) * P], wproj[:, k, :]) for k in range(2)])
                last.then_inc(t_pr, 1)

            def shared_chunk(i):
                pe.wait_ge(t_fn, i + 1)
                transposes(nr, 6).then_inc(t_fnT, 1)
                pe.wait_ge(t_fT, i + 1)
                for j in range(CT):
                    last = accumulate(ps[:, 6, j * E1:(j + 1) * E1], [(xT[:, k, j * P:(j + 1) * P], wg[:, k, :]) for k in range(2)])
                last.then_inc(t_rs, 1)
                for f in range(SF):
                    m = slice(f * P, (f + 1) * P)
                    if f >= 3:
                        pe.wait_ge(t_act, i * SF + f - 2)
                    accumulate(ps[:, 2 * (f % 3), :], [(ws1[:, k, m], xT[:, k, :]) for k in range(2)])
                    accumulate(ps[:, 2 * (f % 3) + 1, :], [(ws3[:, k, m], xT[:, k, :]) for k in range(2)]).then_inc(t_gu, 1)
                pe.wait_ge(t_act, i * SF + SF)
                for j in range(CT):
                    last = accumulate(row_slot(6, j), [(actT1[:, f, j * P:(j + 1) * P], ws2[:, f, :]) for f in range(SF)])
                last.then_inc(t_dn, 1)

            with pe.Fori(0, NCH) as i:
                attention_chunk(i)
                shared_chunk(i)

            route_counts(1, E1)
            expert_blocks(1, NB1, EF1, True)

        @block.vector
        def _(ve):
            def rstd(eps, rms):
                if rms:
                    ve.tensor_tensor(tt[:, :], mv[:, :, 0], mv[:, :, 0], ALU.mult)
                    ve.drain()
                    ve.scalar_tensor_tensor(out=vv[:, :], in0=tt[:, :], scalar=eps, in1=mv[:, :, 1], op0=ALU.add, op1=ALU.add)
                else:
                    ve.tensor_scalar(vv[:, :], mv[:, :, 1], eps, None, ALU.add)
                ve.drain()
                ve.tensor_scalar(ti[:, :], vv[:, :].bitcast(I32), 1, None, ALU.logical_shift_right)
                ve.tensor_scalar(vh[:, :], vv[:, :], -0.5, None, ALU.mult)
                ve.drain()
                ve.tensor_scalar(yy[:, :].bitcast(I32), ti[:, :], -1.0, float(0x5f3759df), ALU.mult, ALU.add)
                for _ in range(3):
                    ve.drain()
                    ve.tensor_tensor(tt[:, :], yy[:, :], yy[:, :], ALU.mult)
                    ve.drain()
                    ve.tensor_tensor(tt[:, :], tt[:, :], vh[:, :], ALU.mult)
                    ve.drain()
                    ve.scalar_tensor_tensor(out=yy[:, :], in0=tt[:, :], scalar=1.5, in1=yy[:, :], op0=ALU.add, op1=ALU.mult)
                ve.drain()

            def norm(dst, src, eps, rms=False):
                for j in range(CT):
                    ve.bn_stats(st[:, j, :], src[:, j, :])
                ve.drain()
                for j in range(CT):
                    ve.bn_aggr(mv[:, j, :], st[:, j, :])
                ve.drain()
                rstd(eps, rms)
                for j in range(CT):
                    if rms:
                        ve.tensor_scalar(dst[:, j, :], src[:, j, :], yy[:, j:j + 1], None, ALU.mult)
                    else:
                        ve.tensor_scalar(dst[:, j, :], src[:, j, :], mv[:, j, 0:1], yy[:, j:j + 1], ALU.subtract, ALU.mult)

            def rows_of(bank):
                return ps[:, bank:bank + 2, 0:2 * D].rearrange("p b (j d) -> p b j d", j=2)

            def quad(t):
                return t[:, :, :].rearrange("p (b j) d -> p b j d", b=2)

            ve.memset(zero, 0.0).then_inc(s_zz, 1)
            for k in range(2):
                ve.memset(dec[k].rearrange("p g (b t) -> p (g b) t", b=CT)[:, :, 0:1], 0.0)
            ve.wait_ge(s_wa, 15 * 16)
            ve.tensor_copy(sel[:, :], cst[0:KH, C_SEL:C_SEL + 32])
            for g in range(DG):
                ve.tensor_scalar(diag_d[:, g, :], ident, col[:, V_DSK + g:V_DSK + g + 1], None, ALU.mult)
            ve.wait_ge(s_neg, 1)
            ve.tensor_scalar(neg_a[:, :, :], neg_a[:, :, :], -1.0, None, ALU.mult)
            ve.drain().then_inc(s_cst, 1)
            ve.wait_ge(s_zero, 32)
            ve.sem_inc(s_bfree, 2)
            ve.sem_inc(s_decfree, 2)

            with ve.Fori(0, NCH) as i:
                chunk = ds(i * CT, CT)
                ve.wait_ge(s_emb, i * (2 * CT * 16) + 2 * CT * 16)
                ve.tensor_tensor(er[:, :, :], h_rows[:, chunk, :], x_rows[:, chunk, :], ALU.add)
                ve.drain()
                ve.tensor_tensor(er[:, :, :], er[:, :, :], pos_b, ALU.add)
                ve.drain()
                norm(er, er, LN_EPS)
                ve.drain()
                ve.tensor_tensor(er[:, :, :], er[:, :, :], gamma_b, ALU.mult)
                ve.drain()
                ve.tensor_tensor(er[:, :, :], er[:, :, :], beta_b, ALU.add)
                ve.drain()
                norm(mr, er, LN_EPS)
                ve.drain()
                norm(nr, mr, RMS_EPS, rms=True)
                ve.drain().then_inc(s_hn, 1)
                ve.wait_ge(s_hnT, i + 1)
                for k in range(2):
                    ve.tensor_scalar(xT[:, k, :], ps[0:KH, k, :], col[0:KH, V_N1 + k:V_N1 + k + 1], None, ALU.mult)
                ve.drain().then_inc(s_xT, 1)
                ve.wait_ge(s_z, i + 1)
                ve.wait_ge(s_sig, i * DG + DG)
                ve.tensor_tensor(zT, ps[:, 2:5, :], tA, ALU.mult)
                ve.drain().then_inc(s_zs, 1)
                ve.wait_ge(s_xbc, i + 1)
                ve.wait_ge(s_dti, i + 1)
                ve.tensor_copy(bc_p[:, :], ps[0:KH, 1, :])
                ve.drain()
                ve.tensor_tensor(bc_r, ps[0:KH, 1, :], bc_p[:, :], ALU.subtract)
                ve.drain()
                ve.tensor_copy(bc_b, bc_r)
                ve.tensor_copy(bc_p[32:64, :], bc_r[32:64, :])
                ve.drain()
                ve.tensor_tensor(bc_r, bc_r, bc_b, ALU.subtract)
                ve.drain()
                ve.tensor_copy(bc_p[64:96, :], bc_r[64:96, :])
                ve.wait_ge(s_sp, i + 1)
                ve.tensor_tensor(dtT, dtT, tA, ALU.add)
                ve.drain()
                ve.tensor_tensor(uT, dtT, zT, ALU.mult)
                ve.drain().then_inc(s_u, 1)
                with ve.Fori(0, NST // 2) as q:
                    for k in range(2):
                        n = i * NST + q * 2 + k
                        ve.wait_ge(s_bb, n + 1)
                        ve.tensor_tensor(bxs[k], uT, ps[:, k:k + 1, :].broadcast_to((P, DG, CN)), ALU.mult)
                        ve.drain().then_inc(s_bfree, 1)
                        ve.wait_ge(s_dec, n + 1)
                        ve.wait_ge(s_cfree, n + 1)
                        ve.tensor_tensor_scan(hid[k].rearrange("p g t -> p (g t)"), dec[k].rearrange("p g t -> p (g t)"),
                                              bxs[k].rearrange("p g t -> p (g t)"), 0.0, ALU.mult, ALU.add).then_inc(s_scan, 1)
                        ve.drain().then_inc(s_decfree, 1)
                ve.wait_ge(s_op, i + 1)
                ve.tensor_tensor(quad(mr), quad(mr), rows_of(0), ALU.add)
                ve.drain()
                ve.tensor_tensor(er[:, :, :], er[:, :, :], mr[:, :, :], ALU.add)
                norm(nr, mr, RMS_EPS, rms=True)
                ve.drain().then_inc(s_hf, 1)
                ve.wait_ge(s_hfT, i + 1)
                for k in range(2):
                    ve.tensor_scalar(xT[:, k, :], ps[0:KH, 2 + k, :], col[0:KH, V_NF + k:V_NF + k + 1], None, ALU.mult)
                ve.drain().then_inc(s_fT, 1)
                for f in range(FF0):
                    ve.wait_ge(s_sl, i * FF0 + f + 1)
                    ve.tensor_tensor(actT0[:, f, :], actT0[:, f, :], ps[:, f, :], ALU.mult).then_inc(s_act, 1)
                ve.wait_ge(s_dn, i + 1)
                ve.tensor_tensor(quad(er), quad(er), rows_of(4), ALU.add)
                ve.drain()
                ve.tensor_copy(h_rows[:, chunk, :], er[:, :, :])
                norm(nr, er, LN_EPS)
                ve.drain().then_inc(s_xn, 1)
                ve.tensor_copy(x_rows[:, chunk, :], nr[:, :, :])
                ve.wait_ge(s_xnT, i + 1)
                ve.tensor_copy(xT[:, :, :], ps[0:KH, 6:8, :])
                ve.drain().then_inc(s_rT, 1)
                ve.wait_ge(s_sc, i + 1)
                ve.tensor_tensor(sc0[:, chunk, :], ps[:, 2, 0:CT * E0].rearrange("p (j e) -> p j e", e=E0),
                                 row[:, R_BR2:R_BR2 + E0].rearrange("p (a e) -> p a e", a=1).broadcast_to((P, CT, E0)), ALU.add)
                ve.drain().then_inc(s_ch, 1)

            def route(m, ne, nb, sc):
                def te(n):
                    return rt(n, B * ne).rearrange("p (t e) -> p t e", t=B)

                def et(n):
                    return rt(n, B * ne).rearrange("p (e t) -> p e t", e=ne)

                def per_tile(ap):
                    return ap.rearrange("p (t a) -> p t a", a=1).broadcast_to((P, B, ne))

                rev = cst[:, C_REV:C_REV + ne].rearrange("p (a e) -> p a e", a=1).broadcast_to((P, B, ne))
                one, two, both, tmp = te(0), te(1), te(2), te(3)
                m1, m2, km = rt(8, B), rt(9, B), rt(10, B)

                def pick(hot, scores, best):
                    ve.tensor_reduce(best, scores, AXX, ALU.max)
                    ve.drain()
                    ve.tensor_tensor(tmp, scores, per_tile(best), ALU.is_equal)
                    ve.drain()
                    ve.tensor_tensor(tmp, tmp, rev, ALU.mult)
                    ve.drain()
                    ve.tensor_reduce(km, tmp, AXX, ALU.max)
                    ve.drain()
                    ve.tensor_tensor(hot, tmp, per_tile(km), ALU.is_equal)
                    ve.drain()

                pick(one, sc[:, :, :], m1)
                rest = te(11)
                ve.scalar_tensor_tensor(out=rest, in0=one, scalar=NEG, in1=sc[:, :, :], op0=ALU.mult, op1=ALU.add)
                ve.drain()
                pick(two, rest, m2)
                ve.tensor_tensor(both, one, two, ALU.add)
                ve.drain().then_inc(s_mask[m], 1)
                ve.tensor_tensor(rt(4, B), m2, m1, ALU.subtract)
                if m:
                    ve.tensor_tensor(te(6), sc[:, :, :], per_tile(m1), ALU.subtract)
                ve.drain().then_inc(s_dl[m], 1)

                ve.wait_ge(s_rank[m], 1)
                ve.tensor_copy(et(12), ps[:, 1, 0:B * ne].rearrange("p (t e) -> p e t", e=ne))
                ve.drain()
                ve.tensor_tensor_scan(rt(13, B * ne), cst[:, C_RES:C_RES + B * ne], rt(12, B * ne), 0.0, ALU.mult, ALU.add)
                ve.drain()
                total = et(13)[:, :, B - 1:B].broadcast_to((P, ne, B))
                ve.tensor_tensor(et(14), total, cst[:, C_THR:C_THR + B].rearrange("p (a t) -> p a t", a=1)
                                 .broadcast_to((P, ne, B)), ALU.is_gt)
                ve.tensor_tensor(rt(12, B * ne), rt(13, B * ne), rt(12, B * ne), ALU.subtract)
                ve.drain()
                blocks, last, start = rt(15, ne), rt(16, ne), rt(17, ne)
                ve.tensor_reduce(blocks, et(14), AXX, ALU.add)
                ve.drain()
                ve.tensor_tensor_scan(last, cst[:, C_ONE:C_ONE + ne], blocks, 0.0, ALU.mult, ALU.add)
                ve.drain()
                ve.tensor_tensor(start, last, blocks, ALU.subtract)
                ve.drain()
                ve.scalar_tensor_tensor(out=et(12), in0=start.rearrange("p (e a) -> p e a", a=1).broadcast_to((P, ne, B)),
                                        scalar=float(P), in1=et(12), op0=ALU.mult, op1=ALU.add)
                ve.drain()
                where = rt(12, B * ne).rearrange("p (e t) -> p t e", e=ne)
                ve.tensor_tensor(te(14), where, ps[:, 0, 0:B * ne].rearrange("p (t e) -> p t e", e=ne), ALU.add)
                ve.drain()
                for r, hot in ((0, one), (1, two)):
                    ve.tensor_tensor(tmp, te(14), hot, ALU.mult)
                    ve.drain()
                    ve.tensor_reduce(km, tmp, AXX, ALU.add)
                    ve.drain()
                    ve.tensor_copy(pos_i[:, r, :], km)
                    ve.drain()
                past = arena[0:1, 15360:15360 + nb * ne].rearrange("p (b e) -> p b e", e=ne)
                ve.tensor_tensor(past, last[0:1, :].rearrange("p (a e) -> p a e", a=1).broadcast_to((1, nb, ne)),
                                 cst[0:1, C_BLK:C_BLK + nb].rearrange("p (b a) -> p b a", a=1).broadcast_to((1, nb, ne)), ALU.is_le)
                ve.drain()
                num = rt(18, nb)[0:1, :]
                ve.tensor_reduce(num, past, AXX, ALU.add)
                ve.drain()
                ve.tensor_scalar(eid[:, 0:nb], num, float(ne - 1), None, ALU.min)
                ve.drain().then_inc(s_pos[m], 1)

                ve.wait_ge(s_ex[m], 1)
                if m:
                    ve.tensor_reduce(rt(19, B), te(7), AXX, ALU.add)
                else:
                    ve.tensor_scalar(rt(19, B), rt(5, B), 1.0, None, ALU.add)
                ve.drain()
                ve.reciprocal(gate_w[:, 0, :], rt(19, B))
                ve.drain()
                ve.tensor_tensor(gate_w[:, 1, :], gate_w[:, 0, :], rt(5, B), ALU.mult)
                ve.drain()

            def expert_rows_out(m, nb, gated):
                for k in range(2):
                    ve.sem_inc(s_ybf[m][k], 1)

                def turn(i):
                    for k in range(2):
                        ve.wait_ge(s_bt[m], i * 2 + k + 1)
                        ve.tensor_copy(xbT[k], ps[0:KH, 7 * k, 0:2 * P].rearrange("p (c t) -> p c t", c=2))\
                            .then_inc(s_bx[m], 1)
                        ve.drain().then_inc(s_xbf[m][k], 1)

                def pair(i, more):
                    if gated:
                        for k in range(2):
                            ve.wait_ge(s_bg[m], i * 2 + k + 1)
                            ve.tensor_tensor(hbT[k][:, 0:EF1, :], hbT[k][:, 0:EF1, :],
                                             ps[:, 2 + 2 * k, :].rearrange("p (f t) -> p f t", f=EF1), ALU.mult)
                            ve.drain().then_inc(s_ba[m], 1)
                    if more:
                        turn(i + 1)
                    for k in range(2):
                        ve.wait_ge(s_by[m], i * 2 + k + 1)
                        ve.wait_ge(s_ybf[m][k], i + 1)
                        if gated:
                            last = ve.tensor_copy(yb[k], ps[:, 5 + k, 0:D])
                        else:
                            last = ve.tensor_tensor(yb[k], ps[:, 5 + k, 0:D], ew_out[k][:, EF0 * D + EF0:], ALU.add)
                        last.then_inc(s_yb[m], 1)
                        ve.drain().then_inc(s_w2f[m][k], 1)

                turn(0)
                with ve.Fori(0, nb // 2 - 1) as i:
                    pair(i, True)
                pair(nb // 2 - 1, False)

            route(0, E0, NB0, sc0)
            expert_rows_out(0, NB0, False)

            def add_experts(m, dst, src, t0):
                for j in range(CT):
                    ve.scalar_tensor_tensor(out=dst(j), in0=g1[:, ds(t0 + j, 1), :], scalar=gate_w[:, 0, ds(t0 + j, 1)],
                                            in1=src(j), op0=ALU.mult, op1=ALU.add)
                ve.drain()
                for j in range(CT):
                    ve.scalar_tensor_tensor(out=dst(j), in0=g2[:, ds(t0 + j, 1), :], scalar=gate_w[:, 1, ds(t0 + j, 1)],
                                            in1=dst(j), op0=ALU.mult, op1=ALU.add)
                ve.drain()

            causal = cst[:, C_CAUSAL:C_CAUSAL + P].rearrange("p (a b k) -> p a b k", a=1, b=1).broadcast_to((P, 4, 3, P))
            ve.memset(vr[:, :, :, HD:HD + 1], 1.0)

            def joined(i):
                ve.wait_ge(s_g[0], i * (2 * CT * 16) + 2 * CT * 16)
                add_experts(0, lambda j: mr[:, j:j + 1, :], lambda j: h_rows[:, ds(i * CT + j, 1), :], i * CT)

            def attention_chunk(i):
                ve.tensor_tensor(er[:, :, :], mr[:, :, :], bproj_b, ALU.add)
                ve.wait_ge(t_xnT, i + 1)
                ve.tensor_copy(xT[:, :, :], ps[0:KH, 0:2, :])
                ve.drain().then_inc(t_xT, 1)
                ve.wait_ge(t_v, i + 1)
                for b in range(2):
                    ve.tensor_tensor(vr[:, 2 * b:2 * b + 2, :, 0:HD],
                                     ps[:, b, 0:2 * D].rearrange("p (t h d) -> p t h d", t=2, h=H),
                                     row[:, R_BV:R_BV + D].rearrange("p (a h d) -> p a h d", a=1, h=H).broadcast_to((P, 2, H, HD)),
                                     ALU.add)
                ve.drain().then_inc(t_vr, 1)

                def masked(t):
                    ve.wait_ge(t_s, i * CT + t + 1)
                    if t >= 2:
                        ve.wait_ge(t_pt, i * CT + t - 1)
                    ve.tensor_tensor(sm[t % 2], ps[:, 2:6, 0:3 * P].rearrange("p b (a k) -> p b a k", a=3), causal, ALU.add)
                    ve.drain().then_inc(t_ms, 1)
                    ve.tensor_reduce(smax.rearrange("p (b a) -> p b a", b=4), sm[t % 2], AXX, ALU.max)
                    ve.drain()
                    ve.tensor_tensor(sm[t % 2], sm[t % 2], smax.rearrange("p (b a k) -> p b a k", b=4, k=1)
                                     .broadcast_to((P, 4, 3, P)), ALU.subtract)
                    ve.drain().then_inc(t_sm, 1)

                def over_sums(t):
                    ve.wait_ge(t_o, i * CT + t + 1)
                    o = ps[:, 1, 0:H * (HD + 1)].rearrange("p (h d) -> p h d", h=H)
                    ve.reciprocal(rden.rearrange("p (h a) -> p h a", a=1), o[:, :, HD:HD + 1])
                    ve.drain()
                    ve.tensor_tensor(nr[:, t, :].rearrange("p (h d) -> p h d", h=H), o[:, :, 0:HD],
                                     rden.rearrange("p (h a) -> p h a", a=1).broadcast_to((P, H, HD)), ALU.mult)
                    ve.drain().then_inc(t_or, 1)

                for t in range(CT + 2):
                    if t < CT:
                        masked(t)
                    if t >= 2:
                        over_sums(t - 2)
                ve.wait_ge(t_oT, i + 1)
                ve.tensor_copy(xT[:, :, :], ps[0:KH, 2:4, :])
                ve.drain().then_inc(t_oTs, 1)
                ve.wait_ge(t_pr, i + 1)
                ve.tensor_tensor(quad(er), quad(er), rows_of(4), ALU.add)
                ve.drain()
                norm(nr, er, LN_EPS)
                ve.drain().then_inc(t_fn, 1)
                ve.tensor_copy(x_rows[:, ds(i * CT, CT), :], nr[:, :, :])

            def shared_chunk(i, more):
                ve.wait_ge(t_fnT, i + 1)
                ve.tensor_copy(xT[:, :, :], ps[0:KH, 6:8, :])
                ve.drain().then_inc(t_fT, 1)
                ve.wait_ge(t_rs, i + 1)
                ve.tensor_copy(sc1[:, ds(i * CT, CT), :], ps[:, 6, 0:CT * E1].rearrange("p (j e) -> p j e", e=E1))
                for f in range(SF):
                    ve.wait_ge(t_sl, i * SF + f + 1)
                    ve.tensor_tensor(actT1[:, f, :], actT1[:, f, :], ps[:, 2 * (f % 3) + 1, :], ALU.mult)
                    ve.drain().then_inc(t_act, 1)
                    if more and f == 1:
                        joined(i + 1)
                    if more and f == 3:
                        norm(nr, mr, LN_EPS)
                        ve.drain().then_inc(t_xn, 1)
                ve.wait_ge(t_dn, i + 1)
                ve.tensor_tensor(h_rows[:, ds(i * CT, CT), :].rearrange("p (b j) d -> p b j d", b=2), quad(er), rows_of(6), ALU.add)
                ve.drain().then_inc(t_ch, 1)

            joined(0)
            norm(nr, mr, LN_EPS)
            ve.drain().then_inc(t_xn, 1)
            with ve.Fori(0, NCH - 1) as i:
                attention_chunk(i)
                shared_chunk(i, True)
            attention_chunk(NCH - 1)
            shared_chunk(NCH - 1, False)

            route(1, E1, NB1, sc1)
            expert_rows_out(1, NB1, True)
            with ve.Fori(0, NCH) as i:
                ve.wait_ge(s_g[1], i * (2 * CT * 16) + 2 * CT * 16)
                hr = lambda j: h_rows[:, ds(i * CT + j, 1), :]
                add_experts(1, hr, hr, i * CT)
                ve.drain().then_inc(s_fin, 1)


def kernel(**inputs):
    import numpy as np
    import concourse.bacc as bacc
    from concourse import mybir as _mybir
    from concourse.bass_utils import run_bass_kernel_spmd as run

    a = {k: np.asarray(v) for k, v in inputs.items()}

    def halves(w):
        return w.reshape(2, KH, -1).transpose(1, 0, 2)

    def groups(w):
        return w.reshape(-1, P, w.shape[-1]).transpose(1, 0, 2)

    def columns(v, p):
        o = np.zeros((P, v.size // p), v.dtype)
        o[:p] = v.reshape(-1, p).T
        return o

    c = np.zeros((P, C_END), np.float32)
    i = np.arange(P)
    c[:, C_ID:C_ID + P] = i[:, None] == i
    c[:, C_TRI:C_TRI + P] = i[:, None] < i
    c[:, C_ONE:C_ONE + P] = 1
    c[:, C_CAUSAL:C_CAUSAL + P] = np.where(i[:, None] >= i, 0, NEG)
    for r in range(3):
        c[32 * r:32 * r + 32, C_SEL:C_SEL + 32] = np.eye(32)
    c[:, C_REV:C_REV + 16] = 16 - np.arange(16)
    c[:, C_THR:C_THR + B] = P * np.arange(B)
    c[:, C_BLK:C_BLK + NB1] = np.arange(NB1)
    c[:, C_RES:C_RES + 256] = np.arange(256) % B != 0

    rows = np.concatenate([a["L0_tok_gamma"], a["L0_tok_beta"], a["L1_attn_c_attn_b"][2 * D:], a["L1_attn_c_proj_b"],
                           a["L0_ffn_br2"]])[None]

    def strips(w):
        o = np.zeros((w.shape[0], H, 32), w.dtype)
        o[:, :, :HD] = w.reshape(w.shape[0], H, HD)
        return o.reshape(w.shape[0], 3 * P)

    wa, ba = a["L1_attn_c_attn_w"], a["L1_attn_c_attn_b"][None]
    bqk = np.concatenate([strips(ba[:, :D]), strips(ba[:, D:2 * D])], 1)[0]
    cols = np.concatenate([columns(a["L0_attn_w_norm1"], KH), columns(a["L0_attn_w_ffn_norm"], KH),
                           columns(a["L0_ffn_br1"], KH), columns(a["L0_attn_b_dt"], P), columns(a["L0_attn_D_skip"], P),
                           columns(bqk, P), groups(a["L0_attn_A_log"]).reshape(P, -1)], 1)
    wx = a["L0_attn_W_xproj"]
    e0_in = np.stack([halves(w.T).reshape(KH, -1) for w in a["L0_ffn_W1"]])
    e0_out = np.stack([np.concatenate([groups(w2.T).reshape(P, -1), columns(b1, P), np.broadcast_to(b2, (P, D))], 1)
                       for w2, b1, b2 in zip(a["L0_ffn_W2"], a["L0_ffn_b1"], a["L0_ffn_b2"])])
    e1_in = np.stack([np.concatenate([halves(w1.T).reshape(KH, -1), halves(w3.T).reshape(KH, -1)], 1)
                      for w1, w3 in zip(a["L1_ffn_w1"], a["L1_ffn_w3"])])
    e1_out = np.stack([groups(w2.T).reshape(P, -1) for w2 in a["L1_ffn_w2"]])
    named = dict(
        tok=a["x"].T, seg=a["mask_BS_i1_0"].T, tok_tab=a["L0_tok_tok_table"], seg_tab=a["L0_tok_seg_table"],
        pos_tab=a["L0_tok_pos_table"], consts=c, rows=rows, cols=cols,
        w_in=halves(a["L0_attn_W_in"].T), w_gate=halves(a["L0_attn_W_gate"].T),
        w_xdt=groups(wx[:KH].T), w_xbc=groups(np.concatenate([wx[KH:].T] * 3, 1)), w_dt=a["L0_attn_W_dt"].T,
        w_out=groups(a["L0_attn_W_out"].T), w_up=halves(a["L0_attn_W_up"].T), w_gf=halves(a["L0_attn_W_gate_ffn"].T),
        w_down=groups(a["L0_attn_W_down"].T), w_r1=halves(a["L0_ffn_Wr1"].T), w_r2=halves(a["L0_ffn_Wr2"].T),
        w_qk=halves(np.concatenate([strips(wa[:, :D]), strips(wa[:, D:2 * D])], 1)), w_v=halves(wa[:, 2 * D:]),
        w_proj=halves(a["L1_attn_c_proj_w"]), w_g=halves(a["L1_ffn_gate_w"].T),
        w_s1=halves(a["L1_ffn_sw1"].T), w_s3=halves(a["L1_ffn_sw3"].T), w_s2=groups(a["L1_ffn_sw2"].T),
        e0_in=e0_in, e0_out=e0_out, e1_in=e1_in, e1_out=e1_out)
    named = {k: np.ascontiguousarray(v) for k, v in named.items()}

    nc = bacc.Bacc("TRN2", target_bir_lowering=False, num_devices=1)
    args = [nc.dram_tensor("in_" + k, v.shape, _mybir.dt.from_np(v.dtype), kind="ExternalInput").ap() for k, v in named.items()]
    out = nc.dram_tensor("out_0", (B, P, D), F32, kind="ExternalOutput").ap()
    tower(nc, *args, out)
    r = run(nc, [{"in_" + k: v for k, v in named.items()}], core_ids=[0])
    return r.results[0]["out_0"]
```

```python
from contextlib import ExitStack

import concourse.bass as bass
from concourse import mybir

F32 = mybir.dt.float32
I32 = mybir.dt.int32
BF16 = mybir.dt.bfloat16
ACT = mybir.ActivationFunctionType
ALU = mybir.AluOpType
AXX = mybir.AxisListType.X
ds = bass.ds

P = 128
B = 16
D = 192
KH = 96
CT = 4
NCH = B // CT
CN = CT * P
NST = 16
DG = 3
FF0 = 4
E0, E1 = 8, 16
EF0, EF1 = 6, 4
SF = 8
H = 12
HD = D // H
NEG = -3.0e38
LN_EPS, RMS_EPS = 1e-5, 1e-6


def blocks_needed(experts):
    n = 2 * B * P // P + experts - 1
    return n + n % 2


NB0, NB1 = blocks_needed(E0), blocks_needed(E1)

C_ID, C_TRI, C_ONE, C_CAUSAL = 0, 128, 256, 384
C_SEL = 512
C_REV = C_SEL + 32
C_THR = C_REV + 16
C_BLK = C_THR + 16
C_RES = C_BLK + NB1
C_END = C_RES + 256
R_GAM, R_BET, R_BV, R_BP, R_BR2, R_END = 0, D, 2 * D, 3 * D, 4 * D, 4 * D + E0
V_N1, V_NF, V_BR1, V_BDT, V_DSK, V_BQK, V_ALOG, V_END = 0, 2, 4, 6, 9, 12, 18, 18 + DG * NST


def tower(nc, tok, seg, tok_tab, seg_tab, pos_tab, consts, rows, cols, w_in, w_gate, w_xdt, w_xbc, w_dt, w_out,
          w_up, w_gf, w_down, w_r1, w_r2, w_qk, w_v, w_proj, w_g, w_s1, w_s3, w_s2, e0_in, e0_out, e1_in, e1_out,
          out):
    with ExitStack() as ctx:
        def sb(name, shape, dt=F32):
            return ctx.enter_context(nc.sbuf_tensor(name, shape, dt))

        def sem(name):
            return ctx.enter_context(nc.semaphore(name))

        ps = ctx.enter_context(nc.psum_tensor("ps", [P, 8, 512], F32))
        sorted_rows = [nc.dram_tensor(f"sorted{n}", (nb * P, D), F32, kind="Internal").ap() for n, nb in ((0, NB0), (1, NB1))]
        expert_rows = [nc.dram_tensor(f"expert{n}", (nb * P, D), F32, kind="Internal").ap() for n, nb in ((0, NB0), (1, NB1))]

        h_rows = sb("h_rows", [P, B, D])
        x_rows = sb("x_rows", [P, B, D])
        tok_i = sb("tok_i", [P, B], I32)
        seg_i = sb("seg_i", [P, B], I32)
        cst = sb("cst", [P, C_END])
        row = sb("row", [P, R_END])
        col = sb("col", [P, V_END])
        pos = sb("pos", [P, D])
        sel = sb("sel", [KH, 32], BF16)
        wreg = sb("wreg", [P, 7936])

        def carve(shapes):
            out, at = [], 0
            for parts, *dims in shapes:
                n = 1
                for d in dims:
                    n *= d
                ap = wreg[0:parts, at:at + n]
                out.append(ap.rearrange("p (a b) -> p a b", a=dims[0]) if len(dims) == 2 else ap)
                at += n
            return out

        win, wgate, wxdt, wxbc, wdt, wout, wup, wgf, wdown, wr1, diag_d, neg_a = carve([
            (KH, 2, DG * P), (KH, 2, DG * P), (P, DG, KH), (P, DG, KH), (KH, DG * P), (P, DG, D), (KH, 2, FF0 * P),
            (KH, 2, FF0 * P), (P, FF0, D), (KH, 2, D), (P, DG, P), (P, DG, NST)])
        wqk, wv, wproj, ws1, ws3, ws2 = carve([
            (KH, 2, 6 * P), (KH, 2, D), (KH, 2, D), (KH, 2, SF * P), (KH, 2, SF * P), (P, SF, D)])
        wr2 = sb("wr2", [KH, 2, E0])
        wg = sb("wg", [KH, 2, E1])
        ew_in_all = [sb(f"ew_in{k}", [P, 2048]) for k in range(2)]
        ew_in = [w[0:KH, :] for w in ew_in_all]
        ew_out = [sb(f"ew_out{k}", [P, EF0 * D + EF0 + D]) for k in range(2)]

        er = sb("er", [P, CT, D])
        mr = sb("mr", [P, CT, D])
        nr = sb("nr", [P, CT, D])
        xT = sb("xT", [KH, 2, CN])
        nrF = sb("nrF", [P, CT, D])
        xTF = sb("xTF", [KH, 2, CN])
        x_rms = sb("x_rms", [P, B])
        st = sb("st", [P, 2 * CT, 6])
        mv = sb("mv", [P, 2 * CT, 2])
        vv, vh, yy, tt = [sb(n, [P, 2 * CT]) for n in ("vv", "vh", "yy", "tt")]
        ti = sb("ti", [P, 2 * CT], I32)
        arena = sb("arena", [P, 13 * 1536 + FF0 * CN])

        def part(n, words, parts=P):
            return arena[0:parts, n:n + words]

        def wide(n):
            return part(n * 1536, 1536).rearrange("p (g t) -> p g t", g=DG)

        zT, dtT, uT, tA = wide(0), wide(1), wide(2), wide(3)
        dec, bxs, hid, hc = [wide(4), wide(5)], wide(6), [wide(7), wide(8)], [wide(9), wide(10)]
        dtN, yT = wide(11), wide(12)
        actT0 = part(13 * 1536, FF0 * CN).rearrange("p (f t) -> p f t", f=FF0)
        bcs = ew_in_all[0][:, :].rearrange("p (k r t) -> p k r t", k=2, r=2)
        dti = xTF[:, 0, :]
        bc_r = xTF[:, 1, :]
        bc_b = nrF[0:KH, 0:2, :].rearrange("p j d -> p (j d)").bitcast(BF16)[:, 0:CN]
        bc_p = sb("bc_p", [KH, CN], BF16)
        bc_n = sb("bc_n", [KH, CN], BF16)
        g1 = part(0, B * D).rearrange("p (t d) -> p t d", t=B)
        g2 = part(B * D, B * D).rearrange("p (t d) -> p t d", t=B)
        ar = er
        qkT = part(6144, 6 * CN).rearrange("p (f t) -> p f t", f=6)
        vr = part(9216, CT * H * (HD + 1)).rearrange("p (t h d) -> p t h d", t=CT, h=H)
        sm = [part(n, H * P).rearrange("p (b a k) -> p b a k", b=4, a=3) for n in (10240, 13824)]
        pT = [part(n, H * P).rearrange("p (h q) -> p h q", h=H) for n in (11776, 15360)]
        xTS = xTF
        rden = part(13312, H)
        smax = part(13328, H)
        actT1 = part(17920, SF * CN).rearrange("p (f t) -> p f t", f=SF)
        xb = [part(6144 + 256 * k, D) for k in range(2)]
        xbT = [part(6656 + 256 * k, 2 * P, KH).rearrange("p (k t) -> p k t", k=2) for k in range(2)]
        hbT = [part(7168 + 768 * k, EF0 * P).rearrange("p (f t) -> p f t", f=EF0) for k in range(2)]
        yb = [part(8704 + 256 * k, D) for k in range(2)]
        NR = 256

        def rt(n, words=NR):
            return part(9216 + NR * n, words)

        sc1 = sb("sc1", [P, B, E1])
        sc0 = sc1[:, :, 0:E0]
        gate_w = sb("gate_w", [P, 2, B])
        pos_i = sb("pos_i", [P, 2, B], I32)
        eid = sb("eid", [1, NB1], I32)
        zero = ew_in_all[1][:, 0:768]

        ident = cst[:, C_ID:C_ID + P]
        bproj_b = row[:, R_BP:R_BP + D].rearrange("p (a d) -> p a d", a=1).broadcast_to((P, CT, D))

        s_idx, s_sm, s_wa, s_wb, s_zero, s_zz = sem("s_idx"), sem("s_sm"), sem("s_wa"), sem("s_wb"), sem("s_zero"), sem("s_zz")
        s_emb = [sem(f"s_emb{c}") for c in range(NCH)]
        s_cst, s_neg = sem("s_cst"), sem("s_neg")
        s_fsum, s_fn, s_femb = sem("s_fsum"), sem("s_fn"), sem("s_femb")
        s_hn, s_hnT, s_xT = sem("s_hn"), sem("s_hnT"), sem("s_xT")
        s_z, s_gate, s_sig, s_zs = sem("s_z"), sem("s_gate"), sem("s_sig"), sem("s_zs")
        s_xd, s_xbc, s_dti, s_bcp, s_dt, s_spf, s_sp = [sem(n) for n in ("s_xd", "s_xbc", "s_dti", "s_bcp", "s_dt", "s_spf", "s_sp")]
        s_step, s_bch = sem("s_step"), sem("s_bch")
        s_cb, s_bfree, s_cfree = sem("s_cb"), sem("s_bfree"), sem("s_cfree")
        s_decfree, s_cbfree = sem("s_decfree"), sem("s_cbfree")
        s_dec, s_scan, s_cs, s_hc, s_sumd = sem("s_dec"), sem("s_scan"), sem("s_cs"), sem("s_hc"), sem("s_sumd")
        s_y, s_yT, s_op, s_opr = sem("s_y"), sem("s_yT"), sem("s_op"), sem("s_opr")
        s_hf, s_hfT, s_fT = sem("s_hf"), sem("s_hfT"), sem("s_fT")
        s_gu, s_sl, s_act, s_dn = sem("s_gu"), sem("s_sl"), sem("s_act"), sem("s_dn")
        s_xn, s_xnT, s_rT, s_r1, s_hr, s_sc, s_ch = [sem(n) for n in ("s_xn", "s_xnT", "s_rT", "s_r1", "s_hr", "s_sc", "s_ch")]
        s_mask, s_rank, s_dl, s_ex, s_pos = [[sem(f"{n}{m}") for m in range(2)] for n in ("s_mask", "s_rank", "s_dl", "s_ex", "s_pos")]
        s_scat = [sem(f"s_scat{m}") for m in range(2)]
        s_w1 = [[sem(f"s_w1_{m}{k}") for k in range(2)] for m in range(2)]
        s_w2 = [[sem(f"s_w2_{m}{k}") for k in range(2)] for m in range(2)]
        s_xb = [[sem(f"s_xb_{m}{k}") for k in range(2)] for m in range(2)]
        s_w1f = [[sem(f"s_w1f_{m}{k}") for k in range(2)] for m in range(2)]
        s_w2f = [[sem(f"s_w2f_{m}{k}") for k in range(2)] for m in range(2)]
        s_xbf = [[sem(f"s_xbf_{m}{k}") for k in range(2)] for m in range(2)]
        s_bt, s_bx, s_bh, s_ba, s_by, s_yb, s_bg = [[sem(f"{n}{m}") for m in range(2)] for n in ("s_bt", "s_bx", "s_bh", "s_ba", "s_by", "s_yb", "s_bg")]
        s_ybf = [[sem(f"s_ybf_{m}{k}") for k in range(2)] for m in range(2)]
        s_yo = [[sem(f"s_yo_{m}{k}") for k in range(2)] for m in range(2)]
        s_g = [sem(f"s_g{m}") for m in range(2)]
        t_xn, t_xnT, t_xT, t_qk, t_qkT, t_v, t_vr = [sem(n) for n in ("t_xn", "t_xnT", "t_xT", "t_qk", "t_qkT", "t_v", "t_vr")]
        t_s, t_ms, t_sm, t_p, t_pt, t_pT, t_o, t_or = [sem(n) for n in ("t_s", "t_ms", "t_sm", "t_p", "t_pt", "t_pT", "t_o", "t_or")]
        t_oT, t_oTs, t_pr, t_fn, t_fnT, t_fT = [sem(n) for n in ("t_oT", "t_oTs", "t_pr", "t_fn", "t_fnT", "t_fT")]
        t_rs, t_rsr, t_g, t_u, t_sl, t_act, t_dn, t_ch = [sem(n) for n in ("t_rs", "t_rsr", "t_g", "t_u", "t_sl", "t_act", "t_dn", "t_ch")]
        s_fin, s_out = sem("s_fin"), sem("s_out")

        ctx.enter_context(nc.allow_non_contiguous_dma("small vectors"))
        block = ctx.enter_context(nc.Block())

        mixed_banks = [(2, 3), (4, 5), (6, 7), (0, 0), (0, 0), (0, 0), (0, 0), (0, 1)]
        last_banks = [(0, 1), (2, 3), (4, 5)] * 2 + [(0, 1), (2, 3)]
        qk_order = (4, 5, 0, 1, 2, 3)

        @block.sync
        def _(sp):
            sp.dma_start(tok_i[:, :], tok).then_inc(s_idx, 16)
            sp.dma_start(seg_i[:, :], seg).then_inc(s_idx, 16)
            small = [(pos[:, :], pos_tab), (row[:, :], rows.broadcast_to((P, R_END))), (col[:, :], cols), (cst[:, :], consts)]
            first = [(win, w_in), (wgate, w_gate), (wxdt, w_xdt), (wxbc, w_xbc),
                     (wdt, w_dt), (wout, w_out), (wup, w_up), (wgf, w_gf),
                     (wdown, w_down), (wr1, w_r1), (wr2[:, :, :], w_r2), (wg[:, :, :], w_g)]
            later = [(wqk, w_qk), (wv, w_v), (wproj, w_proj),
                     (ws1, w_s1), (ws3, w_s3), (ws2, w_s2)]
            for dst, src in small:
                sp.dma_start(dst, src).then_inc(s_sm, 16)
            for dst, src in first:
                sp.dma_start(dst, src).then_inc(s_wa, 16)
            sp.wait_ge(s_zz, 1)
            sp.wait_ge(s_hn, 1)
            for m, nb in ((0, NB0), (1, NB1)):
                dst = sorted_rows[m].rearrange("(p n c) d -> p n (c d)", p=P, c=4)
                sp.dma_start(dst, zero.rearrange("p (a c) -> p a c", a=1).broadcast_to((P, nb // 4, 768)))\
                  .then_inc(s_zero, 16)

            def expert_loads(m, nb, t_in, t_out, n_in, n_out):
                sp.wait_ge(s_pos[m], 1)
                sp.wait_ge(s_scat[m], 32 * 16)
                with sp.Fori(0, nb // 2) as i:
                    for k in range(2):
                        sp.wait_ge(s_xbf[m][k], i + 1)
                        sp.nop(nofuse=True)
                        sp.dma_start(xb[k], sorted_rows[m][ds((i * 2 + k) * P, P), :]).then_inc(s_xb[m][k], 16)
                    e = [sp.value_load(eid[0:1, ds(i * 2 + k, 1)], min_val=0, max_val=t_in.shape[0] - 1) for k in range(2)]
                    for k in range(2):
                        sp.wait_ge(s_w1f[m][k], i + 1)
                        sp.nop(nofuse=True)
                        sp.dma_start(ew_in[k][:, 0:n_in], t_in[ds(e[k], 1), :, :].rearrange("a p n -> (a p) n"))\
                          .then_inc(s_w1[m][k], 16)
                    for k in range(2):
                        sp.wait_ge(s_w2f[m][k], i + 1)
                        sp.nop(nofuse=True)
                        sp.dma_start(ew_out[k][:, 0:n_out], t_out[ds(e[k], 1), :, :].rearrange("a p n -> (a p) n"))\
                          .then_inc(s_w2[m][k], 16)

            sp.wait_ge(s_ch, NCH)
            for dst, src in later:
                sp.dma_start(dst, src).then_inc(s_wb, 16)
            expert_loads(0, NB0, e0_in, e0_out, 2 * EF0 * P, EF0 * D + EF0 + D)
            expert_loads(1, NB1, e1_in, e1_out, 4 * EF1 * P, EF1 * D)
            for c in range(NCH):
                sp.wait_ge(s_fin, c + 1)
                sp.dma_start(out[c * CT:(c + 1) * CT].rearrange("t p d -> p t d"), h_rows[:, c * CT:(c + 1) * CT, :])\
                  .then_inc(s_out, 16)
            sp.wait_ge(s_out, NCH * 16)

        @block.gpsimd
        def _(pool):
            pool.wait_ge(s_idx, 32)
            def embed(c):
                for t in range(c * CT, (c + 1) * CT):
                    pool.indirect_dma_start(h_rows[:, t, :], None, tok_tab, bass.IndirectOffsetOnAxis(tok_i[:, t:t + 1], 0))\
                        .then_inc(s_emb[c], 16)
                    pool.indirect_dma_start(x_rows[:, t, :], None, seg_tab, bass.IndirectOffsetOnAxis(seg_i[:, t:t + 1], 0))\
                        .then_inc(s_emb[c], 16)

            def spread_row(ap, n):
                return ap.rearrange("p (a d) -> p a d", a=1).broadcast_to((P, n * CT, D))

            def embed_sum(c, n):
                for m in range(c, c + n):
                    pool.wait_ge(s_emb[m], 2 * CT * 16)
                h = h_rows[:, c * CT:(c + n) * CT, :]
                pool.tensor_tensor(h, h, x_rows[:, c * CT:(c + n) * CT, :], ALU.add)
                pool.drain()
                pool.tensor_tensor(h, h, spread_row(pos[:, :], n), ALU.add)
                pool.drain().then_inc(s_fsum, n)

            def embed_affine(c, n):
                pool.wait_ge(s_fn, c + n)
                h = h_rows[:, c * CT:(c + n) * CT, :]
                pool.tensor_tensor(h, h, spread_row(row[:, R_GAM:R_GAM + D], n), ALU.mult)
                pool.drain()
                pool.tensor_tensor(h, h, spread_row(row[:, R_BET:R_BET + D], n), ALU.add)
                pool.drain().then_inc(s_femb, n)

            def scan_chunk(i, first):
                for s in range(NST):
                    k, n = s % 2, i * NST + s
                    pool.wait_ge(s_scan, n + 1)
                    pool.wait_ge(s_cs, n + 1)
                    pool.wait_ge(s_sumd, n + 1)
                    pool.tensor_tensor(hc[k], hid[k], bcs[:, k, 1:2, :].broadcast_to((P, DG, CN)), ALU.mult)\
                        .then_inc(s_hc, 1)
                    pool.drain().then_inc(s_cfree, 1)
                    if first and s == 6:
                        embed_sum(2, 2)
                    if first and s == 8:
                        embed_affine(2, 2)

            embed(0)
            pool.wait_ge(s_sm, 4 * 16)
            embed_sum(0, 1)
            embed(1)
            embed_affine(0, 1)
            embed(2)
            embed_sum(1, 1)
            embed(3)
            embed_affine(1, 1)
            pool.sem_inc(s_cfree, 2)
            scan_chunk(0, True)
            with pool.Fori(1, NCH) as i:
                scan_chunk(i, False)

            def scatter(m):
                pool.wait_ge(s_zero, 32)
                pool.wait_ge(s_pos[m], 1)
                for t in range(B):
                    for r in range(2):
                        pool.indirect_dma_start(sorted_rows[m], bass.IndirectOffsetOnAxis(pos_i[:, r, t:t + 1], 0),
                                                x_rows[:, t, :], None).then_inc(s_scat[m], 16)

            def store_blocks(m, nb):
                with pool.Fori(0, nb // 2) as i:
                    for k in range(2):
                        pool.wait_ge(s_yb[m], i * 2 + k + 1)
                        pool.nop(nofuse=True)
                        pool.dma_start(expert_rows[m][ds((i * 2 + k) * P, P), :], yb[k]).then_inc(s_yo[m][k], 16)
                        pool.wait_ge(s_yo[m][k], i * 16 + 16)
                        pool.nop(nofuse=True)
                        pool.drain().then_inc(s_ybf[m][k], 1)

            def gather(m, nb):
                for k in range(2):
                    pool.wait_ge(s_yo[m][k], 16 * (nb // 2))
                for c in range(NCH):
                    for t in range(c * CT, (c + 1) * CT):
                        for r, g in ((0, g1), (1, g2)):
                            pool.indirect_dma_start(g[:, t, :], None, expert_rows[m],
                                                    bass.IndirectOffsetOnAxis(pos_i[:, r, t:t + 1], 0)).then_inc(s_g[m], 16)
                    pool.wait_ge(s_g[m], (c + 1) * 2 * CT * 16)

            for m, nb in ((0, NB0), (1, NB1)):
                scatter(m)
                store_blocks(m, nb)
                gather(m, nb)

        @block.scalar
        def _(act):
            act.wait_ge(s_sm, 4 * 16)
            act.activation(neg_a, col[:, V_ALOG:V_END].rearrange("p (g s) -> p g s", g=DG), ACT.Exp).then_inc(s_neg, 1)

            def enter_gates(c, gs):
                for g in gs:
                    act.wait_ge(s_gate, c * DG + g + 1)
                    act.activation(tA[:, g, :], ps[:, (5, 7, 6)[g], :], ACT.Sigmoid).then_inc(s_sig, 1)

            def enter_low(c):
                act.wait_ge(s_xd, c + 1)
                act.activation(dti, ps[0:KH, 5, :], ACT.Copy).then_inc(s_dti, 1)

            def enter_parts(c):
                for g in range(DG):
                    act.wait_ge(s_dt, c * DG + g + 1)
                    bdt = col[:, V_BDT + g:V_BDT + g + 1]
                    act.activation(tA[:, g, :], ps[:, 5 + g, :], ACT.Abs, bias=bdt)
                    act.activation(dtN[:, g, :], ps[:, 5 + g, :], ACT.Relu, bias=bdt)
                act.drain().then_inc(s_spf, 1)

            def enter_exp():
                act.activation(tA, tA, ACT.Exp, scale=-1.0)
                act.drain()

            def enter_ln():
                act.activation(tA, tA, ACT.Ln, bias=1.0)
                act.drain().then_inc(s_sp, 1)

            def take_steps(c):
                act.wait_ge(s_step, c + 1)
                act.activation(dtT, dtN, ACT.Copy)
                act.drain()

            def leave_silu(c, fs):
                for f in fs:
                    act.wait_ge(s_gu, c * FF0 + f + 1)
                    act.activation(actT0[:, f, :], ps[:, (5, 7, 6, 5)[f], :], ACT.Silu).then_inc(s_sl, 1)

            def leave_router(c):
                act.wait_ge(s_r1, c + 1)
                for k in range(2):
                    act.activation(xT[:, k, :], ps[0:KH, 5 + k, :], ACT.Relu, bias=col[0:KH, V_BR1 + k:V_BR1 + k + 1])
                act.drain().then_inc(s_hr, 1)

            def scan_chunk(i, first, last):
                def keep_rows(s):
                    n = i * NST + s
                    act.wait_ge(s_cb, n + 1)
                    act.wait_ge(s_bfree, n + 1)
                    act.wait_ge(s_cfree, n + 1)
                    act.activation(bcs[:, s % 2, :, :], ps[:, 0:2, :], ACT.Copy).then_inc(s_cs, 1)
                    act.drain().then_inc(s_cbfree, 1)

                if first:
                    keep_rows(0)
                for s in range(NST):
                    k, n = s % 2, i * NST + s
                    act.wait_ge(s_decfree, n + 1)
                    for g in range(DG):
                        o = dec[k][:, g, :].rearrange("p (b t) -> p b t", b=CT)
                        t = dtT[:, g, :].rearrange("p (b t) -> p b t", b=CT)
                        act.activation(o[:, :, 1:P], t[:, :, 1:P], ACT.Exp, scale=neg_a[:, g, s:s + 1])
                    act.drain().then_inc(s_dec, 1)
                    if s + 1 < NST or not last:
                        keep_rows(s + 1)
                    if not first:
                        if s == 0:
                            take_y(i - 1)
                    if not last:
                        if s in (5, 6, 7):
                            enter_gates(i + 1, (s - 5,))
                        if s == 8:
                            enter_low(i + 1)
                        if s == 9:
                            enter_parts(i + 1)
                        if s == 12:
                            enter_exp()
                            enter_ln()
                        if s == 15:
                            take_steps(i + 1)
                    if not first:
                        if s in (10, 11):
                            leave_silu(i - 1, ((0,), (1, 2, 3))[s - 10])
                        if s == 14:
                            leave_router(i - 1)

            def take_y(c):
                act.wait_ge(s_y, c + 1)
                act.activation(yT, ps[:, 2:5, :], ACT.Copy).then_inc(s_yT, 1)

            act.sem_inc(s_cbfree, 1)
            enter_gates(0, (0, 1, 2))
            enter_low(0)
            enter_parts(0)
            enter_exp()
            enter_ln()
            take_steps(0)
            scan_chunk(0, True, False)
            with act.Fori(1, NCH - 1) as i:
                scan_chunk(i, False, False)
            scan_chunk(NCH - 1, False, True)
            take_y(NCH - 1)
            leave_silu(NCH - 1, range(FF0))
            leave_router(NCH - 1)

            def route_exp(m, ne):
                act.wait_ge(s_dl[m], 1)
                act.activation(rt(5, B), rt(4, B), ACT.Exp)
                if m:
                    act.activation(rt(7, B * ne), rt(6, B * ne), ACT.Exp)
                act.drain().then_inc(s_ex[m], 1)

            route_exp(0, E0)
            with act.Fori(0, NB0 // 2) as i:
                for k in range(2):
                    act.wait_ge(s_w2[0][k], i * 16 + 16)
                    act.wait_ge(s_bh[0], i * 2 + k + 1)
                    for f in range(EF0):
                        act.activation(hbT[k][:, f, :], ps[:, 1 + 2 * k + f // 4, (f % 4) * P:(f % 4 + 1) * P], ACT.Relu,
                                       bias=ew_out[k][:, EF0 * D + f:EF0 * D + f + 1])
                    act.drain().then_inc(s_ba[0], 1)

            def shared_silu(i, f, banks):
                act.wait_ge(t_g, i * SF + f + 1)
                act.activation(actT1[:, f, :], ps[:, banks[f][0], :], ACT.Silu).then_inc(t_sl, 1)

            def attention_chunk(i, first):
                if not first:
                    shared_silu(i - 1, 0, mixed_banks)
                    shared_silu(i - 1, 1, mixed_banks)
                for n, f in enumerate(qk_order):
                    act.wait_ge(t_qk, i * 6 + n + 1)
                    act.activation(qkT[:, f, :], ps[:, 2 + f, :], ACT.Identity, bias=col[:, V_BQK + f:V_BQK + f + 1])\
                        .then_inc(t_qkT, 1)
                if not first:
                    shared_silu(i - 1, 2, mixed_banks)
                for t in range(CT):
                    act.wait_ge(t_sm, i * CT + t + 1)
                    act.activation(sm[t % 2], sm[t % 2], ACT.Exp, scale=HD ** -0.5)
                    act.drain().then_inc(t_p, 1)
                    if not first:
                        shared_silu(i - 1, 3 + t, mixed_banks)
                    if t >= 2:
                        act.wait_ge(t_o, i * CT + t - 1)
                    for a, bank in ((0, 6), (1, 7), (2, 6)):
                        act.wait_ge(t_pt, (i * CT + t) * 3 + a + 1)
                        act.activation(pT[t % 2][:, 4 * a:4 * a + 4, :], ps[:, bank, :].rearrange("p (h q) -> p h q", h=4), ACT.Copy)\
                            .then_inc(t_pT, 1)
                if not first:
                    shared_silu(i - 1, 7, mixed_banks)

            attention_chunk(0, True)
            with act.Fori(1, NCH) as i:
                attention_chunk(i, False)
            for f in range(3):
                shared_silu(NCH - 1, f, last_banks)
            route_exp(1, E1)
            for f in range(3, SF):
                shared_silu(NCH - 1, f, last_banks)
            with act.Fori(0, NB1 // 2) as i:
                for k in range(2):
                    act.wait_ge(s_bh[1], i * 2 + k + 1)
                    act.activation(hbT[k][:, 0:EF1, :], ps[:, 1 + 2 * k, :].rearrange("p (f t) -> p f t", f=EF1), ACT.Silu)
                    act.drain().then_inc(s_bg[1], 1)

        @block.tensor
        def _(pe):
            def transposes(src, bank):
                for k in range(2):
                    for j in range(CT):
                        last = pe.transpose(ps[0:KH, bank + k, j * P:(j + 1) * P], src[:, j, k * KH:(k + 1) * KH], ident)
                return last

            def accumulate(o, pairs):
                for n, (lhs, rhs) in enumerate(pairs):
                    last = pe.matmul(o, lhs, rhs, start=(n == 0), stop=(n == len(pairs) - 1))
                return last

            def row_slot(bank, j):
                return ps[:, bank + j // 2, (j % 2) * D:(j % 2 + 1) * D]

            pe.wait_ge(s_sm, 4 * 16)

            def enter_turn(c):
                pe.wait_ge(s_hn, c + 1)
                transposes(nrF, 5).then_inc(s_hnT, 1)

            def enter_in(c, g, after=None):
                m = slice(g * P, (g + 1) * P)
                if g == 0:
                    pe.wait_ge(s_xT, c + 1)
                    if after is not None:
                        pe.wait_ge(s_fT, after)
                if g == 2:
                    pe.wait_ge(s_zs, c * DG + 1)
                accumulate(ps[:, (5, 7, 6)[g], :], [(wgate[:, k, m], xTF[:, k, :]) for k in range(2)]).then_inc(s_gate, 1)
                if g:
                    pe.wait_ge(s_sig, c * DG + g)
                accumulate(ps[:, (6, 5, 7)[g], :], [(win[:, k, m], xTF[:, k, :]) for k in range(2)]).then_inc(s_z, 1)

            def enter_low(c):
                pe.wait_ge(s_zs, c * DG + DG)
                accumulate(ps[0:KH, 5, :], [(wxdt[:, g, :], zT[:, g, :]) for g in range(DG)]).then_inc(s_xd, 1)
                accumulate(ps[0:KH, 6, :], [(wxbc[:, g, :], zT[:, g, :]) for g in range(DG)]).then_inc(s_xbc, 1)

            def enter_steps(c):
                pe.wait_ge(s_dti, c + 1)
                pe.wait_ge(s_bcp, c + 1)
                for g in range(DG):
                    pe.matmul(ps[:, 5 + g, :], wdt[:, g * P:(g + 1) * P], dti, start=True, stop=True).then_inc(s_dt, 1)

            def leave_out(c):
                pe.wait_ge(s_yT, c + 1)
                for j in range(CT):
                    last = accumulate(row_slot(5, j), [(yT[:, g, j * P:(j + 1) * P], wout[:, g, :]) for g in range(DG)])
                last.then_inc(s_op, 1)

            def leave_turn(c):
                pe.wait_ge(s_hf, c + 1)
                transposes(nr, 5).then_inc(s_hfT, 1)

            def leave_mlp(c, f):
                m = slice(f * P, (f + 1) * P)
                if f == 0:
                    pe.wait_ge(s_fT, c + 1)
                if f >= 2:
                    pe.wait_ge(s_act, c * FF0 + f - 1)
                accumulate(ps[:, (5, 7, 6, 5)[f], :], [(wgf[:, k, m], xT[:, k, :]) for k in range(2)])
                if f:
                    pe.wait_ge(s_sl, c * FF0 + f)
                accumulate(ps[:, (6, 5, 7, 6)[f], :], [(wup[:, k, m], xT[:, k, :]) for k in range(2)]).then_inc(s_gu, 1)

            def leave_down(c):
                pe.wait_ge(s_act, c * FF0 + FF0)
                for j in range(CT):
                    o = ps[:, (7, 5)[j // 2], (j % 2) * D:(j % 2 + 1) * D]
                    last = accumulate(o, [(actT0[:, f, j * P:(j + 1) * P], wdown[:, f, :]) for f in range(FF0)])
                last.then_inc(s_dn, 1)

            def leave_turn_again(c):
                pe.wait_ge(s_xn, c + 1)
                transposes(nr, 6).then_inc(s_xnT, 1)

            def leave_router(c):
                pe.wait_ge(s_rT, c + 1)
                for f in range(2):
                    last = accumulate(ps[0:KH, 5 + f, :], [(wr1[:, k, f * KH:(f + 1) * KH], xT[:, k, :]) for k in range(2)])
                last.then_inc(s_r1, 1)

            def leave_scores(c):
                pe.wait_ge(s_hr, c + 1)
                for j in range(CT):
                    last = accumulate(ps[:, 7, j * E0:(j + 1) * E0], [(xT[:, k, j * P:(j + 1) * P], wr2[:, k, :]) for k in range(2)])
                last.then_inc(s_sc, 1)

            def spread(n, s):
                pe.wait_ge(s_cbfree, n + 1)
                pe.nop(nofuse=True)
                pe.matmul(ps[:, 0, :], sel[:, s:s + 1].broadcast_to((KH, P)), bc_p[:, :], start=True, stop=True)
                pe.matmul(ps[:, 1, :], sel[:, NST + s:NST + s + 1].broadcast_to((KH, P)), bc_p[:, :],
                          start=True, stop=True).then_inc(s_cb, 1)

            def scan_chunk(i, first, last):
                if not first:
                    pe.wait_ge(s_yT, i)
                for g in range(DG):
                    pe.matmul(ps[:, 2 + g, :], diag_d[:, g, :], zT[:, g, :], start=True, stop=False)
                for s in range(NST):
                    if s + 2 < NST or not last:
                        if s + 2 == NST:
                            pe.wait_ge(s_bch, i + 2)
                        spread(i * NST + s + 2, (s + 2) % NST)
                    if not first and s == 0:
                        leave_out(i - 1)
                    if not last:
                        if s == 1:
                            if not first:
                                pe.wait_ge(s_opr, i)
                            enter_turn(i + 1)
                    if not first and s == 2:
                        if not last:
                            pe.wait_ge(s_xT, i + 2)
                        leave_turn(i - 1)
                    if not last:
                        if s == 3:
                            enter_in(i + 1, 0, None if first else i)
                        if s in (5, 6):
                            enter_in(i + 1, s - 4)
                        if s == 7:
                            enter_low(i + 1)
                        if s == 8:
                            enter_steps(i + 1)
                    if not first:
                        if s == 9:
                            if not last:
                                pe.wait_ge(s_spf, i + 2)
                            leave_mlp(i - 1, 0)
                        if s == 10:
                            leave_mlp(i - 1, 1)
                        if s == 11:
                            leave_mlp(i - 1, 2)
                            leave_mlp(i - 1, 3)
                            leave_down(i - 1)
                        if s == 13:
                            leave_turn_again(i - 1)
                            leave_router(i - 1)
                        if s == 14:
                            leave_scores(i - 1)
                    pe.wait_ge(s_hc, i * NST + s + 1)
                    for g in range(DG):
                        add = pe.matmul(ps[:, 2 + g, :], ident, hc[s % 2][:, g, :], start=False, stop=(s == NST - 1))
                    add.then_inc(s_sumd, 1)
                pe.drain().then_inc(s_y, 1)

            pe.sem_inc(s_sumd, 2)
            enter_turn(0)
            pe.wait_ge(s_wa, 12 * 16)
            for g in range(DG):
                enter_in(0, g)
            enter_low(0)
            enter_steps(0)
            pe.wait_ge(s_cst, 1)
            pe.wait_ge(s_bch, 1)
            spread(0, 0)
            spread(1, 1)
            scan_chunk(0, True, False)
            with pe.Fori(1, NCH - 1) as i:
                scan_chunk(i, False, False)
            scan_chunk(NCH - 1, False, True)
            leave_out(NCH - 1)
            leave_turn(NCH - 1)
            for f in range(FF0):
                leave_mlp(NCH - 1, f)
            leave_down(NCH - 1)
            leave_turn_again(NCH - 1)
            leave_router(NCH - 1)
            leave_scores(NCH - 1)

            def route_counts(m, ne):
                pe.wait_ge(s_mask[m], 1)
                pe.matmul(ps[:, 6, 0:B * ne], cst[:, C_TRI:C_TRI + P], rt(2, B * ne), start=True, stop=True)
                pe.matmul(ps[:, 7, 0:B * ne], cst[:, C_ONE:C_ONE + P], rt(2, B * ne), start=True, stop=True).then_inc(s_rank[m], 1)

            def expert_blocks(m, nb, fg, gated):
                for k in range(2):
                    pe.sem_inc(s_xbf[m][k], 1)
                    pe.sem_inc(s_w1f[m][k], 1)
                    pe.sem_inc(s_w2f[m][k], 1)
                n_in = fg * P

                def turn(i):
                    for k in range(2):
                        pe.wait_ge(s_xb[m][k], i * 16 + 16)
                        for c in range(2):
                            last = pe.transpose(ps[0:KH, 7 * k, c * P:(c + 1) * P], xb[k][:, c * KH:(c + 1) * KH], ident)
                        last.then_inc(s_bt[m], 1)

                def pair(i, more):
                    for k in range(2):
                        pe.wait_ge(s_bx[m], i * 2 + k + 1)
                        pe.wait_ge(s_w1[m][k], i * 16 + 16)
                        for half in range(2 if gated else 1):
                            for f in range(fg):
                                bank = 1 + 2 * k + (half if gated else f // 4)
                                base = 2 * n_in * half
                                last = accumulate(ps[:, bank, (f % 4) * P:(f % 4 + 1) * P],
                                                  [(ew_in[k][:, base + c * n_in + f * P:base + c * n_in + (f + 1) * P], xbT[k][:, c, :])
                                                   for c in range(2)])
                        last.then_inc(s_bh[m], 1)
                        pe.drain().then_inc(s_w1f[m][k], 1)
                    if more:
                        turn(i + 1)
                    for k in range(2):
                        pe.wait_ge(s_ba[m], i * 2 + k + 1)
                        pe.wait_ge(s_w2[m][k], i * 16 + 16)
                        accumulate(ps[:, 5 + k, 0:D], [(hbT[k][:, f, :], ew_out[k][:, f * D:(f + 1) * D]) for f in range(fg)])\
                            .then_inc(s_by[m], 1)

                turn(0)
                with pe.Fori(0, nb // 2 - 1) as i:
                    pair(i, True)
                pair(nb // 2 - 1, False)

            route_counts(0, E0)
            expert_blocks(0, NB0, EF0, False)

            def shared_gate(i, f, banks):
                m = slice(f * P, (f + 1) * P)
                accumulate(ps[:, banks[f][0], :], [(ws1[:, k, m], xTS[:, k, :]) for k in range(2)]).then_inc(t_g, 1)

            def shared_up(i, f, banks):
                m = slice(f * P, (f + 1) * P)
                if banks[f][0] == banks[f][1]:
                    pe.wait_ge(t_sl, i * SF + f + 1)
                accumulate(ps[:, banks[f][1], :], [(ws3[:, k, m], xTS[:, k, :]) for k in range(2)]).then_inc(t_u, 1)

            def shared_down(i, bank):
                pe.wait_ge(t_act, i * SF + SF)
                for j in range(CT):
                    last = accumulate(row_slot(bank, j), [(actT1[:, f, j * P:(j + 1) * P], ws2[:, f, :]) for f in range(SF)])
                last.then_inc(t_dn, 1)

            def attention_chunk(i, first):
                if not first:
                    pe.wait_ge(t_fT, i)
                    for f in range(2):
                        shared_gate(i - 1, f, mixed_banks)
                        shared_up(i - 1, f, mixed_banks)
                pe.wait_ge(t_xn, i + 1)
                transposes(ar, 0).then_inc(t_xnT, 1)
                pe.wait_ge(t_xT, i + 1)
                for n, f in enumerate(qk_order):
                    if not first and n == 0:
                        pe.wait_ge(t_rsr, i)
                    if not first and n in (2, 4):
                        pe.wait_ge(t_act, (i - 1) * SF + n // 2)
                    accumulate(ps[:, 2 + f, :], [(wqk[:, k, f * P:(f + 1) * P], xT[:, k, :]) for k in range(2)])\
                        .then_inc(t_qk, 1)
                for j in range(CT):
                    last = accumulate(row_slot(0, j), [(xT[:, k, j * P:(j + 1) * P], wv[:, k, :]) for k in range(2)])
                last.then_inc(t_v, 1)
                if not first:
                    pe.wait_ge(t_qkT, i * 6 + 2)
                    shared_gate(i - 1, 2, mixed_banks)
                    shared_up(i - 1, 2, mixed_banks)
                pe.wait_ge(t_qkT, i * 6 + 6)

                def scores(t):
                    if t:
                        pe.wait_ge(t_ms, i * CT + t)
                    m = slice(t * P, (t + 1) * P)
                    for a in range(3):
                        for b in range(4):
                            s = slice(32 * b, 32 * b + 32)
                            last = pe.matmul(ps[:, 2 + b, a * P:(a + 1) * P], qkT[s, a, m], qkT[s, 3 + a, m], start=True, stop=True)
                    last.then_inc(t_s, 1)

                def turn_probs(t, groups):
                    for a in groups:
                        if a == 2:
                            pe.wait_ge(t_pT, (i * CT + t) * 3 + 1)
                        for b in range(4):
                            last = pe.transpose(ps[:, (6, 7, 6)[a], b * P:(b + 1) * P], sm[t % 2][:, b, a, :], ident)
                        last.then_inc(t_pt, 1)

                def values(t):
                    pe.wait_ge(t_pT, (i * CT + t) * 3 + 3)
                    if t:
                        pe.wait_ge(t_or, i * CT + t)
                    for h in range(H):
                        last = pe.matmul(ps[:, 1, h * (HD + 1):(h + 1) * (HD + 1)], pT[t % 2][:, h, :], vr[:, t, h, :],
                                         start=True, stop=True)
                    last.then_inc(t_o, 1)

                scores(0)
                pe.wait_ge(t_vr, i + 1)
                for t in range(CT + 1):
                    if t + 1 < CT:
                        scores(t + 1)
                    if t < CT:
                        if not first:
                            pe.wait_ge(t_act, (i - 1) * SF + 3 + t)
                            shared_gate(i - 1, 3 + t, mixed_banks)
                        pe.wait_ge(t_p, i * CT + t + 1)
                        if t:
                            pe.wait_ge(t_pT, (i * CT + t) * 3)
                        turn_probs(t, (0, 1))
                        if not first:
                            shared_up(i - 1, 3 + t, mixed_banks)
                        turn_probs(t, (2,))
                    if t:
                        values(t - 1)
                pe.wait_ge(t_or, i * CT + CT)
                transposes(nr, 2).then_inc(t_oT, 1)
                if not first:
                    pe.wait_ge(t_act, (i - 1) * SF + 7)
                    shared_gate(i - 1, 7, mixed_banks)
                    shared_up(i - 1, 7, mixed_banks)
                pe.wait_ge(t_oTs, i + 1)
                for j in range(CT):
                    last = accumulate(row_slot(4, j), [(xT[:, k, j * P:(j + 1) * P], wproj[:, k, :]) for k in range(2)])
                last.then_inc(t_pr, 1)
                if not first:
                    shared_down(i - 1, 2)
                pe.wait_ge(t_fn, i + 1)
                transposes(nr, 6).then_inc(t_fnT, 1)
                pe.wait_ge(t_fT, i + 1)
                for j in range(CT):
                    last = accumulate(ps[:, 6, j * E1:(j + 1) * E1], [(xTS[:, k, j * P:(j + 1) * P], wg[:, k, :]) for k in range(2)])
                last.then_inc(t_rs, 1)
                if not first:
                    pe.wait_ge(t_ch, i)

            pe.wait_ge(s_wb, 6 * 16)
            attention_chunk(0, True)
            with pe.Fori(1, NCH) as i:
                attention_chunk(i, False)

            c = NCH - 1
            for f in range(3):
                shared_gate(c, f, last_banks)
                shared_up(c, f, last_banks)
            pe.wait_ge(t_rsr, NCH)
            route_counts(1, E1)
            for f in range(3, SF):
                pe.wait_ge(t_act, c * SF + f - 2)
                shared_gate(c, f, last_banks)
                shared_up(c, f, last_banks)
            pe.wait_ge(s_pos[1], 1)
            shared_down(c, 6)
            pe.wait_ge(t_ch, NCH)
            expert_blocks(1, NB1, EF1, True)

        @block.vector
        def _(ve):
            def rstd(out, n, eps, rms):
                v, h, y, t = vv[:, 0:n], vh[:, 0:n], yy[:, 0:n], tt[:, 0:n]
                if rms:
                    ve.tensor_tensor(t, mv[:, 0:n, 0], mv[:, 0:n, 0], ALU.mult)
                    ve.drain()
                    ve.scalar_tensor_tensor(out=v, in0=t, scalar=eps, in1=mv[:, 0:n, 1], op0=ALU.add, op1=ALU.add)
                else:
                    ve.tensor_scalar(v, mv[:, 0:n, 1], eps, None, ALU.add)
                ve.drain()
                ve.tensor_scalar(ti[:, 0:n], v.bitcast(I32), 1, None, ALU.logical_shift_right)
                ve.tensor_scalar(h, v, -0.5, None, ALU.mult)
                ve.drain()
                ve.tensor_scalar(y.bitcast(I32), ti[:, 0:n], -1.0, float(0x5f3759df), ALU.mult, ALU.add)
                for step in range(3):
                    ve.drain()
                    ve.tensor_tensor(t, y, y, ALU.mult)
                    ve.drain()
                    ve.tensor_tensor(t, t, h, ALU.mult)
                    ve.drain()
                    ve.scalar_tensor_tensor(out=out if step == 2 else y, in0=t, scalar=1.5, in1=y, op0=ALU.add, op1=ALU.mult)
                ve.drain()

            def moments(src, n):
                for j in range(n):
                    ve.bn_stats(st[:, j, :], src[:, j, :])
                ve.drain()
                for j in range(n):
                    ve.bn_aggr(mv[:, j, :], st[:, j, :])
                ve.drain()

            def norm(dst, src, eps, rms=False, n=CT):
                moments(src, n)
                rstd(yy[:, 0:n], n, eps, rms)
                for j in range(n):
                    if rms:
                        ve.tensor_scalar(dst[:, j, :], src[:, j, :], yy[:, j:j + 1], None, ALU.mult)
                    else:
                        ve.tensor_scalar(dst[:, j, :], src[:, j, :], mv[:, j, 0:1], yy[:, j:j + 1], ALU.subtract, ALU.mult)

            def rows_of(bank):
                return ps[:, bank:bank + 2, 0:2 * D].rearrange("p b (j d) -> p b j d", j=2)

            def quad(t):
                return t[:, :, :].rearrange("p (b j) d -> p b j d", b=2)

            ve.memset(zero, 0.0).then_inc(s_zz, 1)
            for k in range(2):
                ve.memset(dec[k].rearrange("p g (b t) -> p (g b) t", b=CT)[:, :, 0:1], 0.0)
            ve.wait_ge(s_sm, 4 * 16)
            ve.tensor_copy(sel[:, :], cst[0:KH, C_SEL:C_SEL + 32])
            for g in range(DG):
                ve.tensor_scalar(diag_d[:, g, :], ident, col[:, V_DSK + g:V_DSK + g + 1], None, ALU.mult)
            ve.drain()
            ve.sem_inc(s_bfree, 2)
            ve.sem_inc(s_decfree, 2)

            def embed_norm(c, n):
                ve.wait_ge(s_fsum, c + n)
                h = h_rows[:, c * CT:(c + n) * CT, :]
                norm(h, h, LN_EPS, n=n * CT)
                ve.drain().then_inc(s_fn, n)

            def embed_rows(c, n):
                ve.wait_ge(s_femb, c + n)
                x = x_rows[:, c * CT:(c + n) * CT, :]
                norm(x, h_rows[:, c * CT:(c + n) * CT, :], LN_EPS, n=n * CT)
                ve.drain()
                moments(x, n * CT)
                rstd(x_rms[:, c * CT:(c + n) * CT], n * CT, RMS_EPS, True)

            def enter_scale(c):
                tiles = ds(c * CT, CT)
                ve.tensor_tensor(nrF[:, :, :], x_rows[:, tiles, :],
                                 x_rms[:, tiles].rearrange("p (t a) -> p t a", a=1).broadcast_to((P, CT, D)), ALU.mult)
                ve.drain().then_inc(s_hn, 1)

            def enter_xT(c):
                ve.wait_ge(s_hnT, c + 1)
                for k in range(2):
                    ve.tensor_scalar(xTF[:, k, :], ps[0:KH, 5 + k, :], col[0:KH, V_N1 + k:V_N1 + k + 1], None, ALU.mult)
                ve.drain().then_inc(s_xT, 1)

            def enter_z(c, gs):
                for g in gs:
                    ve.wait_ge(s_z, c * DG + g + 1)
                    ve.wait_ge(s_sig, c * DG + g + 1)
                    ve.tensor_tensor(zT[:, g, :], ps[:, (6, 5, 7)[g], :], tA[:, g, :], ALU.mult).then_inc(s_zs, 1)

            def enter_bc(c):
                ve.wait_ge(s_xbc, c + 1)
                ve.wait_ge(s_dti, c + 1)
                ve.tensor_copy(bc_n[:, :], ps[0:KH, 6, :])
                ve.drain()
                ve.tensor_tensor(bc_r, ps[0:KH, 6, :], bc_n[:, :], ALU.subtract)
                ve.drain().then_inc(s_bcp, 1)
                ve.tensor_copy(bc_b, bc_r)
                ve.tensor_copy(bc_n[32:64, :], bc_r[32:64, :])
                ve.drain()
                ve.tensor_tensor(bc_r, bc_r, bc_b, ALU.subtract)
                ve.drain()
                ve.tensor_copy(bc_n[64:96, :], bc_r[64:96, :])
                ve.drain()

            def hand_bc():
                ve.tensor_copy(bc_p[:, :], bc_n[:, :])
                ve.drain().then_inc(s_bch, 1)

            def sum_steps(c):
                ve.wait_ge(s_sp, c + 1)
                ve.tensor_tensor(dtN, dtN, tA, ALU.add)
                ve.drain().then_inc(s_step, 1)

            def leave_rows(c):
                ve.wait_ge(s_op, c + 1)
                chunk = ds(c * CT, CT)
                ve.tensor_tensor(quad(mr), x_rows[:, chunk, :].rearrange("p (b j) d -> p b j d", b=2), rows_of(5), ALU.add)
                ve.drain().then_inc(s_opr, 1)
                ve.tensor_tensor(er[:, :, :], h_rows[:, chunk, :], mr[:, :, :], ALU.add)
                norm(nr, mr, RMS_EPS, rms=True)
                ve.drain().then_inc(s_hf, 1)

            def leave_xT(c):
                ve.wait_ge(s_hfT, c + 1)
                for k in range(2):
                    ve.tensor_scalar(xT[:, k, :], ps[0:KH, 5 + k, :], col[0:KH, V_NF + k:V_NF + k + 1], None, ALU.mult)
                ve.drain().then_inc(s_fT, 1)

            def leave_act(c, fs):
                for f in fs:
                    ve.wait_ge(s_sl, c * FF0 + f + 1)
                    ve.tensor_tensor(actT0[:, f, :], actT0[:, f, :], ps[:, (6, 5, 7, 6)[f], :], ALU.mult).then_inc(s_act, 1)

            def leave_norm(c):
                ve.wait_ge(s_dn, c + 1)
                for b, bank in ((0, 7), (1, 5)):
                    ve.tensor_tensor(er[:, 2 * b:2 * b + 2, :], er[:, 2 * b:2 * b + 2, :],
                                     ps[:, bank, 0:2 * D].rearrange("p (j d) -> p j d", j=2), ALU.add)
                ve.drain()
                ve.tensor_copy(h_rows[:, ds(c * CT, CT), :], er[:, :, :])
                norm(nr, er, LN_EPS)
                ve.drain().then_inc(s_xn, 1)
                ve.tensor_copy(x_rows[:, ds(c * CT, CT), :], nr[:, :, :])

            def leave_rT(c):
                ve.wait_ge(s_xnT, c + 1)
                ve.tensor_copy(xT[:, :, :], ps[0:KH, 6:8, :])
                ve.drain().then_inc(s_rT, 1)

            def leave_scores(c):
                ve.wait_ge(s_sc, c + 1)
                ve.tensor_tensor(sc0[:, ds(c * CT, CT), :], ps[:, 7, 0:CT * E0].rearrange("p (j e) -> p j e", e=E0),
                                 row[:, R_BR2:R_BR2 + E0].rearrange("p (a e) -> p a e", a=1).broadcast_to((P, CT, E0)), ALU.add)
                ve.drain().then_inc(s_ch, 1)

            def scan_chunk(i, first, last):
                ve.tensor_tensor(uT, dtN, zT, ALU.mult)
                ve.drain()
                for s in range(NST):
                    k, n = s % 2, i * NST + s
                    ve.wait_ge(s_cs, n + 1)
                    ve.tensor_tensor(bxs, uT, bcs[:, k, 0:1, :].broadcast_to((P, DG, CN)), ALU.mult)
                    ve.drain().then_inc(s_bfree, 1)
                    ve.wait_ge(s_dec, n + 1)
                    ve.wait_ge(s_cfree, n + 1)
                    ve.tensor_tensor_scan(hid[k].rearrange("p g t -> p (g t)"), dec[k].rearrange("p g t -> p (g t)"),
                                          bxs.rearrange("p g t -> p (g t)"), 0.0, ALU.mult, ALU.add).then_inc(s_scan, 1)
                    ve.drain().then_inc(s_decfree, 1)
                    if not first and s == 2:
                        leave_rows(i - 1)
                    if not last:
                        if s == 0:
                            enter_scale(i + 1)
                        if s == 2:
                            enter_xT(i + 1)
                        if s in (6, 7):
                            enter_z(i + 1, ((0,), (1, 2))[s - 6])
                        if s == 8:
                            enter_bc(i + 1)
                        if s == 14:
                            ve.wait_ge(s_cb, i * NST + NST)
                            hand_bc()
                        if s == 15:
                            sum_steps(i + 1)
                    if not first:
                        if s == 3:
                            leave_xT(i - 1)
                        if s in (10, 11):
                            leave_act(i - 1, ((0, 1, 2), (3,))[s - 10])
                        if s == 12:
                            leave_norm(i - 1)
                        if s == 13:
                            leave_rT(i - 1)
                        if s == 15:
                            leave_scores(i - 1)
                    if first:
                        if s == 7:
                            embed_norm(2, 2)
                        if s == 10:
                            embed_rows(2, 2)

            embed_norm(0, 1)
            embed_rows(0, 1)
            enter_scale(0)
            ve.wait_ge(s_neg, 1)
            ve.tensor_scalar(neg_a, neg_a, -1.0, None, ALU.mult)
            ve.drain().then_inc(s_cst, 1)
            enter_xT(0)
            enter_z(0, range(DG))
            embed_norm(1, 1)
            enter_bc(0)
            embed_rows(1, 1)
            hand_bc()
            sum_steps(0)
            scan_chunk(0, True, False)
            with ve.Fori(1, NCH - 1) as i:
                scan_chunk(i, False, False)
            scan_chunk(NCH - 1, False, True)
            leave_rows(NCH - 1)
            leave_xT(NCH - 1)
            leave_act(NCH - 1, range(FF0))
            leave_norm(NCH - 1)
            leave_rT(NCH - 1)
            leave_scores(NCH - 1)

            def route(m, ne, nb, sc, meanwhile=None):
                def te(n):
                    return rt(n, B * ne).rearrange("p (t e) -> p t e", t=B)

                def et(n):
                    return rt(n, B * ne).rearrange("p (e t) -> p e t", e=ne)

                def per_tile(ap):
                    return ap.rearrange("p (t a) -> p t a", a=1).broadcast_to((P, B, ne))

                rev = cst[:, C_REV:C_REV + ne].rearrange("p (a e) -> p a e", a=1).broadcast_to((P, B, ne))
                one, two, both, tmp = te(0), te(1), te(2), te(3)
                m1, m2, km = rt(8, B), rt(9, B), rt(10, B)

                def pick(hot, scores, best):
                    ve.tensor_reduce(best, scores, AXX, ALU.max)
                    ve.drain()
                    ve.tensor_tensor(tmp, scores, per_tile(best), ALU.is_equal)
                    ve.drain()
                    ve.tensor_tensor(tmp, tmp, rev, ALU.mult)
                    ve.drain()
                    ve.tensor_reduce(km, tmp, AXX, ALU.max)
                    ve.drain()
                    ve.tensor_tensor(hot, tmp, per_tile(km), ALU.is_equal)
                    ve.drain()

                pick(one, sc[:, :, :], m1)
                rest = te(11)
                ve.scalar_tensor_tensor(out=rest, in0=one, scalar=NEG, in1=sc[:, :, :], op0=ALU.mult, op1=ALU.add)
                ve.drain()
                pick(two, rest, m2)
                ve.tensor_tensor(both, one, two, ALU.add)
                ve.drain().then_inc(s_mask[m], 1)
                ve.tensor_tensor(rt(4, B), m2, m1, ALU.subtract)
                if m:
                    ve.tensor_tensor(te(6), sc[:, :, :], per_tile(m1), ALU.subtract)
                ve.drain().then_inc(s_dl[m], 1)

                if meanwhile:
                    meanwhile()
                ve.wait_ge(s_rank[m], 1)
                ve.tensor_copy(et(12), ps[:, 7, 0:B * ne].rearrange("p (t e) -> p e t", e=ne))
                ve.drain()
                ve.tensor_tensor_scan(rt(13, B * ne), cst[:, C_RES:C_RES + B * ne], rt(12, B * ne), 0.0, ALU.mult, ALU.add)
                ve.drain()
                total = et(13)[:, :, B - 1:B].broadcast_to((P, ne, B))
                ve.tensor_tensor(et(14), total, cst[:, C_THR:C_THR + B].rearrange("p (a t) -> p a t", a=1)
                                 .broadcast_to((P, ne, B)), ALU.is_gt)
                ve.tensor_tensor(rt(12, B * ne), rt(13, B * ne), rt(12, B * ne), ALU.subtract)
                ve.drain()
                blocks, last, start = rt(15, ne), rt(16, ne), rt(17, ne)
                ve.tensor_reduce(blocks, et(14), AXX, ALU.add)
                ve.drain()
                ve.tensor_tensor_scan(last, cst[:, C_ONE:C_ONE + ne], blocks, 0.0, ALU.mult, ALU.add)
                ve.drain()
                ve.tensor_tensor(start, last, blocks, ALU.subtract)
                ve.drain()
                ve.scalar_tensor_tensor(out=et(12), in0=start.rearrange("p (e a) -> p e a", a=1).broadcast_to((P, ne, B)),
                                        scalar=float(P), in1=et(12), op0=ALU.mult, op1=ALU.add)
                ve.drain()
                where = rt(12, B * ne).rearrange("p (e t) -> p t e", e=ne)
                ve.tensor_tensor(te(14), where, ps[:, 6, 0:B * ne].rearrange("p (t e) -> p t e", e=ne), ALU.add)
                ve.drain()
                for r, hot in ((0, one), (1, two)):
                    ve.tensor_tensor(tmp, te(14), hot, ALU.mult)
                    ve.drain()
                    ve.tensor_reduce(km, tmp, AXX, ALU.add)
                    ve.drain()
                    ve.tensor_copy(pos_i[:, r, :], km)
                    ve.drain()
                past = arena[0:1, 15360:15360 + nb * ne].rearrange("p (b e) -> p b e", e=ne)
                ve.tensor_tensor(past, last[0:1, :].rearrange("p (a e) -> p a e", a=1).broadcast_to((1, nb, ne)),
                                 cst[0:1, C_BLK:C_BLK + nb].rearrange("p (b a) -> p b a", a=1).broadcast_to((1, nb, ne)), ALU.is_le)
                ve.drain()
                num = rt(18, nb)[0:1, :]
                ve.tensor_reduce(num, past, AXX, ALU.add)
                ve.drain()
                ve.tensor_scalar(eid[:, 0:nb], num, float(ne - 1), None, ALU.min)
                ve.drain().then_inc(s_pos[m], 1)

                ve.wait_ge(s_ex[m], 1)
                if m:
                    ve.tensor_reduce(rt(19, B), te(7), AXX, ALU.add)
                else:
                    ve.tensor_scalar(rt(19, B), rt(5, B), 1.0, None, ALU.add)
                ve.drain()
                ve.reciprocal(gate_w[:, 0, :], rt(19, B))
                ve.drain()
                ve.tensor_tensor(gate_w[:, 1, :], gate_w[:, 0, :], rt(5, B), ALU.mult)
                ve.drain()

            def expert_rows_out(m, nb, gated):
                for k in range(2):
                    ve.sem_inc(s_ybf[m][k], 1)

                def turn(i):
                    for k in range(2):
                        ve.wait_ge(s_bt[m], i * 2 + k + 1)
                        ve.tensor_copy(xbT[k], ps[0:KH, 7 * k, 0:2 * P].rearrange("p (c t) -> p c t", c=2))\
                            .then_inc(s_bx[m], 1)
                        ve.drain().then_inc(s_xbf[m][k], 1)

                def pair(i, more):
                    if gated:
                        for k in range(2):
                            ve.wait_ge(s_bg[m], i * 2 + k + 1)
                            ve.tensor_tensor(hbT[k][:, 0:EF1, :], hbT[k][:, 0:EF1, :],
                                             ps[:, 2 + 2 * k, :].rearrange("p (f t) -> p f t", f=EF1), ALU.mult)
                            ve.drain().then_inc(s_ba[m], 1)
                    if more:
                        turn(i + 1)
                    for k in range(2):
                        ve.wait_ge(s_by[m], i * 2 + k + 1)
                        ve.wait_ge(s_ybf[m][k], i + 1)
                        if gated:
                            last = ve.tensor_copy(yb[k], ps[:, 5 + k, 0:D])
                        else:
                            last = ve.tensor_tensor(yb[k], ps[:, 5 + k, 0:D], ew_out[k][:, EF0 * D + EF0:], ALU.add)
                        last.then_inc(s_yb[m], 1)
                        ve.drain().then_inc(s_w2f[m][k], 1)

                turn(0)
                with ve.Fori(0, nb // 2 - 1) as i:
                    pair(i, True)
                pair(nb // 2 - 1, False)

            route(0, E0, NB0, sc0)
            expert_rows_out(0, NB0, False)

            def add_experts(m, dst, src, t0):
                for j in range(CT):
                    ve.scalar_tensor_tensor(out=dst(j), in0=g1[:, ds(t0 + j, 1), :], scalar=gate_w[:, 0, ds(t0 + j, 1)],
                                            in1=src(j), op0=ALU.mult, op1=ALU.add)
                ve.drain()
                for j in range(CT):
                    ve.scalar_tensor_tensor(out=dst(j), in0=g2[:, ds(t0 + j, 1), :], scalar=gate_w[:, 1, ds(t0 + j, 1)],
                                            in1=dst(j), op0=ALU.mult, op1=ALU.add)
                ve.drain()

            causal = cst[:, C_CAUSAL:C_CAUSAL + P].rearrange("p (a b k) -> p a b k", a=1, b=1).broadcast_to((P, 4, 3, P))
            ve.memset(vr[:, :, :, HD:HD + 1], 1.0)

            def joined(i):
                ve.wait_ge(s_g[0], i * (2 * CT * 16) + 2 * CT * 16)
                hr = lambda j: h_rows[:, ds(i * CT + j, 1), :]
                add_experts(0, hr, hr, i * CT)
                norm(ar, h_rows[:, ds(i * CT, CT), :], LN_EPS)
                ve.drain().then_inc(t_xn, 1)

            def shared_mul(i, f, banks):
                ve.wait_ge(t_u, i * SF + f + 1)
                ve.wait_ge(t_sl, i * SF + f + 1)
                ve.tensor_tensor(actT1[:, f, :], actT1[:, f, :], ps[:, banks[f][1], :], ALU.mult).then_inc(t_act, 1)

            def shared_rows(i, bank):
                ve.wait_ge(t_dn, i + 1)
                h = h_rows[:, ds(i * CT, CT), :].rearrange("p (b j) d -> p b j d", b=2)
                ve.tensor_tensor(h, h, rows_of(bank), ALU.add)
                ve.drain().then_inc(t_ch, 1)

            def attention_chunk(i, first, more):
                chunk = h_rows[:, ds(i * CT, CT), :]
                if not first:
                    shared_mul(i - 1, 0, mixed_banks)
                    shared_mul(i - 1, 1, mixed_banks)
                ve.wait_ge(t_xnT, i + 1)
                ve.tensor_copy(xT[:, :, :], ps[0:KH, 0:2, :])
                ve.drain().then_inc(t_xT, 1)
                ve.tensor_tensor(chunk, chunk, bproj_b, ALU.add)
                if more:
                    joined(i + 1)
                ve.wait_ge(t_v, i + 1)
                for b in range(2):
                    ve.tensor_tensor(vr[:, 2 * b:2 * b + 2, :, 0:HD],
                                     ps[:, b, 0:2 * D].rearrange("p (t h d) -> p t h d", t=2, h=H),
                                     row[:, R_BV:R_BV + D].rearrange("p (a h d) -> p a h d", a=1, h=H).broadcast_to((P, 2, H, HD)),
                                     ALU.add)
                ve.drain().then_inc(t_vr, 1)
                if not first:
                    shared_mul(i - 1, 2, mixed_banks)

                def masked(t):
                    ve.wait_ge(t_s, i * CT + t + 1)
                    if t >= 2:
                        ve.wait_ge(t_pt, (i * CT + t - 1) * 3)
                    ve.tensor_tensor(sm[t % 2], ps[:, 2:6, 0:3 * P].rearrange("p b (a k) -> p b a k", a=3), causal, ALU.add)
                    ve.drain().then_inc(t_ms, 1)
                    ve.tensor_reduce(smax.rearrange("p (b a) -> p b a", b=4), sm[t % 2], AXX, ALU.max)
                    ve.drain()
                    ve.tensor_tensor(sm[t % 2], sm[t % 2], smax.rearrange("p (b a k) -> p b a k", b=4, k=1)
                                     .broadcast_to((P, 4, 3, P)), ALU.subtract)
                    ve.drain().then_inc(t_sm, 1)

                def over_sums(t):
                    ve.wait_ge(t_o, i * CT + t + 1)
                    o = ps[:, 1, 0:H * (HD + 1)].rearrange("p (h d) -> p h d", h=H)
                    ve.reciprocal(rden.rearrange("p (h a) -> p h a", a=1), o[:, :, HD:HD + 1])
                    ve.drain()
                    ve.tensor_tensor(nr[:, t, :].rearrange("p (h d) -> p h d", h=H), o[:, :, 0:HD],
                                     rden.rearrange("p (h a) -> p h a", a=1).broadcast_to((P, H, HD)), ALU.mult)
                    ve.drain().then_inc(t_or, 1)

                for t in range(CT + 2):
                    if t < CT:
                        masked(t)
                    if not first and 1 <= t <= CT:
                        shared_mul(i - 1, 2 + t, mixed_banks)
                    if t >= 2:
                        over_sums(t - 2)
                ve.wait_ge(t_oT, i + 1)
                ve.tensor_copy(xT[:, :, :], ps[0:KH, 2:4, :])
                ve.drain().then_inc(t_oTs, 1)
                if not first:
                    shared_mul(i - 1, 7, mixed_banks)
                ve.wait_ge(t_pr, i + 1)
                rows = chunk.rearrange("p (b j) d -> p b j d", b=2)
                ve.tensor_tensor(rows, rows, rows_of(4), ALU.add)
                ve.drain()
                norm(nr, chunk, LN_EPS)
                ve.drain().then_inc(t_fn, 1)
                ve.tensor_copy(x_rows[:, ds(i * CT, CT), :], nr[:, :, :])
                if not first:
                    shared_rows(i - 1, 2)
                ve.wait_ge(t_fnT, i + 1)
                ve.tensor_copy(xTS[:, :, :], ps[0:KH, 6:8, :])
                ve.drain().then_inc(t_fT, 1)
                ve.wait_ge(t_rs, i + 1)
                ve.tensor_copy(sc1[:, ds(i * CT, CT), :], ps[:, 6, 0:CT * E1].rearrange("p (j e) -> p j e", e=E1))
                ve.drain().then_inc(t_rsr, 1)

            joined(0)
            attention_chunk(0, True, True)
            with ve.Fori(1, NCH - 1) as i:
                attention_chunk(i, False, True)
            attention_chunk(NCH - 1, False, False)

            def first_three():
                for f in range(3):
                    shared_mul(NCH - 1, f, last_banks)

            route(1, E1, NB1, sc1, first_three)
            for f in range(3, SF):
                shared_mul(NCH - 1, f, last_banks)
            shared_rows(NCH - 1, 6)
            expert_rows_out(1, NB1, True)
            with ve.Fori(0, NCH) as i:
                ve.wait_ge(s_g[1], i * (2 * CT * 16) + 2 * CT * 16)
                hr = lambda j: h_rows[:, ds(i * CT + j, 1), :]
                add_experts(1, hr, hr, i * CT)
                ve.drain().then_inc(s_fin, 1)


def kernel(**inputs):
    import numpy as np
    import concourse.bacc as bacc
    from concourse import mybir as _mybir
    from concourse.bass_utils import run_bass_kernel_spmd as run

    a = {k: np.asarray(v) for k, v in inputs.items()}

    def halves(w):
        return w.reshape(2, KH, -1).transpose(1, 0, 2)

    def groups(w):
        return w.reshape(-1, P, w.shape[-1]).transpose(1, 0, 2)

    def columns(v, p):
        o = np.zeros((P, v.size // p), v.dtype)
        o[:p] = v.reshape(-1, p).T
        return o

    c = np.zeros((P, C_END), np.float32)
    i = np.arange(P)
    c[:, C_ID:C_ID + P] = i[:, None] == i
    c[:, C_TRI:C_TRI + P] = i[:, None] < i
    c[:, C_ONE:C_ONE + P] = 1
    c[:, C_CAUSAL:C_CAUSAL + P] = np.where(i[:, None] >= i, 0, NEG)
    for r in range(3):
        c[32 * r:32 * r + 32, C_SEL:C_SEL + 32] = np.eye(32)
    c[:, C_REV:C_REV + 16] = 16 - np.arange(16)
    c[:, C_THR:C_THR + B] = P * np.arange(B)
    c[:, C_BLK:C_BLK + NB1] = np.arange(NB1)
    c[:, C_RES:C_RES + 256] = np.arange(256) % B != 0

    rows = np.concatenate([a["L0_tok_gamma"], a["L0_tok_beta"], a["L1_attn_c_attn_b"][2 * D:], a["L1_attn_c_proj_b"],
                           a["L0_ffn_br2"]])[None]

    def strips(w):
        o = np.zeros((w.shape[0], H, 32), w.dtype)
        o[:, :, :HD] = w.reshape(w.shape[0], H, HD)
        return o.reshape(w.shape[0], 3 * P)

    wa, ba = a["L1_attn_c_attn_w"], a["L1_attn_c_attn_b"][None]
    bqk = np.concatenate([strips(ba[:, :D]), strips(ba[:, D:2 * D])], 1)[0]
    cols = np.concatenate([columns(a["L0_attn_w_norm1"], KH), columns(a["L0_attn_w_ffn_norm"], KH),
                           columns(a["L0_ffn_br1"], KH), columns(a["L0_attn_b_dt"], P), columns(a["L0_attn_D_skip"], P),
                           columns(bqk, P), groups(a["L0_attn_A_log"]).reshape(P, -1)], 1)
    wx = a["L0_attn_W_xproj"]
    e0_in = np.stack([halves(w.T).reshape(KH, -1) for w in a["L0_ffn_W1"]])
    e0_out = np.stack([np.concatenate([groups(w2.T).reshape(P, -1), columns(b1, P), np.broadcast_to(b2, (P, D))], 1)
                       for w2, b1, b2 in zip(a["L0_ffn_W2"], a["L0_ffn_b1"], a["L0_ffn_b2"])])
    e1_in = np.stack([np.concatenate([halves(w1.T).reshape(KH, -1), halves(w3.T).reshape(KH, -1)], 1)
                      for w1, w3 in zip(a["L1_ffn_w1"], a["L1_ffn_w3"])])
    e1_out = np.stack([groups(w2.T).reshape(P, -1) for w2 in a["L1_ffn_w2"]])
    named = dict(
        tok=a["x"].T, seg=a["mask_BS_i1_0"].T, tok_tab=a["L0_tok_tok_table"], seg_tab=a["L0_tok_seg_table"],
        pos_tab=a["L0_tok_pos_table"], consts=c, rows=rows, cols=cols,
        w_in=halves(a["L0_attn_W_in"].T), w_gate=halves(a["L0_attn_W_gate"].T),
        w_xdt=groups(wx[:KH].T), w_xbc=groups(np.concatenate([wx[KH:].T] * 3, 1)), w_dt=a["L0_attn_W_dt"].T,
        w_out=groups(a["L0_attn_W_out"].T), w_up=halves(a["L0_attn_W_up"].T), w_gf=halves(a["L0_attn_W_gate_ffn"].T),
        w_down=groups(a["L0_attn_W_down"].T), w_r1=halves(a["L0_ffn_Wr1"].T), w_r2=halves(a["L0_ffn_Wr2"].T),
        w_qk=halves(np.concatenate([strips(wa[:, :D]), strips(wa[:, D:2 * D])], 1)), w_v=halves(wa[:, 2 * D:]),
        w_proj=halves(a["L1_attn_c_proj_w"]), w_g=halves(a["L1_ffn_gate_w"].T),
        w_s1=halves(a["L1_ffn_sw1"].T), w_s3=halves(a["L1_ffn_sw3"].T), w_s2=groups(a["L1_ffn_sw2"].T),
        e0_in=e0_in, e0_out=e0_out, e1_in=e1_in, e1_out=e1_out)
    named = {k: np.ascontiguousarray(v) for k, v in named.items()}

    nc = bacc.Bacc("TRN2", target_bir_lowering=False, num_devices=1)
    args = [nc.dram_tensor("in_" + k, v.shape, _mybir.dt.from_np(v.dtype), kind="ExternalInput").ap() for k, v in named.items()]
    out = nc.dram_tensor("out_0", (B, P, D), F32, kind="ExternalOutput").ap()
    tower(nc, *args, out)
    r = run(nc, [{"in_" + k: v for k, v in named.items()}], core_ids=[0])
    return r.results[0]["out_0"]
```

```python
from contextlib import ExitStack

import concourse.bass as bass
from concourse import mybir

F32 = mybir.dt.float32
I32 = mybir.dt.int32
BF16 = mybir.dt.bfloat16
ACT = mybir.ActivationFunctionType
ALU = mybir.AluOpType
AXX = mybir.AxisListType.X
ds = bass.ds

P = 128
B = 16
D = 192
KH = 96
CT = 4
NCH = B // CT
CN = CT * P
NST = 16
DG = 3
FF0 = 4
E0, E1 = 8, 16
EF0, EF1 = 6, 4
SF = 8
H = 12
HD = D // H
NEG = -3.0e38
LN_EPS, RMS_EPS = 1e-5, 1e-6


def blocks_needed(experts):
    n = 2 * B * P // P + experts - 1
    return n + n % 2


NB0, NB1 = blocks_needed(E0), blocks_needed(E1)
REG = (B + 1) * P

C_ID, C_TRI, C_ONE, C_CAUSAL = 0, 128, 256, 384
C_SEL = 512
C_REV = C_SEL + 32
C_THR = C_REV + 16
C_BLK = C_THR + 16
C_REG = C_BLK + NB1
C_END = C_REG + E1
R_GAM, R_BET, R_BV, R_BP, R_BR2, R_END = 0, D, 2 * D, 3 * D, 4 * D, 4 * D + E0
V_N1, V_NF, V_BR1, V_BDT, V_DSK, V_BQK, V_ALOG, V_END = 0, 2, 4, 6, 9, 12, 18, 18 + DG * NST


def tower(nc, tok, seg, tok_tab, seg_tab, pos_tab, consts, rows, cols, w_in, w_gate, w_x, w_dt, w_out,
          w_up, w_gf, w_down, w_r1, w_r2, w_qk, w_v, w_proj, w_g, w_s1, w_s3, w_s2, e0_in, e0_out, e1_in, e1_out,
          out):
    with ExitStack() as ctx:
        def sb(name, shape, dt=F32):
            return ctx.enter_context(nc.sbuf_tensor(name, shape, dt))

        def sem(name):
            return ctx.enter_context(nc.semaphore(name))

        ps = ctx.enter_context(nc.psum_tensor("ps", [P, 8, 512], F32))
        sorted_rows = [nc.dram_tensor(f"sorted{n}", (ne * REG + P, D), F32, kind="Internal").ap() for n, ne in ((0, E0), (1, E1))]
        expert_rows = [nc.dram_tensor(f"expert{n}", (nb * P, D), F32, kind="Internal").ap() for n, nb in ((0, NB0), (1, NB1))]

        h_rows = sb("h_rows", [P, B, D])
        x_rows = sb("x_rows", [P, B, D])
        tok_i = sb("tok_i", [P, B], I32)
        seg_i = sb("seg_i", [P, B], I32)
        cst = sb("cst", [P, C_END])
        row = sb("row", [P, R_END])
        col = sb("col", [P, V_END])
        pos = sb("pos", [P, D])
        sel = sb("sel", [KH, 32], BF16)
        wreg = sb("wreg", [P, 7936])

        def carve(shapes):
            out, at = [], 0
            for parts, *dims in shapes:
                n = 1
                for d in dims:
                    n *= d
                ap = wreg[0:parts, at:at + n]
                out.append(ap.rearrange("p (a b) -> p a b", a=dims[0]) if len(dims) == 2 else ap)
                at += n
            return out

        win, wgate, wx, wdt, wout, wup, wgf, wdown, wr1, diag_d, neg_a = carve([
            (KH, 2, DG * P), (KH, 2, DG * P), (P, DG, P), (KH, DG * P), (P, DG, D), (KH, 2, FF0 * P),
            (KH, 2, FF0 * P), (P, FF0, D), (KH, 2, D), (P, DG, P), (P, DG, NST)])
        wqk, wv, wproj, ws1, ws3, ws2 = carve([
            (KH, 2, 6 * P), (KH, 2, D), (KH, 2, D), (KH, 2, SF * P), (KH, 2, SF * P), (P, SF, D)])
        wr2 = sb("wr2", [KH, 2, E0])
        wg = sb("wg", [KH, 2, E1])
        ew_in_all = [sb(f"ew_in{k}", [P, 2048]) for k in range(2)]
        ew_in = [w[0:KH, :] for w in ew_in_all]
        ew_out = [sb(f"ew_out{k}", [P, EF0 * D + EF0 + D]) for k in range(2)]

        er = sb("er", [P, CT, D])
        mr = sb("mr", [P, CT, D])
        nr = sb("nr", [P, CT, D])
        xT = sb("xT", [KH, 2, CN])
        nrF = sb("nrF", [P, CT, D])
        xTF = sb("xTF", [KH, 2, CN])
        x_rms = sb("x_rms", [P, B])
        st = sb("st", [P, 2 * CT, 6])
        mv = sb("mv", [P, 2 * CT, 2])
        vv, vh, yy, tt = [sb(n, [P, 2 * CT]) for n in ("vv", "vh", "yy", "tt")]
        ti = sb("ti", [P, 2 * CT], I32)
        arena = sb("arena", [P, 13 * 1536 + FF0 * CN])

        def part(n, words, parts=P):
            return arena[0:parts, n:n + words]

        def wide(n):
            return part(n * 1536, 1536).rearrange("p (g t) -> p g t", g=DG)

        zT, dtT, uT, tA = wide(0), wide(1), wide(2), wide(3)
        dec, bxs, hid, hc = [wide(4), wide(5)], wide(6), [wide(7), wide(8)], [wide(9), wide(10)]
        dtN, yT = wide(11), wide(12)
        actT0 = part(13 * 1536, FF0 * CN).rearrange("p (f t) -> p f t", f=FF0)
        bcs = ew_in_all[0][:, :].rearrange("p (k r t) -> p k r t", k=2, r=2)
        dti = xTF[:, 0, :]
        BC = slice(KH, P)
        nrF_flat = nrF[BC, :, :].rearrange("p j d -> p (j d)")
        bc_r = nrF_flat[:, 0:CN]
        bc_b = nrF_flat[:, CN:CN + CN // 2].bitcast(BF16)
        bc_p = sb("bc_p", [KH, CN], BF16)
        bc_n = sb("bc_n", [KH, CN], BF16)
        g1 = part(0, B * D).rearrange("p (t d) -> p t d", t=B)
        g2 = part(B * D, B * D).rearrange("p (t d) -> p t d", t=B)
        ar = er
        qkT = part(6144, 6 * CN).rearrange("p (f t) -> p f t", f=6)
        vr = part(9216, CT * H * (HD + 1)).rearrange("p (t h d) -> p t h d", t=CT, h=H)
        sm = [part(n, H * P).rearrange("p (b a k) -> p b a k", b=4, a=3) for n in (10240, 13824)]
        pT = [part(n, H * P).rearrange("p (h q) -> p h q", h=H) for n in (11776, 15360)]
        xTS = xTF
        rden = part(13312, H)
        smax = part(13328, H)
        actT1 = part(17920, SF * CN).rearrange("p (f t) -> p f t", f=SF)
        xb = [part(6144 + 256 * k, D) for k in range(2)]
        xbT = [part(6656 + 256 * k, 2 * P, KH).rearrange("p (k t) -> p k t", k=2) for k in range(2)]
        hbT = [part(7168 + 768 * k, EF0 * P).rearrange("p (f t) -> p f t", f=EF0) for k in range(2)]
        yb = [part(8704 + 256 * k, D) for k in range(2)]
        sc1 = sb("sc1", [P, B, E1])
        sc0 = sc1[:, :, 0:E0]
        hot_all = [sb(f"hot{r}", [P, B * E1]) for r in range(2)]
        row_f = sb("row_f", [P, 2, B])
        row_i = sb("row_i", [P, 2, B], I32)
        seen_all = sb("seen", [P, E1])
        best = sb("best", [P, 2, B])
        gate_w = sb("gate_w", [P, 2, B])
        pos_i = sb("pos_i", [P, 2, B], I32)
        eid = sb("eid", [1, NB1], I32)
        rid = sb("rid", [1, NB1], I32)
        zid = sb("zid", [1, E1], I32)
        zero = sb("zero", [P, D])

        def rt(n, words=256):
            return ew_in_all[1][:, 256 * n:256 * n + words]

        def rb(n, words=256):
            return part(9216 + 256 * n, words)

        def tiles_by(words, t0, nt, ne):
            return words[:, t0 * ne:(t0 + nt) * ne].rearrange("p (t e) -> p t e", e=ne)

        ident = cst[:, C_ID:C_ID + P]
        bproj_b = row[:, R_BP:R_BP + D].rearrange("p (a d) -> p a d", a=1).broadcast_to((P, CT, D))

        s_idx, s_sm, s_wa, s_wb = sem("s_idx"), sem("s_sm"), sem("s_wa"), sem("s_wb")
        s_emb = [sem(f"s_emb{c}") for c in range(3)]
        s_cst, s_neg = sem("s_cst"), sem("s_neg")
        s_fsum, s_fn, s_femb = sem("s_fsum"), sem("s_fn"), sem("s_femb")
        s_hn, s_hnT, s_xT = sem("s_hn"), sem("s_hnT"), sem("s_xT")
        s_z, s_gate, s_sig, s_zs = sem("s_z"), sem("s_gate"), sem("s_sig"), sem("s_zs")
        s_xd, s_dti, s_bcp, s_dt, s_spf, s_sp = [sem(n) for n in ("s_xd", "s_dti", "s_bcp", "s_dt", "s_spf", "s_sp")]
        s_step, s_bch = sem("s_step"), sem("s_bch")
        s_cb, s_bfree, s_cfree = sem("s_cb"), sem("s_bfree"), sem("s_cfree")
        s_decfree, s_cbfree = sem("s_decfree"), sem("s_cbfree")
        s_dec, s_scan, s_cs, s_hc, s_sumd = sem("s_dec"), sem("s_scan"), sem("s_cs"), sem("s_hc"), sem("s_sumd")
        s_y, s_yT, s_op, s_opr = sem("s_y"), sem("s_yT"), sem("s_op"), sem("s_opr")
        s_hf, s_hfT, s_fT = sem("s_hf"), sem("s_hfT"), sem("s_fT")
        s_gu, s_sl, s_act, s_dn = sem("s_gu"), sem("s_sl"), sem("s_act"), sem("s_dn")
        s_xn, s_xnT, s_rT, s_r1, s_hr, s_sc, s_ch = [sem(n) for n in ("s_xn", "s_xnT", "s_rT", "s_r1", "s_hr", "s_sc", "s_ch")]
        s_mask, s_rank, s_row, s_dl, s_ex, s_zid, s_pos, s_gw, s_zero = [[sem(f"{n}{m}") for m in range(2)] for n in
                                                                    ("s_mask", "s_rank", "s_row", "s_dl", "s_ex", "s_zid", "s_pos", "s_gw", "s_zero")]
        s_scat = [sem(f"s_scat{m}") for m in range(2)]
        s_w1 = [[sem(f"s_w1_{m}{k}") for k in range(2)] for m in range(2)]
        s_w2 = [[sem(f"s_w2_{m}{k}") for k in range(2)] for m in range(2)]
        s_xb = [[sem(f"s_xb_{m}{k}") for k in range(2)] for m in range(2)]
        s_w1f = [[sem(f"s_w1f_{m}{k}") for k in range(2)] for m in range(2)]
        s_w2f = [[sem(f"s_w2f_{m}{k}") for k in range(2)] for m in range(2)]
        s_xbf = [[sem(f"s_xbf_{m}{k}") for k in range(2)] for m in range(2)]
        s_bt, s_bx, s_bh, s_ba, s_by, s_yb = [[sem(f"{n}{m}") for m in range(2)] for n in ("s_bt", "s_bx", "s_bh", "s_ba", "s_by", "s_yb")]
        s_bg = sem("s_bg")
        s_ybf = [[sem(f"s_ybf_{m}{k}") for k in range(2)] for m in range(2)]
        s_yo = [[sem(f"s_yo_{m}{k}") for k in range(2)] for m in range(2)]
        s_g = [sem(f"s_g{m}") for m in range(2)]
        t_xn, t_xnT, t_xT, t_qk, t_qkT, t_v, t_vr = [sem(n) for n in ("t_xn", "t_xnT", "t_xT", "t_qk", "t_qkT", "t_v", "t_vr")]
        t_s, t_ms, t_sm, t_p, t_pt, t_pT, t_o, t_or = [sem(n) for n in ("t_s", "t_ms", "t_sm", "t_p", "t_pt", "t_pT", "t_o", "t_or")]
        t_oT, t_oTs, t_pr, t_fn, t_fnT, t_fT = [sem(n) for n in ("t_oT", "t_oTs", "t_pr", "t_fn", "t_fnT", "t_fT")]
        t_rs, t_rsr, t_g, t_u, t_sl, t_act, t_dn, t_ch = [sem(n) for n in ("t_rs", "t_rsr", "t_g", "t_u", "t_sl", "t_act", "t_dn", "t_ch")]
        s_fin, s_out = sem("s_fin"), sem("s_out")

        ctx.enter_context(nc.allow_non_contiguous_dma("small vectors"))
        block = ctx.enter_context(nc.Block())

        leave_at = dict(out=0, rows=2, turn=2, xT=3, mlp=(8, 9, 9, 10), silu=(9, 9, 10, 10), act=(9, 9, 10, 10),
                        down=11, norm=12, turn_again=13, rT=13, router=13, relu=14, scores=14, take_scores=15)
        leave_early = dict(out=0, rows=2, turn=2, xT=3, mlp=(3, 4, 5, 6), silu=(4, 5, 6, 7), act=(4, 5, 6, 7),
                           down=8, norm=10, turn_again=11, rT=11, router=11, relu=12, scores=12, take_scores=13)

        LAST = NCH - 1
        HT, HN = CT // 2, CN // 2

        def half_cols(x):
            return slice(x * HN, (x + 1) * HN)

        mixed_banks = [(2, 3), (4, 5), (6, 7), (0, 0), (0, 0), (0, 0), (0, 0), (0, 1)]
        last_banks = [(0, 1), (2, 3), (4, 5)] * 2 + [(0, 1), (2, 3)]
        qk_order = (4, 5, 0, 1, 2, 3)

        @block.sync
        def _(sp):
            sp.dma_start(tok_i[:, :], tok).then_inc(s_idx, 16)
            sp.dma_start(seg_i[:, :], seg).then_inc(s_idx, 16)
            small = [(pos[:, :], pos_tab), (row[:, :], rows.broadcast_to((P, R_END))), (col[:, :], cols), (cst[:, :], consts)]
            first = [(win, w_in), (wgate, w_gate), (wx, w_x),
                     (wdt, w_dt), (wout, w_out), (wup, w_up), (wgf, w_gf),
                     (wdown, w_down), (wr1, w_r1), (wr2[:, :, :], w_r2), (wg[:, :, :], w_g)]
            later = [(wqk, w_qk), (wv, w_v), (wproj, w_proj),
                     (ws1, w_s1), (ws3, w_s3), (ws2, w_s2)]
            for dst, src in small:
                sp.dma_start(dst, src).then_inc(s_sm, 16)
            for dst, src in first:
                sp.dma_start(dst, src).then_inc(s_wa, 16)

            def expert_loads(m, ne, nb, t_in, t_out, n_in, n_out):
                sp.wait_ge(s_zid[m], 1)
                sp.dma_start(sorted_rows[m][ne * REG:ne * REG + P, :], zero[:, :]).then_inc(s_zero[m], 16)
                with sp.Fori(0, ne // 2) as e:
                    at = [sp.value_load(zid[0:1, ds(e * 2 + k, 1)], min_val=0, max_val=ne * REG - P) for k in range(2)]
                    for r in at:
                        sp.dma_start(sorted_rows[m][ds(r, P), :], zero[:, :]).then_inc(s_zero[m], 16)
                sp.wait_ge(s_pos[m], 1)
                sp.wait_ge(s_scat[m], 2 * B * 16)
                sp.wait_ge(s_zero[m], (ne + 1) * 16)
                with sp.Fori(0, nb // 2) as i:
                    for k in range(2):
                        sp.wait_ge(s_xbf[m][k], i + 1)
                        sp.nop(nofuse=True)
                        r = sp.value_load(rid[0:1, ds(i * 2 + k, 1)], min_val=0, max_val=ne * REG)
                        sp.dma_start(xb[k], sorted_rows[m][ds(r, P), :]).then_inc(s_xb[m][k], 16)
                    e = [sp.value_load(eid[0:1, ds(i * 2 + k, 1)], min_val=0, max_val=ne - 1) for k in range(2)]
                    for k in range(2):
                        sp.wait_ge(s_w1f[m][k], i + 1)
                        sp.nop(nofuse=True)
                        sp.dma_start(ew_in[k][:, 0:n_in], t_in[ds(e[k], 1), :, :].rearrange("a p n -> (a p) n"))\
                          .then_inc(s_w1[m][k], 16)
                    for k in range(2):
                        sp.wait_ge(s_w2f[m][k], i + 1)
                        sp.nop(nofuse=True)
                        sp.dma_start(ew_out[k][:, 0:n_out], t_out[ds(e[k], 1), :, :].rearrange("a p n -> (a p) n"))\
                          .then_inc(s_w2[m][k], 16)

            sp.wait_ge(s_ch, NCH + 1)
            for dst, src in later:
                sp.dma_start(dst, src).then_inc(s_wb, 16)
            expert_loads(0, E0, NB0, e0_in, e0_out, 2 * EF0 * P, EF0 * D + EF0 + D)
            expert_loads(1, E1, NB1, e1_in, e1_out, 4 * EF1 * P, EF1 * D)
            for c in range(NCH):
                sp.wait_ge(s_fin, c + 1)
                sp.dma_start(out[c * CT:(c + 1) * CT].rearrange("t p d -> p t d"), h_rows[:, c * CT:(c + 1) * CT, :])\
                  .then_inc(s_out, 16)
            sp.wait_ge(s_out, NCH * 16)

        @block.gpsimd
        def _(pool):
            pool.wait_ge(s_idx, 32)
            def embed(c):
                for t in range(c * CT, (c + 1) * CT):
                    pool.indirect_dma_start(h_rows[:, t, :], None, tok_tab, bass.IndirectOffsetOnAxis(tok_i[:, t:t + 1], 0))\
                        .then_inc(s_emb[min(c, 2)], 16)
                    pool.indirect_dma_start(x_rows[:, t, :], None, seg_tab, bass.IndirectOffsetOnAxis(seg_i[:, t:t + 1], 0))\
                        .then_inc(s_emb[min(c, 2)], 16)

            def spread_row(ap, n):
                return ap.rearrange("p (a d) -> p a d", a=1).broadcast_to((P, n * CT, D))

            def embed_sum(c, n):
                pool.wait_ge(s_emb[c], n * 2 * CT * 16)
                h = h_rows[:, c * CT:(c + n) * CT, :]
                pool.tensor_tensor(h, h, x_rows[:, c * CT:(c + n) * CT, :], ALU.add)
                pool.drain()
                pool.tensor_tensor(h, h, spread_row(pos[:, :], n), ALU.add)
                pool.drain().then_inc(s_fsum, n)

            def embed_affine(c, n):
                pool.wait_ge(s_fn, c + n)
                h = h_rows[:, c * CT:(c + n) * CT, :]
                pool.tensor_tensor(h, h, spread_row(row[:, R_GAM:R_GAM + D], n), ALU.mult)
                pool.drain()
                pool.tensor_tensor(h, h, spread_row(row[:, R_BET:R_BET + D], n), ALU.add)
                pool.drain().then_inc(s_femb, n)

            def scatter(m, n, t0, nt):
                pool.wait_ge(s_row[m], n)
                for t in range(t0, t0 + nt):
                    for r in range(2):
                        pool.indirect_dma_start(sorted_rows[m], bass.IndirectOffsetOnAxis(row_i[:, r, t:t + 1], 0),
                                                x_rows[:, t, :], None).then_inc(s_scat[m], 16)

            def scan_chunk(i, first):
                for s in range(NST):
                    k, n = s % 2, i * NST + s
                    pool.wait_ge(s_scan, n + 1)
                    pool.wait_ge(s_cs, n + 1)
                    pool.wait_ge(s_sumd, n + 1)
                    pool.tensor_tensor(hc[k], hid[k], bcs[:, k, 1:2, :].broadcast_to((P, DG, CN)), ALU.mult)\
                        .then_inc(s_hc, 1)
                    pool.drain().then_inc(s_cfree, 1)
                    if first and s == 2:
                        embed_sum(2, 2)
                    if first and s == 5:
                        embed_affine(2, 2)
            embed(0)
            pool.wait_ge(s_sm, 4 * 16)
            embed_sum(0, 1)
            embed_affine(0, 1)
            embed(1)
            embed(2)
            embed_sum(1, 1)
            embed(3)
            embed_affine(1, 1)
            pool.sem_inc(s_cfree, 2)
            scan_chunk(0, True)
            with pool.Fori(1, NCH) as i:
                scan_chunk(i, False)

            def store_blocks(m, nb):
                with pool.Fori(0, nb // 2) as i:
                    for k in range(2):
                        pool.wait_ge(s_yb[m], i * 2 + k + 1)
                        pool.nop(nofuse=True)
                        pool.dma_start(expert_rows[m][ds((i * 2 + k) * P, P), :], yb[k]).then_inc(s_yo[m][k], 16)
                        pool.wait_ge(s_yo[m][k], i * 16 + 16)
                        pool.nop(nofuse=True)
                        pool.drain().then_inc(s_ybf[m][k], 1)

            def gather(m, nb):
                pool.wait_ge(s_gw[m], 1)
                for k in range(2):
                    pool.wait_ge(s_yo[m][k], 16 * (nb // 2))
                for c in range(NCH):
                    for t in range(c * CT, (c + 1) * CT):
                        for r, g in ((0, g1), (1, g2)):
                            pool.indirect_dma_start(g[:, t, :], None, expert_rows[m],
                                                    bass.IndirectOffsetOnAxis(pos_i[:, r, t:t + 1], 0)).then_inc(s_g[m], 16)
                    pool.wait_ge(s_g[m], (c + 1) * 2 * CT * 16)

            for m, nb, parts in ((0, NB0, ((1, 0, 8), (2, 8, 4), (3, 12, 4))), (1, NB1, ((1, 0, 12), (2, 12, 4)))):
                for n, t0, nt in parts:
                    scatter(m, n, t0, nt)
                store_blocks(m, nb)
                gather(m, nb)

        @block.scalar
        def _(act):
            act.wait_ge(s_sm, 4 * 16)
            act.activation(neg_a, col[:, V_ALOG:V_END].rearrange("p (g s) -> p g s", g=DG), ACT.Exp).then_inc(s_neg, 1)

            def enter_gates(c, gs):
                for g in gs:
                    act.wait_ge(s_gate, c * DG + g + 1)
                    act.activation(tA[:, g, :], ps[:, (5, 7, 6)[g], :], ACT.Sigmoid).then_inc(s_sig, 1)

            def enter_low(c):
                act.wait_ge(s_xd, c + 1)
                act.activation(dti, ps[0:KH, 5, :], ACT.Copy).then_inc(s_dti, 1)

            def enter_parts(c):
                for g in range(DG):
                    act.wait_ge(s_dt, c * DG + g + 1)
                    bdt = col[:, V_BDT + g:V_BDT + g + 1]
                    act.activation(tA[:, g, :], ps[:, 5 + g, :], ACT.Abs, bias=bdt)
                    act.activation(dtN[:, g, :], ps[:, 5 + g, :], ACT.Relu, bias=bdt)
                act.drain().then_inc(s_spf, 1)

            def enter_exp():
                act.activation(tA, tA, ACT.Exp, scale=-1.0)
                act.drain()

            def enter_ln():
                act.activation(tA, tA, ACT.Ln, bias=1.0)
                act.drain().then_inc(s_sp, 1)

            def take_steps(c):
                act.wait_ge(s_step, c + 1)
                act.activation(dtT, dtN, ACT.Copy)
                act.drain()

            def leave_silu(c, fs):
                for f in fs:
                    act.wait_ge(s_gu, c * FF0 + f + 1)
                    act.activation(actT0[:, f, :], ps[:, (5, 7, 6, 5)[f], :], ACT.Silu).then_inc(s_sl, 1)

            def leave_router(c):
                act.wait_ge(s_r1, c + 1)
                for k in range(2):
                    act.activation(xT[:, k, :], ps[0:KH, 5 + k, :], ACT.Relu, bias=col[0:KH, V_BR1 + k:V_BR1 + k + 1])
                act.drain().then_inc(s_hr, 1)

            def scan_chunk(i, first, last):
                def keep_rows(s):
                    n = i * NST + s
                    act.wait_ge(s_cb, n + 1)
                    act.wait_ge(s_bfree, n + 1)
                    act.wait_ge(s_cfree, n + 1)
                    act.activation(bcs[:, s % 2, :, :], ps[:, 0:2, :], ACT.Copy).then_inc(s_cs, 1)
                    act.drain().then_inc(s_cbfree, 1)

                at = leave_early if last else leave_at
                if first:
                    keep_rows(0)
                for s in range(NST):
                    k, n = s % 2, i * NST + s
                    act.wait_ge(s_decfree, n + 1)
                    for g in range(DG):
                        o = dec[k][:, g, :].rearrange("p (b t) -> p b t", b=CT)
                        t = dtT[:, g, :].rearrange("p (b t) -> p b t", b=CT)
                        act.activation(o[:, :, 1:P], t[:, :, 1:P], ACT.Exp, scale=neg_a[:, g, s:s + 1])
                    act.drain().then_inc(s_dec, 1)
                    if s + 1 < NST or not last:
                        keep_rows(s + 1)
                    if not first:
                        if s == 0:
                            take_y(i - 1)
                    if not last:
                        if s in (4, 5, 6):
                            enter_gates(i + 1, (s - 4,))
                        if s == 7:
                            enter_low(i + 1)
                        if s == 8:
                            enter_parts(i + 1)
                        if s == 12:
                            enter_exp()
                            enter_ln()
                        if s == 15:
                            take_steps(i + 1)
                    if not first:
                        leave_silu(i - 1, [f for f in range(FF0) if at["silu"][f] == s])
                        if s == at["relu"]:
                            leave_router(i - 1)

            def take_y(c):
                act.wait_ge(s_y, c + 1)
                act.activation(yT, ps[:, 2:5, :], ACT.Copy).then_inc(s_yT, 1)

            act.sem_inc(s_cbfree, 1)
            enter_gates(0, (0, 1, 2))
            enter_low(0)
            enter_parts(0)
            enter_exp()
            enter_ln()
            take_steps(0)
            scan_chunk(0, True, False)
            with act.Fori(1, NCH - 1) as i:
                scan_chunk(i, False, False)
            scan_chunk(NCH - 1, False, True)
            take_y(NCH - 1)

            def half_silu(x, f):
                act.wait_ge(s_gu, LAST * FF0 + x * FF0 + f + 1)
                act.activation(actT0[:, f, half_cols(x)], ps[:, 4 * x + f % 2, 0:HN], ACT.Silu).then_inc(s_sl, 1)

            def half_router(x):
                act.wait_ge(s_r1, LAST + x + 1)
                for k in range(2):
                    act.activation(xT[:, k, half_cols(x)], ps[0:KH, 4 * x + 2, k * HN:(k + 1) * HN], ACT.Relu,
                                   bias=col[0:KH, V_BR1 + k:V_BR1 + k + 1])
                act.drain().then_inc(s_hr, 1)

            for x in range(2):
                for f in range(FF0):
                    half_silu(x, f)
            half_router(0)
            half_router(1)

            def route_exp(m, ne):
                act.wait_ge(s_dl[m], 1)
                act.activation(rb(3, B), rb(2, B), ACT.Exp)
                if m:
                    act.activation(rb(5, B * ne), rb(4, B * ne), ACT.Exp)
                act.drain().then_inc(s_ex[m], 1)

            route_exp(0, E0)
            with act.Fori(0, NB0 // 2) as i:
                for k in range(2):
                    act.wait_ge(s_w2[0][k], i * 16 + 16)
                    act.wait_ge(s_bh[0], i * 2 + k + 1)
                    for f in range(EF0):
                        act.activation(hbT[k][:, f, :], ps[:, 1 + 2 * k + f // 4, (f % 4) * P:(f % 4 + 1) * P], ACT.Relu,
                                       bias=ew_out[k][:, EF0 * D + f:EF0 * D + f + 1])
                    act.drain().then_inc(s_ba[0], 1)

            def shared_silu(i, f, banks):
                act.wait_ge(t_g, i * SF + f + 1)
                act.activation(actT1[:, f, :], ps[:, banks[f][0], :], ACT.Silu).then_inc(t_sl, 1)

            def attention_chunk(i, first):
                if not first:
                    shared_silu(i - 1, 0, mixed_banks)
                    shared_silu(i - 1, 1, mixed_banks)
                for n, f in enumerate(qk_order):
                    act.wait_ge(t_qk, i * 6 + n + 1)
                    act.activation(qkT[:, f, :], ps[:, 2 + f, :], ACT.Identity, bias=col[:, V_BQK + f:V_BQK + f + 1])\
                        .then_inc(t_qkT, 1)
                if not first:
                    shared_silu(i - 1, 2, mixed_banks)
                for t in range(CT):
                    act.wait_ge(t_sm, i * CT + t + 1)
                    act.activation(sm[t % 2], sm[t % 2], ACT.Exp, scale=HD ** -0.5)
                    act.drain().then_inc(t_p, 1)
                    if not first:
                        shared_silu(i - 1, 3 + t, mixed_banks)
                    if t >= 2:
                        act.wait_ge(t_o, i * CT + t - 1)
                    for a, bank in ((0, 6), (1, 7), (2, 6)):
                        act.wait_ge(t_pt, (i * CT + t) * 3 + a + 1)
                        act.activation(pT[t % 2][:, 4 * a:4 * a + 4, :], ps[:, bank, :].rearrange("p (h q) -> p h q", h=4), ACT.Copy)\
                            .then_inc(t_pT, 1)
                if not first:
                    shared_silu(i - 1, 7, mixed_banks)

            attention_chunk(0, True)
            with act.Fori(1, NCH) as i:
                attention_chunk(i, False)
            for f in range(3):
                shared_silu(NCH - 1, f, last_banks)
            route_exp(1, E1)
            for f in range(3, SF):
                shared_silu(NCH - 1, f, last_banks)
            with act.Fori(0, NB1 // 2) as i:
                for k in range(2):
                    act.wait_ge(s_bh[1], i * 2 + k + 1)
                    act.activation(hbT[k][:, 0:EF1, :], ps[:, 1 + 2 * k, :].rearrange("p (f t) -> p f t", f=EF1), ACT.Silu)
                    act.drain().then_inc(s_bg, 1)

        @block.tensor
        def _(pe):
            def transposes(src, bank):
                for k in range(2):
                    for j in range(CT):
                        last = pe.transpose(ps[0:KH, bank + k, j * P:(j + 1) * P], src[:, j, k * KH:(k + 1) * KH], ident)
                return last

            def accumulate(o, pairs):
                for n, (lhs, rhs) in enumerate(pairs):
                    last = pe.matmul(o, lhs, rhs, start=(n == 0), stop=(n == len(pairs) - 1))
                return last

            def row_slot(bank, j):
                return ps[:, bank + j // 2, (j % 2) * D:(j % 2 + 1) * D]

            pe.wait_ge(s_sm, 4 * 16)

            def route_ranks(m, ne, n, nt, bank):
                pe.wait_ge(s_mask[m], n)
                pe.matmul(ps[:, bank, 0:nt * ne], cst[:, C_ONE:C_ONE + P], rt(2, nt * ne), start=True, stop=False)
                pe.matmul(ps[:, bank, 0:nt * ne], cst[:, C_TRI:C_TRI + P], rt(1, nt * ne), start=False, stop=True)\
                    .then_inc(s_rank[m], 1)

            def route_totals(m, ne, bank):
                pe.matmul(ps[:, bank, 0:ne], cst[:, C_ONE:C_ONE + P], seen_all[:, 0:ne], start=True, stop=True)\
                    .then_inc(s_rank[m], 1)

            def enter_turn(c):
                pe.wait_ge(s_hn, c + 1)
                transposes(nrF, 5).then_inc(s_hnT, 1)

            def enter_in(c, g, after=None):
                m = slice(g * P, (g + 1) * P)
                if g == 0:
                    pe.wait_ge(s_xT, c + 1)
                    if after is not None:
                        pe.wait_ge(s_fT, after)
                if g == 2:
                    pe.wait_ge(s_zs, c * DG + 1)
                accumulate(ps[:, (5, 7, 6)[g], :], [(wgate[:, k, m], xTF[:, k, :]) for k in range(2)]).then_inc(s_gate, 1)
                if g:
                    pe.wait_ge(s_sig, c * DG + g)
                accumulate(ps[:, (6, 5, 7)[g], :], [(win[:, k, m], xTF[:, k, :]) for k in range(2)]).then_inc(s_z, 1)

            def enter_low(c):
                pe.wait_ge(s_zs, c * DG + DG)
                accumulate(ps[:, 5, :], [(wx[:, g, :], zT[:, g, :]) for g in range(DG)]).then_inc(s_xd, 1)

            def enter_steps(c):
                pe.wait_ge(s_dti, c + 1)
                pe.wait_ge(s_bcp, c + 1)
                for g in range(DG):
                    pe.matmul(ps[:, 5 + g, :], wdt[:, g * P:(g + 1) * P], dti, start=True, stop=True).then_inc(s_dt, 1)

            def leave_out(c):
                pe.wait_ge(s_yT, c + 1)
                for j in range(CT):
                    last = accumulate(row_slot(5, j), [(yT[:, g, j * P:(j + 1) * P], wout[:, g, :]) for g in range(DG)])
                last.then_inc(s_op, 1)

            def leave_turn(c):
                pe.wait_ge(s_hf, c + 1)
                transposes(nr, 5).then_inc(s_hfT, 1)

            def leave_mlp(c, f):
                m = slice(f * P, (f + 1) * P)
                if f == 0:
                    pe.wait_ge(s_fT, c + 1)
                if f >= 2:
                    pe.wait_ge(s_act, c * FF0 + f - 1)
                accumulate(ps[:, (5, 7, 6, 5)[f], :], [(wgf[:, k, m], xT[:, k, :]) for k in range(2)])
                if f:
                    pe.wait_ge(s_sl, c * FF0 + f)
                accumulate(ps[:, (6, 5, 7, 6)[f], :], [(wup[:, k, m], xT[:, k, :]) for k in range(2)]).then_inc(s_gu, 1)

            def leave_down(c):
                pe.wait_ge(s_act, c * FF0 + FF0)
                for j in range(CT):
                    o = ps[:, (7, 5)[j // 2], (j % 2) * D:(j % 2 + 1) * D]
                    last = accumulate(o, [(actT0[:, f, j * P:(j + 1) * P], wdown[:, f, :]) for f in range(FF0)])
                last.then_inc(s_dn, 1)

            def leave_turn_again(c):
                pe.wait_ge(s_xn, c + 1)
                transposes(nr, 6).then_inc(s_xnT, 1)

            def leave_router(c):
                pe.wait_ge(s_rT, c + 1)
                for f in range(2):
                    last = accumulate(ps[0:KH, 5 + f, :], [(wr1[:, k, f * KH:(f + 1) * KH], xT[:, k, :]) for k in range(2)])
                last.then_inc(s_r1, 1)

            def leave_scores(c):
                pe.wait_ge(s_hr, c + 1)
                for j in range(CT):
                    last = accumulate(ps[:, 7, j * E0:(j + 1) * E0], [(xT[:, k, j * P:(j + 1) * P], wr2[:, k, :]) for k in range(2)])
                last.then_inc(s_sc, 1)

            def spread(n, s):
                pe.wait_ge(s_cbfree, n + 1)
                pe.nop(nofuse=True)
                pe.matmul(ps[:, 0, :], sel[:, s:s + 1].broadcast_to((KH, P)), bc_p[:, :], start=True, stop=True)
                pe.matmul(ps[:, 1, :], sel[:, NST + s:NST + s + 1].broadcast_to((KH, P)), bc_p[:, :],
                          start=True, stop=True).then_inc(s_cb, 1)

            def scan_chunk(i, first, last):
                at = leave_early if last else leave_at
                if not first:
                    pe.wait_ge(s_yT, i)
                for g in range(DG):
                    pe.matmul(ps[:, 2 + g, :], diag_d[:, g, :], zT[:, g, :], start=True, stop=False)
                for s in range(NST):
                    if s + 2 < NST or not last:
                        if s + 2 == NST:
                            pe.wait_ge(s_bch, i + 2)
                        spread(i * NST + s + 2, (s + 2) % NST)
                    if not first and s == at["out"]:
                        leave_out(i - 1)
                    if not last and s == 1:
                        if not first:
                            pe.wait_ge(s_opr, i)
                        enter_turn(i + 1)
                    if not first and s == at["turn"]:
                        if not last:
                            pe.wait_ge(s_xT, i + 2)
                        leave_turn(i - 1)
                    if not last:
                        if s == 3:
                            enter_in(i + 1, 0, None if first else i)
                        if s in (4, 5):
                            enter_in(i + 1, s - 3)
                        if s == 6:
                            enter_low(i + 1)
                        if s == 7:
                            enter_steps(i + 1)
                    if not first:
                        for f in range(FF0):
                            if s == at["mlp"][f]:
                                if f == 0 and not last:
                                    pe.wait_ge(s_spf, i + 2)
                                leave_mlp(i - 1, f)
                        if s == at["down"]:
                            leave_down(i - 1)
                        if s == at["turn_again"]:
                            leave_turn_again(i - 1)
                        if s == at["router"]:
                            leave_router(i - 1)
                        if s == at["scores"]:
                            leave_scores(i - 1)
                    if last and s == 13:
                        route_ranks(0, E0, 1, 2 * CT, 6)
                    if last and s == 15:
                        route_ranks(0, E0, 2, CT, 6)
                    pe.wait_ge(s_hc, i * NST + s + 1)
                    for g in range(DG):
                        add = pe.matmul(ps[:, 2 + g, :], ident, hc[s % 2][:, g, :], start=False, stop=(s == NST - 1))
                    add.then_inc(s_sumd, 1)
                pe.drain().then_inc(s_y, 1)

            pe.sem_inc(s_sumd, 2)
            enter_turn(0)
            pe.wait_ge(s_wa, 11 * 16)
            for g in range(DG):
                enter_in(0, g)
            enter_low(0)
            enter_steps(0)
            pe.wait_ge(s_cst, 1)
            pe.wait_ge(s_bch, 1)
            spread(0, 0)
            spread(1, 1)
            scan_chunk(0, True, False)
            with pe.Fori(1, NCH - 1) as i:
                scan_chunk(i, False, False)
            scan_chunk(NCH - 1, False, True)

            def half_out(x):
                pe.wait_ge(s_yT, NCH)
                for j in range(HT):
                    t = slice((HT * x + j) * P, (HT * x + j + 1) * P)
                    last = accumulate(ps[:, 4 * x, j * D:(j + 1) * D], [(yT[:, g, t], wout[:, g, :]) for g in range(DG)])
                last.then_inc(s_op, 1)

            def half_turn(x, ready, done):
                pe.wait_ge(ready, LAST + x + 1)
                for k in range(2):
                    for j in range(HT):
                        last = pe.transpose(ps[0:KH, 4 * x + 1, k * HN + j * P:k * HN + (j + 1) * P],
                                            nr[:, HT * x + j, k * KH:(k + 1) * KH], ident)
                last.then_inc(done, 1)

            def half_mlp(x, f):
                m, n = slice(f * P, (f + 1) * P), (LAST + x) * FF0
                if f == 0:
                    pe.wait_ge(s_fT, LAST + x + 1)
                if f >= 2:
                    pe.wait_ge(s_act, n + f - 1)
                accumulate(ps[:, 4 * x + f % 2, 0:HN], [(wgf[:, k, m], xT[:, k, half_cols(x)]) for k in range(2)])
                accumulate(ps[:, 4 * x + 2 + f % 2, 0:HN], [(wup[:, k, m], xT[:, k, half_cols(x)]) for k in range(2)])\
                    .then_inc(s_gu, 1)

            def half_down(x):
                pe.wait_ge(s_act, (LAST + x) * FF0 + FF0)
                for j in range(HT):
                    t = slice((HT * x + j) * P, (HT * x + j + 1) * P)
                    last = accumulate(ps[:, 4 * x, j * D:(j + 1) * D], [(actT0[:, f, t], wdown[:, f, :]) for f in range(FF0)])
                last.then_inc(s_dn, 1)

            def half_router(x):
                pe.wait_ge(s_rT, LAST + x + 1)
                for k in range(2):
                    last = accumulate(ps[0:KH, 4 * x + 2, k * HN:(k + 1) * HN],
                                      [(wr1[:, c, k * KH:(k + 1) * KH], xT[:, c, half_cols(x)]) for c in range(2)])
                last.then_inc(s_r1, 1)

            def half_scores(x):
                pe.wait_ge(s_hr, LAST + x + 1)
                for j in range(HT):
                    t = slice((HT * x + j) * P, (HT * x + j + 1) * P)
                    last = accumulate(ps[:, 4 * x + 3, j * E0:(j + 1) * E0], [(xT[:, k, t], wr2[:, k, :]) for k in range(2)])
                last.then_inc(s_sc, 1)

            half_out(0)
            half_out(1)
            half_turn(0, s_hf, s_hfT)
            half_mlp(0, 0)
            half_mlp(0, 1)
            half_turn(1, s_hf, s_hfT)
            half_mlp(0, 2)
            half_mlp(0, 3)
            half_mlp(1, 0)
            half_down(0)
            half_mlp(1, 1)
            half_mlp(1, 2)
            half_mlp(1, 3)
            half_turn(0, s_xn, s_xnT)
            half_down(1)
            half_router(0)
            half_scores(0)
            half_turn(1, s_xn, s_xnT)
            half_router(1)
            half_scores(1)

            def expert_blocks(m, nb, fg, gated):
                for k in range(2):
                    pe.sem_inc(s_xbf[m][k], 1)
                    pe.sem_inc(s_w1f[m][k], 1)
                    pe.sem_inc(s_w2f[m][k], 1)
                n_in = fg * P

                def turn(i):
                    for k in range(2):
                        pe.wait_ge(s_xb[m][k], i * 16 + 16)
                        for c in range(2):
                            last = pe.transpose(ps[0:KH, 7 * k, c * P:(c + 1) * P], xb[k][:, c * KH:(c + 1) * KH], ident)
                        last.then_inc(s_bt[m], 1)

                def pair(i, more):
                    for k in range(2):
                        pe.wait_ge(s_bx[m], i * 2 + k + 1)
                        pe.wait_ge(s_w1[m][k], i * 16 + 16)
                        for half in range(2 if gated else 1):
                            for f in range(fg):
                                bank = 1 + 2 * k + (half if gated else f // 4)
                                base = 2 * n_in * half
                                last = accumulate(ps[:, bank, (f % 4) * P:(f % 4 + 1) * P],
                                                  [(ew_in[k][:, base + c * n_in + f * P:base + c * n_in + (f + 1) * P], xbT[k][:, c, :])
                                                   for c in range(2)])
                        last.then_inc(s_bh[m], 1)
                        pe.drain().then_inc(s_w1f[m][k], 1)
                    if more:
                        turn(i + 1)
                    for k in range(2):
                        pe.wait_ge(s_ba[m], i * 2 + k + 1)
                        pe.wait_ge(s_w2[m][k], i * 16 + 16)
                        accumulate(ps[:, 5 + k, 0:D], [(hbT[k][:, f, :], ew_out[k][:, f * D:(f + 1) * D]) for f in range(fg)])\
                            .then_inc(s_by[m], 1)

                turn(0)
                with pe.Fori(0, nb // 2 - 1) as i:
                    pair(i, True)
                pair(nb // 2 - 1, False)

            route_ranks(0, E0, 3, CT, 6)
            route_totals(0, E0, 5)
            expert_blocks(0, NB0, EF0, False)

            def shared_gate(i, f, banks):
                m = slice(f * P, (f + 1) * P)
                accumulate(ps[:, banks[f][0], :], [(ws1[:, k, m], xTS[:, k, :]) for k in range(2)]).then_inc(t_g, 1)

            def shared_up(i, f, banks):
                m = slice(f * P, (f + 1) * P)
                if banks[f][0] == banks[f][1]:
                    pe.wait_ge(t_sl, i * SF + f + 1)
                accumulate(ps[:, banks[f][1], :], [(ws3[:, k, m], xTS[:, k, :]) for k in range(2)]).then_inc(t_u, 1)

            def shared_down(i, bank):
                pe.wait_ge(t_act, i * SF + SF)
                for j in range(CT):
                    last = accumulate(row_slot(bank, j), [(actT1[:, f, j * P:(j + 1) * P], ws2[:, f, :]) for f in range(SF)])
                last.then_inc(t_dn, 1)

            def attention_chunk(i, first, final):
                if not first:
                    pe.wait_ge(t_fT, i)
                    for f in range(2):
                        shared_gate(i - 1, f, mixed_banks)
                        shared_up(i - 1, f, mixed_banks)
                pe.wait_ge(t_xn, i + 1)
                transposes(ar, 0).then_inc(t_xnT, 1)
                pe.wait_ge(t_xT, i + 1)
                for n, f in enumerate(qk_order):
                    if not first and n == 0:
                        pe.wait_ge(t_rsr, i)
                    if not first and n in (2, 4):
                        pe.wait_ge(t_act, (i - 1) * SF + n // 2)
                    accumulate(ps[:, 2 + f, :], [(wqk[:, k, f * P:(f + 1) * P], xT[:, k, :]) for k in range(2)])\
                        .then_inc(t_qk, 1)
                for j in range(CT):
                    last = accumulate(row_slot(0, j), [(xT[:, k, j * P:(j + 1) * P], wv[:, k, :]) for k in range(2)])
                last.then_inc(t_v, 1)
                if not first:
                    pe.wait_ge(t_qkT, i * 6 + 2)
                    shared_gate(i - 1, 2, mixed_banks)
                    shared_up(i - 1, 2, mixed_banks)
                pe.wait_ge(t_qkT, i * 6 + 6)

                def scores(t):
                    if t:
                        pe.wait_ge(t_ms, i * CT + t)
                    m = slice(t * P, (t + 1) * P)
                    for a in range(3):
                        for b in range(4):
                            s = slice(32 * b, 32 * b + 32)
                            last = pe.matmul(ps[:, 2 + b, a * P:(a + 1) * P], qkT[s, a, m], qkT[s, 3 + a, m], start=True, stop=True)
                    last.then_inc(t_s, 1)

                def turn_probs(t, groups):
                    for a in groups:
                        if a == 2:
                            pe.wait_ge(t_pT, (i * CT + t) * 3 + 1)
                        for b in range(4):
                            last = pe.transpose(ps[:, (6, 7, 6)[a], b * P:(b + 1) * P], sm[t % 2][:, b, a, :], ident)
                        last.then_inc(t_pt, 1)

                def values(t):
                    pe.wait_ge(t_pT, (i * CT + t) * 3 + 3)
                    if t:
                        pe.wait_ge(t_or, i * CT + t)
                    for h in range(H):
                        last = pe.matmul(ps[:, 1, h * (HD + 1):(h + 1) * (HD + 1)], pT[t % 2][:, h, :], vr[:, t, h, :],
                                         start=True, stop=True)
                    last.then_inc(t_o, 1)

                scores(0)
                pe.wait_ge(t_vr, i + 1)
                for t in range(CT + 1):
                    if t + 1 < CT:
                        scores(t + 1)
                    if t < CT:
                        if not first:
                            pe.wait_ge(t_act, (i - 1) * SF + 3 + t)
                            shared_gate(i - 1, 3 + t, mixed_banks)
                        pe.wait_ge(t_p, i * CT + t + 1)
                        if t:
                            pe.wait_ge(t_pT, (i * CT + t) * 3)
                        turn_probs(t, (0, 1))
                        if not first:
                            shared_up(i - 1, 3 + t, mixed_banks)
                        turn_probs(t, (2,))
                    if t:
                        values(t - 1)
                pe.wait_ge(t_or, i * CT + CT)
                transposes(nr, 2).then_inc(t_oT, 1)
                if not first:
                    pe.wait_ge(t_act, (i - 1) * SF + 7)
                    shared_gate(i - 1, 7, mixed_banks)
                    shared_up(i - 1, 7, mixed_banks)
                pe.wait_ge(t_oTs, i + 1)
                for j in range(CT):
                    last = accumulate(row_slot(4, j), [(xT[:, k, j * P:(j + 1) * P], wproj[:, k, :]) for k in range(2)])
                last.then_inc(t_pr, 1)
                if final:
                    pe.wait_ge(t_act, (i - 1) * SF + SF)
                    route_ranks(1, E1, 1, (NCH - 1) * CT, 0)
                if not first:
                    shared_down(i - 1, 2)
                pe.wait_ge(t_fn, i + 1)
                transposes(nr, 6).then_inc(t_fnT, 1)
                pe.wait_ge(t_fT, i + 1)
                for j in range(CT):
                    last = accumulate(ps[:, 6, j * E1:(j + 1) * E1], [(xTS[:, k, j * P:(j + 1) * P], wg[:, k, :]) for k in range(2)])
                last.then_inc(t_rs, 1)
                if not first:
                    pe.wait_ge(t_ch, i)

            pe.wait_ge(s_wb, 6 * 16)
            attention_chunk(0, True, False)
            with pe.Fori(1, NCH - 1) as i:
                attention_chunk(i, False, False)
            attention_chunk(NCH - 1, False, True)

            c = NCH - 1
            pe.wait_ge(s_row[1], 1)
            for f in range(3):
                shared_gate(c, f, last_banks)
                shared_up(c, f, last_banks)
            pe.wait_ge(t_rsr, NCH)
            route_ranks(1, E1, 2, CT, 6)
            route_totals(1, E1, 7)
            for f in range(3, SF):
                pe.wait_ge(t_act, c * SF + f - 2)
                shared_gate(c, f, last_banks)
                shared_up(c, f, last_banks)
            pe.wait_ge(s_pos[1], 1)
            shared_down(c, 6)
            pe.wait_ge(t_ch, NCH)
            expert_blocks(1, NB1, EF1, True)

        @block.vector
        def _(ve):
            def rstd(out, n, eps, rms):
                v, h, y, t = vv[:, 0:n], vh[:, 0:n], yy[:, 0:n], tt[:, 0:n]
                if rms:
                    ve.tensor_tensor(t, mv[:, 0:n, 0], mv[:, 0:n, 0], ALU.mult)
                    ve.drain()
                    ve.scalar_tensor_tensor(out=v, in0=t, scalar=eps, in1=mv[:, 0:n, 1], op0=ALU.add, op1=ALU.add)
                else:
                    ve.tensor_scalar(v, mv[:, 0:n, 1], eps, None, ALU.add)
                ve.drain()
                ve.tensor_scalar(ti[:, 0:n], v.bitcast(I32), 1, None, ALU.logical_shift_right)
                ve.tensor_scalar(h, v, -0.5, None, ALU.mult)
                ve.drain()
                ve.tensor_scalar(y.bitcast(I32), ti[:, 0:n], -1.0, float(0x5f3759df), ALU.mult, ALU.add)
                for step in range(3):
                    ve.drain()
                    ve.tensor_tensor(t, y, y, ALU.mult)
                    ve.drain()
                    ve.tensor_tensor(t, t, h, ALU.mult)
                    ve.drain()
                    ve.scalar_tensor_tensor(out=out if step == 2 else y, in0=t, scalar=1.5, in1=y, op0=ALU.add, op1=ALU.mult)
                ve.drain()

            def moments(src, n):
                for j in range(n):
                    ve.bn_stats(st[:, j, :], src[:, j, :])
                ve.drain()
                for j in range(n):
                    ve.bn_aggr(mv[:, j, :], st[:, j, :])
                ve.drain()

            def norm(dst, src, eps, rms=False, n=CT):
                moments(src, n)
                rstd(yy[:, 0:n], n, eps, rms)
                for j in range(n):
                    if rms:
                        ve.tensor_scalar(dst[:, j, :], src[:, j, :], yy[:, j:j + 1], None, ALU.mult)
                    else:
                        ve.tensor_scalar(dst[:, j, :], src[:, j, :], mv[:, j, 0:1], yy[:, j:j + 1], ALU.subtract, ALU.mult)

            def rows_of(bank):
                return ps[:, bank:bank + 2, 0:2 * D].rearrange("p b (j d) -> p b j d", j=2)

            def quad(t):
                return t[:, :, :].rearrange("p (b j) d -> p b j d", b=2)

            ve.memset(zero[:, :], 0.0)
            ve.memset(seen_all[:, :], 0.0)
            for k in range(2):
                ve.memset(dec[k].rearrange("p g (b t) -> p (g b) t", b=CT)[:, :, 0:1], 0.0)
            ve.wait_ge(s_sm, 4 * 16)
            ve.tensor_copy(sel[:, :], cst[0:KH, C_SEL:C_SEL + 32])
            for g in range(DG):
                ve.tensor_scalar(diag_d[:, g, :], ident, col[:, V_DSK + g:V_DSK + g + 1], None, ALU.mult)
            ve.drain()
            ve.sem_inc(s_bfree, 2)
            ve.sem_inc(s_decfree, 2)

            def embed_norm(c, n):
                ve.wait_ge(s_fsum, c + n)
                h = h_rows[:, c * CT:(c + n) * CT, :]
                norm(h, h, LN_EPS, n=n * CT)
                ve.drain().then_inc(s_fn, n)

            def embed_rows(c, n):
                ve.wait_ge(s_femb, c + n)
                x = x_rows[:, c * CT:(c + n) * CT, :]
                norm(x, h_rows[:, c * CT:(c + n) * CT, :], LN_EPS, n=n * CT)
                ve.drain()
                moments(x, n * CT)
                rstd(x_rms[:, c * CT:(c + n) * CT], n * CT, RMS_EPS, True)

            def enter_scale(c):
                tiles = ds(c * CT, CT)
                ve.tensor_tensor(nrF[:, :, :], x_rows[:, tiles, :],
                                 x_rms[:, tiles].rearrange("p (t a) -> p t a", a=1).broadcast_to((P, CT, D)), ALU.mult)
                ve.drain().then_inc(s_hn, 1)

            def enter_xT(c):
                ve.wait_ge(s_hnT, c + 1)
                for k in range(2):
                    ve.tensor_scalar(xTF[:, k, :], ps[0:KH, 5 + k, :], col[0:KH, V_N1 + k:V_N1 + k + 1], None, ALU.mult)
                ve.drain().then_inc(s_xT, 1)

            def enter_z(c, gs):
                for g in gs:
                    ve.wait_ge(s_z, c * DG + g + 1)
                    ve.wait_ge(s_sig, c * DG + g + 1)
                    ve.tensor_tensor(zT[:, g, :], ps[:, (6, 5, 7)[g], :], tA[:, g, :], ALU.mult).then_inc(s_zs, 1)

            def enter_bc(c):
                ve.wait_ge(s_xd, c + 1)
                ve.tensor_copy(bc_b, ps[BC, 5, :])
                ve.drain()
                ve.tensor_tensor(bc_r, ps[BC, 5, :], bc_b, ALU.subtract)
                ve.tensor_copy(bc_n[0:32, :], bc_b)
                ve.drain().then_inc(s_bcp, 1)
                ve.tensor_copy(bc_b, bc_r)
                ve.drain()
                ve.tensor_tensor(bc_r, bc_r, bc_b, ALU.subtract)
                ve.tensor_copy(bc_n[32:64, :], bc_b)
                ve.drain()
                ve.tensor_copy(bc_n[64:96, :], bc_r)
                ve.drain()

            def hand_bc():
                ve.tensor_copy(bc_p[:, :], bc_n[:, :])
                ve.drain().then_inc(s_bch, 1)

            def sum_steps(c):
                ve.wait_ge(s_sp, c + 1)
                ve.tensor_tensor(dtN, dtN, tA, ALU.add)
                ve.drain().then_inc(s_step, 1)

            def leave_rows(c):
                ve.wait_ge(s_op, c + 1)
                chunk = ds(c * CT, CT)
                ve.tensor_tensor(quad(mr), x_rows[:, chunk, :].rearrange("p (b j) d -> p b j d", b=2), rows_of(5), ALU.add)
                ve.drain().then_inc(s_opr, 1)
                ve.tensor_tensor(er[:, :, :], h_rows[:, chunk, :], mr[:, :, :], ALU.add)
                norm(nr, mr, RMS_EPS, rms=True)
                ve.drain().then_inc(s_hf, 1)

            def leave_xT(c):
                ve.wait_ge(s_hfT, c + 1)
                for k in range(2):
                    ve.tensor_scalar(xT[:, k, :], ps[0:KH, 5 + k, :], col[0:KH, V_NF + k:V_NF + k + 1], None, ALU.mult)
                ve.drain().then_inc(s_fT, 1)

            def leave_act(c, fs):
                for f in fs:
                    ve.wait_ge(s_sl, c * FF0 + f + 1)
                    ve.tensor_tensor(actT0[:, f, :], actT0[:, f, :], ps[:, (6, 5, 7, 6)[f], :], ALU.mult).then_inc(s_act, 1)

            def leave_norm(c):
                ve.wait_ge(s_dn, c + 1)
                for b, bank in ((0, 7), (1, 5)):
                    ve.tensor_tensor(er[:, 2 * b:2 * b + 2, :], er[:, 2 * b:2 * b + 2, :],
                                     ps[:, bank, 0:2 * D].rearrange("p (j d) -> p j d", j=2), ALU.add)
                ve.drain()
                norm(nr, er, LN_EPS)
                ve.drain().then_inc(s_xn, 1)
                ve.tensor_copy(h_rows[:, ds(c * CT, CT), :], er[:, :, :])
                ve.tensor_copy(x_rows[:, ds(c * CT, CT), :], nr[:, :, :])

            def leave_rT(c):
                ve.wait_ge(s_xnT, c + 1)
                ve.tensor_copy(xT[:, :, :], ps[0:KH, 6:8, :])
                ve.drain().then_inc(s_rT, 1)

            def leave_scores(c):
                ve.wait_ge(s_sc, c + 1)
                ve.tensor_tensor(sc0[:, ds(c * CT, CT), :], ps[:, 7, 0:CT * E0].rearrange("p (j e) -> p j e", e=E0),
                                 row[:, R_BR2:R_BR2 + E0].rearrange("p (a e) -> p a e", a=1).broadcast_to((P, CT, E0)), ALU.add)
                ve.drain().then_inc(s_ch, 1)

            def route_picks(m, ne, t0, nt):
                sc = sc1[:, t0:t0 + nt, 0:ne]
                hot = [tiles_by(h[:, :], t0, nt, ne) for h in hot_all]
                tmp, rest, before = [tiles_by(rt(n), 0, nt, ne) for n in (0, 3, 2)]
                both = tiles_by(rt(1), 0, nt, ne)
                key = rt(4, nt)
                rev = cst[:, C_REV:C_REV + ne].rearrange("p (a e) -> p a e", a=1).broadcast_to((P, nt, ne))

                def per_tile(ap):
                    return ap.rearrange("p (t a) -> p t a", a=1).broadcast_to((P, nt, ne))

                for r, scores in ((0, sc), (1, rest)):
                    top = best[:, r, t0:t0 + nt]
                    ve.tensor_reduce(top, scores, AXX, ALU.max)
                    ve.drain()
                    ve.tensor_tensor(tmp, scores, per_tile(top), ALU.is_equal)
                    ve.drain()
                    ve.tensor_tensor(tmp, tmp, rev, ALU.mult)
                    ve.drain()
                    ve.tensor_reduce(key, tmp, AXX, ALU.max)
                    ve.drain()
                    ve.tensor_tensor(hot[r], tmp, per_tile(key), ALU.is_equal)
                    ve.drain()
                    if r == 0:
                        ve.scalar_tensor_tensor(out=rest, in0=hot[0], scalar=NEG, in1=sc, op0=ALU.mult, op1=ALU.add)
                        ve.drain()
                ve.tensor_tensor(both, hot[0], hot[1], ALU.add)
                ve.tensor_copy(before[:, 0, :], seen_all[:, 0:ne])
                ve.drain()
                for t in range(nt):
                    after = before[:, t + 1, :] if t + 1 < nt else seen_all[:, 0:ne]
                    ve.tensor_tensor(after, before[:, t, :], both[:, t, :], ALU.add)
                    ve.drain()
                ve.drain().then_inc(s_mask[m], 1)

            def route_places(m, ne, n, t0, nt, bank):
                ve.wait_ge(s_rank[m], n)
                where = tiles_by(rt(0), 0, nt, ne)
                first = cst[:, C_REG:C_REG + ne].rearrange("p (a e) -> p a e", a=1).broadcast_to((P, nt, ne))
                ve.tensor_tensor(where, ps[:, bank, 0:nt * ne].rearrange("p (t e) -> p t e", e=ne), first, ALU.add)
                ve.drain()
                for r in range(2):
                    ve.tensor_tensor(tiles_by(rt(3 + r), 0, nt, ne), where, tiles_by(hot_all[r][:, :], t0, nt, ne), ALU.mult)
                ve.drain()
                for r in range(2):
                    ve.tensor_reduce(row_f[:, r, t0:t0 + nt], tiles_by(rt(3 + r), 0, nt, ne), AXX, ALU.add)
                ve.drain()
                ve.tensor_copy(row_i[:, :, t0:t0 + nt], row_f[:, :, t0:t0 + nt])
                ve.drain().then_inc(s_row[m], 1)

            def route_blocks(m, ne, n, nb, bank):
                ve.wait_ge(s_rank[m], n)
                total, blocks, last, shift = rb(0, ne), rb(3, ne), rb(4, ne), rb(5, ne)
                over = rb(6, ne * B).rearrange("p (e t) -> p e t", e=ne)
                ve.tensor_copy(total, ps[:, bank, 0:ne])
                ve.drain()
                ve.tensor_tensor(over, total.rearrange("p (e a) -> p e a", a=1).broadcast_to((P, ne, B)),
                                 cst[:, C_THR:C_THR + B].rearrange("p (a t) -> p a t", a=1).broadcast_to((P, ne, B)), ALU.is_gt)
                ve.tensor_tensor(zid[:, 0:ne], total[0:1, :], cst[0:1, C_REG:C_REG + ne], ALU.add)
                ve.drain().then_inc(s_zid[m], 1)
                ve.tensor_reduce(blocks, over, AXX, ALU.add)
                ve.drain()
                ve.tensor_tensor_scan(last, cst[:, C_ONE:C_ONE + ne], blocks, 0.0, ALU.mult, ALU.add)
                ve.drain()
                past, theirs = [arena[0:1, n:n + nb * ne].rearrange("p (b e) -> p b e", e=ne) for n in (15360, 16384)]
                num, done = [arena[0:1, n:n + nb] for n in (17408, 17472)]
                block = cst[0:1, C_BLK:C_BLK + nb]
                ve.tensor_tensor(past, last[0:1, :].rearrange("p (a e) -> p a e", a=1).broadcast_to((1, nb, ne)),
                                 block.rearrange("p (b a) -> p b a", a=1).broadcast_to((1, nb, ne)), ALU.is_le)
                ve.drain()
                ve.tensor_tensor(theirs, past, blocks[0:1, :].rearrange("p (a e) -> p a e", a=1).broadcast_to((1, nb, ne)), ALU.mult)
                ve.tensor_reduce(num, past, AXX, ALU.add)
                ve.drain()
                ve.tensor_reduce(done, theirs, AXX, ALU.add)
                ve.tensor_scalar(eid[:, 0:nb], num, float(ne - 1), None, ALU.min)
                ve.drain()
                ve.tensor_tensor(done, block, done, ALU.subtract)
                ve.tensor_scalar(num, num, float(REG), None, ALU.mult)
                ve.drain()
                ve.scalar_tensor_tensor(out=num, in0=done, scalar=float(P), in1=num, op0=ALU.mult, op1=ALU.add)
                ve.drain()
                ve.tensor_scalar(rid[:, 0:nb], num, float(ne * REG), None, ALU.min)
                ve.drain().then_inc(s_pos[m], 1)
                ve.tensor_tensor(shift, last, blocks, ALU.subtract)
                ve.drain()
                ve.scalar_tensor_tensor(out=shift, in0=shift, scalar=float(P), in1=cst[:, C_REG:C_REG + ne],
                                        op0=ALU.mult, op1=ALU.subtract)
                ve.drain()
                moved = tiles_by(rb(6), 0, B, ne)
                for r in range(2):
                    ve.tensor_tensor(moved, tiles_by(hot_all[r][:, :], 0, B, ne),
                                     shift.rearrange("p (a e) -> p a e", a=1).broadcast_to((P, B, ne)), ALU.mult)
                    ve.drain()
                    ve.tensor_reduce(rb(7, B), moved, AXX, ALU.add)
                    ve.drain()
                    ve.tensor_tensor(pos_i[:, r, :], rb(7, B), row_f[:, r, :], ALU.add)
                    ve.drain()

            def route_weights(m, ne):
                first, second = best[:, 0, :], best[:, 1, :]
                ve.tensor_tensor(rb(2, B), second, first, ALU.subtract)
                if m:
                    ve.tensor_tensor(tiles_by(rb(4), 0, B, ne), sc1[:, :, :],
                                     first.rearrange("p (t a) -> p t a", a=1).broadcast_to((P, B, ne)), ALU.subtract)
                ve.drain().then_inc(s_dl[m], 1)
                ve.wait_ge(s_ex[m], 1)
                if m:
                    ve.tensor_reduce(rb(6, B), tiles_by(rb(5), 0, B, ne), AXX, ALU.add)
                else:
                    ve.tensor_scalar(rb(6, B), rb(3, B), 1.0, None, ALU.add)
                ve.drain()
                ve.reciprocal(gate_w[:, 0, :], rb(6, B))
                ve.drain()
                ve.tensor_tensor(gate_w[:, 1, :], gate_w[:, 0, :], rb(3, B), ALU.mult)
                ve.drain().then_inc(s_gw[m], 1)

            def scan_chunk(i, first, last):
                at = leave_early if last else leave_at
                ve.tensor_tensor(uT, dtN, zT, ALU.mult)
                ve.drain()
                for s in range(NST):
                    k, n = s % 2, i * NST + s
                    ve.wait_ge(s_cs, n + 1)
                    ve.tensor_tensor(bxs, uT, bcs[:, k, 0:1, :].broadcast_to((P, DG, CN)), ALU.mult)
                    ve.drain().then_inc(s_bfree, 1)
                    ve.wait_ge(s_dec, n + 1)
                    ve.wait_ge(s_cfree, n + 1)
                    ve.tensor_tensor_scan(hid[k].rearrange("p g t -> p (g t)"), dec[k].rearrange("p g t -> p (g t)"),
                                          bxs.rearrange("p g t -> p (g t)"), 0.0, ALU.mult, ALU.add).then_inc(s_scan, 1)
                    ve.drain().then_inc(s_decfree, 1)
                    if not first and s == at["rows"]:
                        leave_rows(i - 1)
                    if not last:
                        if s == 0:
                            enter_scale(i + 1)
                        if s == 2:
                            enter_xT(i + 1)
                        if s in (5, 6):
                            enter_z(i + 1, ((0,), (1, 2))[s - 5])
                        if s == 7:
                            enter_bc(i + 1)
                        if s == 14:
                            ve.wait_ge(s_cb, i * NST + NST)
                            hand_bc()
                        if s == 15:
                            sum_steps(i + 1)
                    if not first:
                        if s == at["xT"]:
                            leave_xT(i - 1)
                        leave_act(i - 1, [f for f in range(FF0) if at["act"][f] == s])
                        if s == at["norm"]:
                            leave_norm(i - 1)
                        if s == at["rT"]:
                            leave_rT(i - 1)
                        if s == at["take_scores"]:
                            leave_scores(i - 1)
                    if first:
                        if s == 4:
                            embed_norm(2, 2)
                        if s == 10:
                            embed_rows(2, 2)
                    if last:
                        if s == 6:
                            route_picks(0, E0, 0, 2 * CT)
                        if s == 14:
                            route_places(0, E0, 1, 0, 2 * CT, 6)
                            route_picks(0, E0, 2 * CT, CT)

            embed_norm(0, 1)
            embed_rows(0, 1)
            enter_scale(0)
            ve.wait_ge(s_neg, 1)
            ve.tensor_scalar(neg_a, neg_a, -1.0, None, ALU.mult)
            ve.drain().then_inc(s_cst, 1)
            enter_xT(0)
            enter_z(0, range(DG))
            embed_norm(1, 1)
            enter_bc(0)
            embed_rows(1, 1)
            hand_bc()
            sum_steps(0)
            scan_chunk(0, True, False)
            with ve.Fori(1, NCH - 1) as i:
                scan_chunk(i, False, False)
            scan_chunk(NCH - 1, False, True)

            def half_tiles(x):
                return slice(LAST * CT + HT * x, LAST * CT + HT * (x + 1)), slice(HT * x, HT * (x + 1))

            def half_rows(x):
                ve.wait_ge(s_op, LAST + x + 1)
                rows, mine = half_tiles(x)
                ve.tensor_tensor(mr[:, mine, :], x_rows[:, rows, :], ps[:, 4 * x, 0:HT * D].rearrange("p (j d) -> p j d", j=HT), ALU.add)
                ve.drain()
                norm(nr[:, mine, :], mr[:, mine, :], RMS_EPS, rms=True, n=HT)
                ve.drain().then_inc(s_hf, 1)
                ve.tensor_tensor(er[:, mine, :], h_rows[:, rows, :], mr[:, mine, :], ALU.add)

            def half_xT(x):
                ve.wait_ge(s_hfT, LAST + x + 1)
                for k in range(2):
                    ve.tensor_scalar(xT[:, k, half_cols(x)], ps[0:KH, 4 * x + 1, k * HN:(k + 1) * HN],
                                     col[0:KH, V_NF + k:V_NF + k + 1], None, ALU.mult)
                ve.drain().then_inc(s_fT, 1)

            def half_act(x, f):
                ve.wait_ge(s_sl, (LAST + x) * FF0 + f + 1)
                o = actT0[:, f, half_cols(x)]
                ve.tensor_tensor(o, o, ps[:, 4 * x + 2 + f % 2, 0:HN], ALU.mult).then_inc(s_act, 1)

            def half_norm(x):
                ve.wait_ge(s_dn, LAST + x + 1)
                rows, mine = half_tiles(x)
                ve.tensor_tensor(er[:, mine, :], er[:, mine, :], ps[:, 4 * x, 0:HT * D].rearrange("p (j d) -> p j d", j=HT), ALU.add)
                ve.drain()
                norm(nr[:, mine, :], er[:, mine, :], LN_EPS, n=HT)
                ve.drain().then_inc(s_xn, 1)
                ve.tensor_copy(h_rows[:, rows, :], er[:, mine, :])
                ve.tensor_copy(x_rows[:, rows, :], nr[:, mine, :])

            def half_rT(x):
                ve.wait_ge(s_xnT, LAST + x + 1)
                ve.tensor_copy(xT[:, :, half_cols(x)], ps[0:KH, 4 * x + 1, :].rearrange("p (k t) -> p k t", k=2))
                ve.drain().then_inc(s_rT, 1)

            def half_scores(x):
                ve.wait_ge(s_sc, LAST + x + 1)
                rows, mine = half_tiles(x)
                ve.tensor_tensor(sc0[:, rows, :], ps[:, 4 * x + 3, 0:HT * E0].rearrange("p (j e) -> p j e", e=E0),
                                 row[:, R_BR2:R_BR2 + E0].rearrange("p (a e) -> p a e", a=1).broadcast_to((P, HT, E0)), ALU.add)
                ve.drain().then_inc(s_ch, 1)

            route_places(0, E0, 2, 2 * CT, CT, 6)
            half_rows(0)
            half_xT(0)
            half_rows(1)
            half_act(0, 0)
            half_act(0, 1)
            half_xT(1)
            half_act(0, 2)
            half_act(0, 3)
            half_act(1, 0)
            half_act(1, 1)
            half_norm(0)
            half_act(1, 2)
            half_act(1, 3)
            half_rT(0)
            half_norm(1)
            half_scores(0)
            half_rT(1)
            half_scores(1)
            route_picks(0, E0, 3 * CT, CT)
            route_places(0, E0, 3, 3 * CT, CT, 6)
            route_blocks(0, E0, 4, NB0, 5)
            route_weights(0, E0)

            def expert_rows_out(m, nb, gated):
                for k in range(2):
                    ve.sem_inc(s_ybf[m][k], 1)

                def turn(i):
                    for k in range(2):
                        ve.wait_ge(s_bt[m], i * 2 + k + 1)
                        ve.tensor_copy(xbT[k], ps[0:KH, 7 * k, 0:2 * P].rearrange("p (c t) -> p c t", c=2))\
                            .then_inc(s_bx[m], 1)
                        ve.drain().then_inc(s_xbf[m][k], 1)

                def pair(i, more):
                    if gated:
                        for k in range(2):
                            ve.wait_ge(s_bg, i * 2 + k + 1)
                            ve.tensor_tensor(hbT[k][:, 0:EF1, :], hbT[k][:, 0:EF1, :],
                                             ps[:, 2 + 2 * k, :].rearrange("p (f t) -> p f t", f=EF1), ALU.mult)
                            ve.drain().then_inc(s_ba[m], 1)
                    if more:
                        turn(i + 1)
                    for k in range(2):
                        ve.wait_ge(s_by[m], i * 2 + k + 1)
                        ve.wait_ge(s_ybf[m][k], i + 1)
                        if gated:
                            last = ve.tensor_copy(yb[k], ps[:, 5 + k, 0:D])
                        else:
                            last = ve.tensor_tensor(yb[k], ps[:, 5 + k, 0:D], ew_out[k][:, EF0 * D + EF0:], ALU.add)
                        last.then_inc(s_yb[m], 1)
                        ve.drain().then_inc(s_w2f[m][k], 1)

                turn(0)
                with ve.Fori(0, nb // 2 - 1) as i:
                    pair(i, True)
                pair(nb // 2 - 1, False)

            expert_rows_out(0, NB0, False)

            def add_experts(m, dst, src, t0):
                for j in range(CT):
                    ve.scalar_tensor_tensor(out=dst(j), in0=g1[:, ds(t0 + j, 1), :], scalar=gate_w[:, 0, ds(t0 + j, 1)],
                                            in1=src(j), op0=ALU.mult, op1=ALU.add)
                ve.drain()
                for j in range(CT):
                    ve.scalar_tensor_tensor(out=dst(j), in0=g2[:, ds(t0 + j, 1), :], scalar=gate_w[:, 1, ds(t0 + j, 1)],
                                            in1=dst(j), op0=ALU.mult, op1=ALU.add)
                ve.drain()

            causal = cst[:, C_CAUSAL:C_CAUSAL + P].rearrange("p (a b k) -> p a b k", a=1, b=1).broadcast_to((P, 4, 3, P))
            ve.memset(vr[:, :, :, HD:HD + 1], 1.0)

            def joined(i):
                ve.wait_ge(s_g[0], i * (2 * CT * 16) + 2 * CT * 16)
                hr = lambda j: h_rows[:, ds(i * CT + j, 1), :]
                add_experts(0, hr, hr, i * CT)
                norm(ar, h_rows[:, ds(i * CT, CT), :], LN_EPS)
                ve.drain().then_inc(t_xn, 1)

            def shared_mul(i, f, banks):
                ve.wait_ge(t_u, i * SF + f + 1)
                ve.wait_ge(t_sl, i * SF + f + 1)
                ve.tensor_tensor(actT1[:, f, :], actT1[:, f, :], ps[:, banks[f][1], :], ALU.mult).then_inc(t_act, 1)

            def shared_rows(i, bank):
                ve.wait_ge(t_dn, i + 1)
                h = h_rows[:, ds(i * CT, CT), :].rearrange("p (b j) d -> p b j d", b=2)
                ve.tensor_tensor(h, h, rows_of(bank), ALU.add)
                ve.drain().then_inc(t_ch, 1)

            def attention_chunk(i, first, more):
                chunk = h_rows[:, ds(i * CT, CT), :]
                if not first:
                    shared_mul(i - 1, 0, mixed_banks)
                    shared_mul(i - 1, 1, mixed_banks)
                ve.wait_ge(t_xnT, i + 1)
                ve.tensor_copy(xT[:, :, :], ps[0:KH, 0:2, :])
                ve.drain().then_inc(t_xT, 1)
                ve.tensor_tensor(chunk, chunk, bproj_b, ALU.add)
                if more:
                    joined(i + 1)
                else:
                    route_picks(1, E1, 0, (NCH - 1) * CT)
                ve.wait_ge(t_v, i + 1)
                for b in range(2):
                    ve.tensor_tensor(vr[:, 2 * b:2 * b + 2, :, 0:HD],
                                     ps[:, b, 0:2 * D].rearrange("p (t h d) -> p t h d", t=2, h=H),
                                     row[:, R_BV:R_BV + D].rearrange("p (a h d) -> p a h d", a=1, h=H).broadcast_to((P, 2, H, HD)),
                                     ALU.add)
                ve.drain().then_inc(t_vr, 1)
                if not first:
                    shared_mul(i - 1, 2, mixed_banks)

                def masked(t):
                    ve.wait_ge(t_s, i * CT + t + 1)
                    if t >= 2:
                        ve.wait_ge(t_pt, (i * CT + t - 1) * 3)
                    ve.tensor_tensor(sm[t % 2], ps[:, 2:6, 0:3 * P].rearrange("p b (a k) -> p b a k", a=3), causal, ALU.add)
                    ve.drain().then_inc(t_ms, 1)
                    ve.tensor_reduce(smax.rearrange("p (b a) -> p b a", b=4), sm[t % 2], AXX, ALU.max)
                    ve.drain()
                    ve.tensor_tensor(sm[t % 2], sm[t % 2], smax.rearrange("p (b a k) -> p b a k", b=4, k=1)
                                     .broadcast_to((P, 4, 3, P)), ALU.subtract)
                    ve.drain().then_inc(t_sm, 1)

                def over_sums(t):
                    ve.wait_ge(t_o, i * CT + t + 1)
                    o = ps[:, 1, 0:H * (HD + 1)].rearrange("p (h d) -> p h d", h=H)
                    ve.reciprocal(rden.rearrange("p (h a) -> p h a", a=1), o[:, :, HD:HD + 1])
                    ve.drain()
                    ve.tensor_tensor(nr[:, t, :].rearrange("p (h d) -> p h d", h=H), o[:, :, 0:HD],
                                     rden.rearrange("p (h a) -> p h a", a=1).broadcast_to((P, H, HD)), ALU.mult)
                    ve.drain().then_inc(t_or, 1)

                for t in range(CT + 2):
                    if t < CT:
                        masked(t)
                    if not first and 1 <= t <= CT:
                        shared_mul(i - 1, 2 + t, mixed_banks)
                    if t >= 2:
                        over_sums(t - 2)
                ve.wait_ge(t_oT, i + 1)
                ve.tensor_copy(xT[:, :, :], ps[0:KH, 2:4, :])
                ve.drain().then_inc(t_oTs, 1)
                if not first:
                    shared_mul(i - 1, 7, mixed_banks)
                ve.wait_ge(t_pr, i + 1)
                rows = chunk.rearrange("p (b j) d -> p b j d", b=2)
                ve.tensor_tensor(rows, rows, rows_of(4), ALU.add)
                ve.drain()
                norm(nr, chunk, LN_EPS)
                ve.drain().then_inc(t_fn, 1)
                ve.tensor_copy(x_rows[:, ds(i * CT, CT), :], nr[:, :, :])
                if not first:
                    shared_rows(i - 1, 2)
                if not more:
                    route_places(1, E1, 1, 0, (NCH - 1) * CT, 0)
                ve.wait_ge(t_fnT, i + 1)
                ve.tensor_copy(xTS[:, :, :], ps[0:KH, 6:8, :])
                ve.drain().then_inc(t_fT, 1)
                ve.wait_ge(t_rs, i + 1)
                ve.tensor_copy(sc1[:, ds(i * CT, CT), :], ps[:, 6, 0:CT * E1].rearrange("p (j e) -> p j e", e=E1))
                ve.drain().then_inc(t_rsr, 1)

            ve.memset(seen_all[:, :], 0.0)
            joined(0)
            attention_chunk(0, True, True)
            with ve.Fori(1, NCH - 1) as i:
                attention_chunk(i, False, True)
            attention_chunk(NCH - 1, False, False)

            route_picks(1, E1, (NCH - 1) * CT, CT)
            for f in range(3):
                shared_mul(NCH - 1, f, last_banks)
            route_places(1, E1, 2, (NCH - 1) * CT, CT, 6)
            route_blocks(1, E1, 3, NB1, 7)
            route_weights(1, E1)
            for f in range(3, SF):
                shared_mul(NCH - 1, f, last_banks)
            shared_rows(NCH - 1, 6)
            expert_rows_out(1, NB1, True)
            with ve.Fori(0, NCH) as i:
                ve.wait_ge(s_g[1], i * (2 * CT * 16) + 2 * CT * 16)
                hr = lambda j: h_rows[:, ds(i * CT + j, 1), :]
                add_experts(1, hr, hr, i * CT)
                ve.drain().then_inc(s_fin, 1)


def kernel(**inputs):
    import numpy as np
    import concourse.bacc as bacc
    from concourse import mybir as _mybir
    from concourse.bass_utils import run_bass_kernel_spmd as run

    a = {k: np.asarray(v) for k, v in inputs.items()}

    def halves(w):
        return w.reshape(2, KH, -1).transpose(1, 0, 2)

    def groups(w):
        return w.reshape(-1, P, w.shape[-1]).transpose(1, 0, 2)

    def columns(v, p):
        o = np.zeros((P, v.size // p), v.dtype)
        o[:p] = v.reshape(-1, p).T
        return o

    c = np.zeros((P, C_END), np.float32)
    i = np.arange(P)
    c[:, C_ID:C_ID + P] = i[:, None] == i
    c[:, C_TRI:C_TRI + P] = i[:, None] < i
    c[:, C_ONE:C_ONE + P] = 1
    c[:, C_CAUSAL:C_CAUSAL + P] = np.where(i[:, None] >= i, 0, NEG)
    for r in range(3):
        c[32 * r:32 * r + 32, C_SEL:C_SEL + 32] = np.eye(32)
    c[:, C_REV:C_REV + 16] = 16 - np.arange(16)
    c[:, C_THR:C_THR + B] = P * np.arange(B)
    c[:, C_BLK:C_BLK + NB1] = np.arange(NB1)
    c[:, C_REG:C_REG + E1] = REG * np.arange(E1)

    rows = np.concatenate([a["L0_tok_gamma"], a["L0_tok_beta"], a["L1_attn_c_attn_b"][2 * D:], a["L1_attn_c_proj_b"],
                           a["L0_ffn_br2"]])[None]

    def strips(w):
        o = np.zeros((w.shape[0], H, 32), w.dtype)
        o[:, :, :HD] = w.reshape(w.shape[0], H, HD)
        return o.reshape(w.shape[0], 3 * P)

    wa, ba = a["L1_attn_c_attn_w"], a["L1_attn_c_attn_b"][None]
    bqk = np.concatenate([strips(ba[:, :D]), strips(ba[:, D:2 * D])], 1)[0]
    cols = np.concatenate([columns(a["L0_attn_w_norm1"], KH), columns(a["L0_attn_w_ffn_norm"], KH),
                           columns(a["L0_ffn_br1"], KH), columns(a["L0_attn_b_dt"], P), columns(a["L0_attn_D_skip"], P),
                           columns(bqk, P), groups(a["L0_attn_A_log"]).reshape(P, -1)], 1)
    e0_in = np.stack([halves(w.T).reshape(KH, -1) for w in a["L0_ffn_W1"]])
    e0_out = np.stack([np.concatenate([groups(w2.T).reshape(P, -1), columns(b1, P), np.broadcast_to(b2, (P, D))], 1)
                       for w2, b1, b2 in zip(a["L0_ffn_W2"], a["L0_ffn_b1"], a["L0_ffn_b2"])])
    e1_in = np.stack([np.concatenate([halves(w1.T).reshape(KH, -1), halves(w3.T).reshape(KH, -1)], 1)
                      for w1, w3 in zip(a["L1_ffn_w1"], a["L1_ffn_w3"])])
    e1_out = np.stack([groups(w2.T).reshape(P, -1) for w2 in a["L1_ffn_w2"]])
    named = dict(
        tok=a["x"].T, seg=a["mask_BS_i1_0"].T, tok_tab=a["L0_tok_tok_table"], seg_tab=a["L0_tok_seg_table"],
        pos_tab=a["L0_tok_pos_table"], consts=c, rows=rows, cols=cols,
        w_in=halves(a["L0_attn_W_in"].T), w_gate=halves(a["L0_attn_W_gate"].T),
        w_x=groups(a["L0_attn_W_xproj"].T), w_dt=a["L0_attn_W_dt"].T,
        w_out=groups(a["L0_attn_W_out"].T), w_up=halves(a["L0_attn_W_up"].T), w_gf=halves(a["L0_attn_W_gate_ffn"].T),
        w_down=groups(a["L0_attn_W_down"].T), w_r1=halves(a["L0_ffn_Wr1"].T), w_r2=halves(a["L0_ffn_Wr2"].T),
        w_qk=halves(np.concatenate([strips(wa[:, :D]), strips(wa[:, D:2 * D])], 1)), w_v=halves(wa[:, 2 * D:]),
        w_proj=halves(a["L1_attn_c_proj_w"]), w_g=halves(a["L1_ffn_gate_w"].T),
        w_s1=halves(a["L1_ffn_sw1"].T), w_s3=halves(a["L1_ffn_sw3"].T), w_s2=groups(a["L1_ffn_sw2"].T),
        e0_in=e0_in, e0_out=e0_out, e1_in=e1_in, e1_out=e1_out)
    named = {k: np.ascontiguousarray(v) for k, v in named.items()}

    nc = bacc.Bacc("TRN2", target_bir_lowering=False, num_devices=1)
    args = [nc.dram_tensor("in_" + k, v.shape, _mybir.dt.from_np(v.dtype), kind="ExternalInput").ap() for k, v in named.items()]
    out = nc.dram_tensor("out_0", (B, P, D), F32, kind="ExternalOutput").ap()
    tower(nc, *args, out)
    r = run(nc, [{"in_" + k: v for k, v in named.items()}], core_ids=[0])
    return r.results[0]["out_0"]
```
